# Optimizing a Trainium2 kernel written in Bass

```python
import numpy as np
import jax
import jax.numpy as jnp

def _softmax(x, axis=-1):
    return jax.nn.softmax(x, axis=axis)

def _gelu(x):
    return jax.nn.gelu(x, approximate=True)

def _silu(x):
    return jax.nn.silu(x)

def _sigmoid(x):
    return jax.nn.sigmoid(x)

def _layernorm(x, axis=-1, eps=1e-05):
    m = jnp.mean(x, axis=axis, keepdims=True)
    v = jnp.var(x, axis=axis, keepdims=True)
    return (x - m) / jnp.sqrt(v + eps)

def _scatter_add(tgt, idx, src, axis=0):
    return tgt.at[idx].add(src)

def _segment_sum(src, seg, n):
    return jax.ops.segment_sum(src, seg, n)
kernel_name = 'mk_xattn_ffn_d2_seqx_r8_4af31b'

def setup_inputs(seed: int=0):
    np.random.seed(seed)
    _w = jnp.asarray

    def _rec_inputs():
        import jax
        import jax.numpy as jnp
        _rk = jax.random.key(seed)
        x = -0.0002928 + 1 * jax.random.normal(jax.random.fold_in(_rk, 1), (32, 128, 128), jnp.float32)
        _lenS = 128 - jax.random.randint(jax.random.fold_in(_rk, 7), (32,), 0, max(1, 128 // 4) + 1, jnp.int32)
        _lenS2 = 120 - jax.random.randint(jax.random.fold_in(_rk, 8), (32,), 0, max(1, 120 // 4) + 1, jnp.int32)
        _ctx_1024P = jax.random.normal(jax.random.fold_in(_rk, 11), (32, 16, 128), jnp.float32)
        _ctx_1024c = jax.random.dirichlet(jax.random.fold_in(_rk, 511), 0.3 * jnp.ones((16,), jnp.float32), (32, 120))
        _ctx_1024t = jnp.einsum('bsk,bkd->bsd', _ctx_1024c, _ctx_1024P)
        _ctx_1024t = _ctx_1024t * jax.lax.rsqrt(jnp.mean(jnp.square(_ctx_1024t)) + 1e-12) * 0.953939
        ctx_1024 = -1.39393e-06 + 0.999914 * (_ctx_1024t + 0.3 * jax.random.normal(jax.random.fold_in(_rk, 611), (32, 120, 128), jnp.float32))
        return (x, ctx_1024)
    x, ctx_1024 = _rec_inputs()

    def _L0_xattn_setup():
        import jax, jax.numpy as jnp
        import numpy as np
        import math
        EMBED_DIM = 128
        NUM_HEADS = 16
        HEAD_DIM = EMBED_DIM // NUM_HEADS
        SUB_HEAD_DIM = HEAD_DIM // 2
        SCALING = 1.0 / math.sqrt(SUB_HEAD_DIM)
        LAMBDA_INIT = 0.8 - 0.6 * math.exp(-0.3 * 0)
        key = jax.random.key(seed)
        ks = jax.random.split(key, 10)
        B, T, D = (2, 256, EMBED_DIM)
        xav = math.sqrt(6.0 / (D + D))
        return {'query': jax.random.normal(ks[0], (B, T, D), jnp.float32), 'key': jax.random.normal(ks[1], (B, T, D), jnp.float32), 'value': jax.random.normal(ks[2], (B, T, D), jnp.float32), 'in_proj_weight': jax.random.uniform(ks[3], (3 * D, D), jnp.float32, -xav, xav), 'in_proj_bias': jnp.zeros((3 * D,), jnp.float32), 'out_proj_weight': jax.random.uniform(ks[4], (D, D), jnp.float32, -xav, xav), 'out_proj_bias': jnp.zeros((D,), jnp.float32), 'lambda_q1': 0.1 * jax.random.normal(ks[5], (SUB_HEAD_DIM,), jnp.float32), 'lambda_k1': 0.1 * jax.random.normal(ks[6], (SUB_HEAD_DIM,), jnp.float32), 'lambda_q2': 0.1 * jax.random.normal(ks[7], (SUB_HEAD_DIM,), jnp.float32), 'lambda_k2': 0.1 * jax.random.normal(ks[8], (SUB_HEAD_DIM,), jnp.float32)}
    _L0_xattn_all = _L0_xattn_setup()
    _L0_xattn_in = {k: v for k, v in _L0_xattn_all.items() if k in ('in_proj_weight', 'in_proj_bias', 'out_proj_weight', 'out_proj_bias', 'lambda_q1', 'lambda_k1', 'lambda_q2', 'lambda_k2')}
    del _L0_xattn_all

    def _L0_ffn_setup():
        import jax, jax.numpy as jnp
        import numpy as np
        B, S, D, H, E, K, F = (1, 128, 128, 16, 8, 2, 512)

        def layernorm(x, g, b, eps=1e-05):
            m = x.mean(-1, keepdims=True)
            v = ((x - m) ** 2).mean(-1, keepdims=True)
            return (x - m) * jax.lax.rsqrt(v + eps) * g + b
        key = jax.random.key(seed)
        ks = jax.random.split(key, 8)
        n = lambda k, shape, sc: jax.random.normal(k, shape, dtype=jnp.float32) * sc
        return {'x': n(ks[0], (B, S, D), 1.0), 'w_qkv': n(ks[1], (D, 3 * D), D ** (-0.5)), 'w_o': n(ks[2], (D, D), D ** (-0.5)), 'g1': jnp.ones((D,), jnp.float32), 'b1': jnp.zeros((D,), jnp.float32), 'wg': n(ks[3], (D, E), D ** (-0.5)), 'w1': n(ks[4], (E, D, F), D ** (-0.5)), 'bb1': jnp.zeros((E, F), jnp.float32), 'w2': n(ks[5], (E, F, D), F ** (-0.5)), 'bb2': jnp.zeros((E, D), jnp.float32), 'g2': jnp.ones((D,), jnp.float32), 'b2': jnp.zeros((D,), jnp.float32)}
    _L0_ffn_all = _L0_ffn_setup()
    _L0_ffn_in = {k: v for k, v in _L0_ffn_all.items() if k in ('w_qkv', 'w_o', 'g1', 'b1', 'wg', 'w1', 'bb1', 'w2', 'bb2', 'g2', 'b2')}
    del _L0_ffn_all

    def _L1_xattn_setup():
        import jax, jax.numpy as jnp
        import numpy as np
        D_MODEL = 128
        NUM_HEADS = 16
        HEAD_DIM = D_MODEL // NUM_HEADS
        B, S = (4, 256)
        key = jax.random.key(seed)
        ks = jax.random.split(key, 11)
        scale = 1.0 / np.sqrt(D_MODEL)
        return {'query': jax.random.normal(ks[0], (B, S, D_MODEL), dtype=jnp.float32), 'key': jax.random.normal(ks[1], (B, S, D_MODEL), dtype=jnp.float32), 'value': jax.random.normal(ks[2], (B, S, D_MODEL), dtype=jnp.float32), 'Wq': jax.random.normal(ks[3], (D_MODEL, D_MODEL), dtype=jnp.float32) * scale, 'bq': jnp.zeros((D_MODEL,), dtype=jnp.float32), 'Wk': jax.random.normal(ks[4], (D_MODEL, D_MODEL), dtype=jnp.float32) * scale, 'bk': jnp.zeros((D_MODEL,), dtype=jnp.float32), 'Wv': jax.random.normal(ks[5], (D_MODEL, D_MODEL), dtype=jnp.float32) * scale, 'bv': jnp.zeros((D_MODEL,), dtype=jnp.float32), 'Wo': jax.random.normal(ks[6], (D_MODEL, D_MODEL), dtype=jnp.float32) * scale, 'bo': jnp.zeros((D_MODEL,), dtype=jnp.float32)}
    _L1_xattn_all = _L1_xattn_setup()
    _L1_xattn_in = {k: v for k, v in _L1_xattn_all.items() if k in ('Wq', 'bq', 'Wk', 'bk', 'Wv', 'bv', 'Wo', 'bo')}
    del _L1_xattn_all

    def _L1_ffn_setup():
        import jax, jax.numpy as jnp
        import numpy as np
        L, E, H, F, K = (4, 4, 128, 512, 2)
        B, S = (4, 256)
        EPS = 1e-05

        def _moe_layer(x, rw, rb, g, b, w1, b1, w2, b2):
            logits = jnp.einsum('bsh,he->bse', x, rw) + rb
            probs = jax.nn.softmax(logits, axis=-1)
            vals, idx = jax.lax.top_k(probs, K)
            vals = vals / vals.sum(axis=-1, keepdims=True)
            mu = x.mean(axis=-1, keepdims=True)
            xc = x - mu
            xhat = xc * jax.lax.rsqrt((xc * xc).mean(axis=-1, keepdims=True) + EPS)
            xe = xhat[None] * g[:, None, None, :] + b[:, None, None, :]
            h = jax.nn.gelu(jnp.einsum('ebsh,ehf->ebsf', xe, w1) + b1[:, None, None, :], approximate=False)
            y = jnp.einsum('ebsf,efh->ebsh', h, w2) + b2[:, None, None, :]
            expert_out = x[None] + y
            comb = jnp.einsum('bsk,bske->bse', vals, jax.nn.one_hot(idx, E, dtype=x.dtype))
            return jnp.einsum('bse,ebsh->bsh', comb, expert_out)
        key = jax.random.key(seed)
        ks = jax.random.split(key, 4)
        return {'hidden_states': jax.random.normal(ks[0], (B, S, H), jnp.float32), 'router_w': 0.02 * jax.random.normal(ks[1], (L, H, E), jnp.float32), 'router_b': jnp.zeros((L, E), jnp.float32), 'ln_g': jnp.ones((L, E, H), jnp.float32), 'ln_b': jnp.zeros((L, E, H), jnp.float32), 'w1': 0.02 * jax.random.normal(ks[2], (L, E, H, F), jnp.float32), 'b1': jnp.zeros((L, E, F), jnp.float32), 'w2': 0.02 * jax.random.normal(ks[3], (L, E, F, H), jnp.float32), 'b2': jnp.zeros((L, E, H), jnp.float32)}
    _L1_ffn_all = _L1_ffn_setup()
    _L1_ffn_in = {k: v for k, v in _L1_ffn_all.items() if k in ('router_w', 'router_b', 'ln_g', 'ln_b', 'w1', 'b1', 'w2', 'b2')}
    del _L1_ffn_all
    return {'x': x, 'ctx_1024': ctx_1024, 'L0_xattn_in_proj_weight': _L0_xattn_in['in_proj_weight'], 'L0_xattn_in_proj_bias': _L0_xattn_in['in_proj_bias'], 'L0_xattn_out_proj_weight': _L0_xattn_in['out_proj_weight'], 'L0_xattn_out_proj_bias': _L0_xattn_in['out_proj_bias'], 'L0_xattn_lambda_q1': _L0_xattn_in['lambda_q1'], 'L0_xattn_lambda_k1': _L0_xattn_in['lambda_k1'], 'L0_xattn_lambda_q2': _L0_xattn_in['lambda_q2'], 'L0_xattn_lambda_k2': _L0_xattn_in['lambda_k2'], 'L0_ffn_w_qkv': _L0_ffn_in['w_qkv'], 'L0_ffn_w_o': _L0_ffn_in['w_o'], 'L0_ffn_g1': _L0_ffn_in['g1'], 'L0_ffn_b1': _L0_ffn_in['b1'], 'L0_ffn_wg': _L0_ffn_in['wg'], 'L0_ffn_w1': _L0_ffn_in['w1'], 'L0_ffn_bb1': _L0_ffn_in['bb1'], 'L0_ffn_w2': _L0_ffn_in['w2'], 'L0_ffn_bb2': _L0_ffn_in['bb2'], 'L0_ffn_g2': _L0_ffn_in['g2'], 'L0_ffn_b2': _L0_ffn_in['b2'], 'L1_xattn_Wq': _L1_xattn_in['Wq'], 'L1_xattn_bq': _L1_xattn_in['bq'], 'L1_xattn_Wk': _L1_xattn_in['Wk'], 'L1_xattn_bk': _L1_xattn_in['bk'], 'L1_xattn_Wv': _L1_xattn_in['Wv'], 'L1_xattn_bv': _L1_xattn_in['bv'], 'L1_xattn_Wo': _L1_xattn_in['Wo'], 'L1_xattn_bo': _L1_xattn_in['bo'], 'L1_ffn_router_w': _L1_ffn_in['router_w'], 'L1_ffn_router_b': _L1_ffn_in['router_b'], 'L1_ffn_ln_g': _L1_ffn_in['ln_g'], 'L1_ffn_ln_b': _L1_ffn_in['ln_b'], 'L1_ffn_w1': _L1_ffn_in['w1'], 'L1_ffn_b1': _L1_ffn_in['b1'], 'L1_ffn_w2': _L1_ffn_in['w2'], 'L1_ffn_b2': _L1_ffn_in['b2']}

def reference(x, ctx_1024, L0_xattn_in_proj_weight, L0_xattn_in_proj_bias, L0_xattn_out_proj_weight, L0_xattn_out_proj_bias, L0_xattn_lambda_q1, L0_xattn_lambda_k1, L0_xattn_lambda_q2, L0_xattn_lambda_k2, L0_ffn_w_qkv, L0_ffn_w_o, L0_ffn_g1, L0_ffn_b1, L0_ffn_wg, L0_ffn_w1, L0_ffn_bb1, L0_ffn_w2, L0_ffn_bb2, L0_ffn_g2, L0_ffn_b2, L1_xattn_Wq, L1_xattn_bq, L1_xattn_Wk, L1_xattn_bk, L1_xattn_Wv, L1_xattn_bv, L1_xattn_Wo, L1_xattn_bo, L1_ffn_router_w, L1_ffn_router_b, L1_ffn_ln_g, L1_ffn_ln_b, L1_ffn_w1, L1_ffn_b1, L1_ffn_w2, L1_ffn_b2):
    import jax
    import jax.numpy as jnp

    def _L0_xattn_ref(query, key, value, in_proj_weight, in_proj_bias, out_proj_weight, out_proj_bias, lambda_q1, lambda_k1, lambda_q2, lambda_k2):
        import jax, jax.numpy as jnp
        import numpy as np
        import math
        EMBED_DIM = 128
        NUM_HEADS = 16
        HEAD_DIM = EMBED_DIM // NUM_HEADS
        SUB_HEAD_DIM = HEAD_DIM // 2
        SCALING = 1.0 / math.sqrt(SUB_HEAD_DIM)
        LAMBDA_INIT = 0.8 - 0.6 * math.exp(-0.3 * 0)
        B, T, D = query.shape
        S = key.shape[1]
        H, hd, sd = (NUM_HEADS, HEAD_DIM, SUB_HEAD_DIM)
        qw, kw, vw = jnp.split(in_proj_weight, 3, axis=0)
        qb, kb, vb = jnp.split(in_proj_bias, 3, axis=0)
        q = query @ qw.T + qb
        k = key @ kw.T + kb
        v = value @ vw.T + vb
        q = q.reshape(B, T, H, hd).transpose(0, 2, 1, 3)
        k = k.reshape(B, S, H, hd).transpose(0, 2, 1, 3)
        v = v.reshape(B, S, H, hd).transpose(0, 2, 1, 3)
        q1, q2 = (q[..., :sd], q[..., sd:])
        k1, k2 = (k[..., :sd], k[..., sd:])
        logits_1 = jnp.einsum('bhtd,bhsd->bhts', q1, k1) * SCALING
        logits_2 = jnp.einsum('bhtd,bhsd->bhts', q2, k2) * SCALING
        a1 = jax.nn.softmax(logits_1, axis=-1)
        a2 = jax.nn.softmax(logits_2, axis=-1)
        lam = jnp.exp(jnp.dot(lambda_q1, lambda_k1)) - jnp.exp(jnp.dot(lambda_q2, lambda_k2)) + LAMBDA_INIT
        diff_weights = a1 - lam * a2
        attn_output = jnp.einsum('bhts,bhsd->bhtd', diff_weights, v)
        attn_output = attn_output * (1.0 - LAMBDA_INIT)
        attn_output = attn_output.transpose(0, 2, 1, 3).reshape(B, T, D)
        output = attn_output @ out_proj_weight.T + out_proj_bias
        return output

    def _L0_ffn_ref(x, w_qkv, w_o, g1, b1, wg, w1, bb1, w2, bb2, g2, b2):
        import jax, jax.numpy as jnp
        import numpy as np
        B, S, D, H, E, K, F = (1, 128, 128, 16, 8, 2, 512)

        def layernorm(x, g, b, eps=1e-05):
            m = x.mean(-1, keepdims=True)
            v = ((x - m) ** 2).mean(-1, keepdims=True)
            return (x - m) * jax.lax.rsqrt(v + eps) * g + b
        b, s, d = x.shape
        hd = d // H
        qkv = x @ w_qkv
        q, k, v = jnp.split(qkv, 3, axis=-1)
        to_heads = lambda t: t.reshape(b, s, H, hd).transpose(0, 2, 1, 3)
        q, k, v = (to_heads(q), to_heads(k), to_heads(v))
        scores = jnp.einsum('bhqd,bhkd->bhqk', q, k) / jnp.sqrt(jnp.float32(hd))
        causal = jnp.tril(jnp.ones((s, s), bool))
        scores = jnp.where(causal, scores, jnp.finfo(scores.dtype).min)
        attn = jax.nn.softmax(scores, axis=-1)
        o = jnp.einsum('bhqk,bhkd->bhqd', attn, v)
        o = o.transpose(0, 2, 1, 3).reshape(b, s, d) @ w_o
        h = layernorm(x + o, g1, b1)
        probs = jax.nn.softmax(h @ wg, axis=-1)
        topv, topi = jax.lax.top_k(probs, K)
        topv = topv / topv.sum(-1, keepdims=True)
        w = (topv[..., None] * jax.nn.one_hot(topi, E, dtype=h.dtype)).sum(-2)
        h1 = jax.nn.gelu(jnp.einsum('bsd,edf->ebsf', h, w1) + bb1[:, None, None, :])
        y = jnp.einsum('ebsf,efd->ebsd', h1, w2) + bb2[:, None, None, :]
        moe = jnp.einsum('ebsd,bse->bsd', y, w)
        return layernorm(h + moe, g2, b2)

    def _L1_xattn_ref(query, key, value, Wq, bq, Wk, bk, Wv, bv, Wo, bo):
        import jax, jax.numpy as jnp
        import numpy as np
        D_MODEL = 128
        NUM_HEADS = 16
        HEAD_DIM = D_MODEL // NUM_HEADS
        B, S = (4, 256)
        b = query.shape[0]
        Q = (query @ Wq + bq).reshape(b, -1, NUM_HEADS, HEAD_DIM).transpose(0, 2, 1, 3)
        K = (key @ Wk + bk).reshape(b, -1, NUM_HEADS, HEAD_DIM).transpose(0, 2, 1, 3)
        V = (value @ Wv + bv).reshape(b, -1, NUM_HEADS, HEAD_DIM).transpose(0, 2, 1, 3)
        scores = jnp.einsum('bhqd,bhkd->bhqk', Q, K) / jnp.sqrt(jnp.asarray(HEAD_DIM, dtype=jnp.float32))
        attn = jax.nn.softmax(scores, axis=-1)
        out = jnp.einsum('bhqk,bhkd->bhqd', attn, V)
        out = out.transpose(0, 2, 1, 3).reshape(b, -1, D_MODEL)
        return out @ Wo + bo

    def _L1_ffn_ref(hidden_states, router_w, router_b, ln_g, ln_b, w1, b1, w2, b2):
        import jax, jax.numpy as jnp
        import numpy as np
        L, E, H, F, K = (4, 4, 128, 512, 2)
        B, S = (4, 256)
        EPS = 1e-05

        def _moe_layer(x, rw, rb, g, b, w1, b1, w2, b2):
            logits = jnp.einsum('bsh,he->bse', x, rw) + rb
            probs = jax.nn.softmax(logits, axis=-1)
            vals, idx = jax.lax.top_k(probs, K)
            vals = vals / vals.sum(axis=-1, keepdims=True)
            mu = x.mean(axis=-1, keepdims=True)
            xc = x - mu
            xhat = xc * jax.lax.rsqrt((xc * xc).mean(axis=-1, keepdims=True) + EPS)
            xe = xhat[None] * g[:, None, None, :] + b[:, None, None, :]
            h = jax.nn.gelu(jnp.einsum('ebsh,ehf->ebsf', xe, w1) + b1[:, None, None, :], approximate=False)
            y = jnp.einsum('ebsf,efh->ebsh', h, w2) + b2[:, None, None, :]
            expert_out = x[None] + y
            comb = jnp.einsum('bsk,bske->bse', vals, jax.nn.one_hot(idx, E, dtype=x.dtype))
            return jnp.einsum('bse,ebsh->bsh', comb, expert_out)
        x = hidden_states
        for l in range(L):
            x = _moe_layer(x, router_w[l], router_b[l], ln_g[l], ln_b[l], w1[l], b1[l], w2[l], b2[l])
        return x
    x = x + _L0_xattn_ref(_layernorm(x, axis=-1), ctx_1024, ctx_1024, L0_xattn_in_proj_weight, L0_xattn_in_proj_bias, L0_xattn_out_proj_weight, L0_xattn_out_proj_bias, L0_xattn_lambda_q1, L0_xattn_lambda_k1, L0_xattn_lambda_q2, L0_xattn_lambda_k2)
    x = x + _L0_ffn_ref(_layernorm(x, axis=-1), L0_ffn_w_qkv, L0_ffn_w_o, L0_ffn_g1, L0_ffn_b1, L0_ffn_wg, L0_ffn_w1, L0_ffn_bb1, L0_ffn_w2, L0_ffn_bb2, L0_ffn_g2, L0_ffn_b2)
    x = x + _L1_xattn_ref(_layernorm(x, axis=-1), ctx_1024, ctx_1024, L1_xattn_Wq, L1_xattn_bq, L1_xattn_Wk, L1_xattn_bk, L1_xattn_Wv, L1_xattn_bv, L1_xattn_Wo, L1_xattn_bo)
    x = x + _L1_ffn_ref(_layernorm(x, axis=-1), L1_ffn_router_w, L1_ffn_router_b, L1_ffn_ln_g, L1_ffn_ln_b, L1_ffn_w1, L1_ffn_b1, L1_ffn_w2, L1_ffn_b2)
    return x

_drawn_inputs = setup_inputs


def setup_inputs(seed=0):
    import zlib

    import numpy as np

    out = dict(_drawn_inputs(seed))
    spreads = {'L0_xattn_in_proj_bias': (0.0, 0.1),
     'L0_xattn_out_proj_bias': (0.0, 0.1),
     'L0_ffn_g1': (1.0, 0.2),
     'L0_ffn_b1': (0.0, 0.1),
     'L0_ffn_bb1': (0.0, 0.352),
     'L0_ffn_bb2': (0.0, 0.1),
     'L0_ffn_g2': (1.0, 0.2),
     'L0_ffn_b2': (0.0, 0.1),
     'L1_xattn_bq': (0.0, 0.663),
     'L1_xattn_bk': (0.0, 2.0),
     'L1_xattn_bv': (0.0, 0.1),
     'L1_xattn_bo': (0.0, 0.1),
     'L1_ffn_router_b': (0.0, 0.286),
     'L1_ffn_ln_g': (1.0, 0.6),
     'L1_ffn_ln_b': (0.0, 2.0),
     'L1_ffn_b1': (0.0, 0.608),
     'L1_ffn_b2': (0.0, 0.1)}
    factors = {'L0_xattn_lambda_q1': 7.043,
     'L0_xattn_lambda_k1': 7.043,
     'L0_xattn_lambda_q2': 3.128,
     'L0_xattn_lambda_k2': 3.128}
    for name, (base, spread) in spreads.items():
        noise = np.random.default_rng([zlib.crc32(name.encode()), seed]).standard_normal(out[name].shape)
        drawn = base * np.exp(spread * noise) if base else spread * noise
        out[name] = jnp.asarray(drawn.astype(out[name].dtype))
    for name, factor in factors.items():
        out[name] = (out[name] * factor).astype(out[name].dtype)
    return out
```

```python
from contextlib import ExitStack

import concourse.bass as bass
from concourse import mybir

F32 = mybir.dt.float32
BF16 = mybir.dt.bfloat16
ALU = mybir.AluOpType
ACT = mybir.ActivationFunctionType
AX = mybir.AxisListType

P = 128
HEADS = 16
HD = P // HEADS
QUAD = 32
BANK = 512
EPS = 1e-5
LAMBDA_INIT = 0.2
CB = 4
CT = CB * P
NEG = -1.0e30


def after(eng, sem, value):
    if not isinstance(value, int) or value > 0:
        eng.wait_ge(sem, value)


def pairs(eng, slot, n):
    slot(0, 0)
    slot(0, 1)
    with eng.Fori(1, n // 2 - 1) as i:
        slot(i, 0)
        slot(i, 1)
    slot(n // 2 - 1, 0)
    slot(n // 2 - 1, 1)


def apart(nc, env):
    nc.vector.memset(env.scratch[:, :], 0.0)


class Chain:

    def __init__(self, eng, sem):
        self.eng, self.sem, self.base, self.n = eng, sem, 0, 0

    def slot(self, base):
        self.base, self.n = base, 0

    def link(self, ins):
        self.n += 1
        ins.then_inc(self.sem, 1)
        self.eng.wait_ge(self.sem, self.base + self.n)


def clear(nc, sems):
    with nc.Block() as block:
        @block.sync
        def _(sp):
            for s in sems:
                sp.sem_clear(s)


class Env:
    pass


def attention(nc, env, tag, NB, S, NS, causal, diff, norm, d):
    DS = P // NS
    J = NS // 4
    JG = J // 4
    NM = NS // 4
    NP = NM // 2
    SCALE = 1.0 / float(DS) ** 0.5
    X, H, ident = env.X, env.H, env.ident
    W = S + P
    kv = P if not causal else 0
    WS = W if not causal else P

    with ExitStack() as ctx:
        def sb(name, shape, dt=F32):
            return ctx.enter_context(nc.sbuf_tensor(f"{tag}_{name}", shape, dt))

        def ps(name, shape):
            return ctx.enter_context(nc.psum_tensor(f"{tag}_{name}", shape, F32))

        sems = []

        def sem(name):
            sems.append(ctx.enter_context(nc.semaphore(f"{tag}_{name}")))
            return sems[-1]

        wT = sb("wT", [P, 4, P])
        qkb = sb("qkb", [P, 2])
        qbs = sb("qbs", [P, 1])
        rows = sb("rows", [1, 3, P])
        mask_j = sb("mask_j", [P, J])
        mask_m = sb("mask_m", [2 * QUAD, J])
        sel_q = sb("sel_q", [2 * QUAD, 4, S], BF16)
        xn = sb("xn", [P, 2, P])
        stats = sb("stats", [P, 6])
        mv = sb("mv", [P, 2, 2])
        veps = sb("veps", [P, 1])
        rstd = sb("rstd", [P, 2])
        cx = sb("cx", [P, 2, P])
        srcT = sb("srcT", [P, 2, W])
        Qb = sb("Qb", [P, 2, P])
        Kb = sb("Kb", [P, 2, S])
        Va = sb("Va", [P, 2, HEADS, HD + 1])
        Qm = sb("Qm", [P, 2, J, P])
        Km = sb("Km", [P, 2, J, S])
        M = sb("M", [P, NS])
        nM = sb("nM", [P, 2, P], BF16)
        Mm = sb("Mm", [2 * QUAD, 2, J, P], BF16)
        E = sb("E", [P, 2, NS, P])
        rec = sb("rec", [P, NS])
        pv = sb("pv", [P, NS, HD])
        att = sb("att", [P, HEADS, HD])
        attT = sb("attT", [P, P])
        if causal:
            cm = sb("cm", [P, 2, 4, P], BF16)
            z = sb("z", [P, P])
            gb = sb("gb", [P, 2, P])
        if norm:
            stats2 = sb("stats2", [P, 6])
            mv2 = sb("mv2", [P, 2])
            veps2 = sb("veps2", [P, 1])
            rstd2 = sb("rstd2", [P, 1])
        if diff:
            lq = sb("lq", [P, 4, DS])
            lp = sb("lp", [P, 2, DS])
            ld = sb("ld", [P, 2])
            le = sb("le", [P, 2])
            nlam = sb("nlam", [P, 1])

        psA = ps("psA", [P, 2, BANK])
        psB = ps("psB", [P, 4, BANK])
        psH = ps("psH", [P, BANK])
        psO = ps("psO", [P, BANK])
        psHb = psH[:, :].bitcast(BF16)

        w_in = sem("w_in")
        x_first = sem("x_first")
        x_rest = sem("x_rest")
        ctx_in = [sem("ctx_in0"), sem("ctx_in1")]
        setup_done = sem("setup_done")
        lam_dots = sem("lam_dots")
        lam_exp = sem("lam_exp")
        stats_ready = sem("stats_ready")
        rstd_ready = sem("rstd_ready")
        xn_ready = sem("xn_ready")
        xn_kept = sem("xn_kept")
        src_transposed = sem("src_transposed")
        srcT_ready = sem("srcT_ready")
        projected = sem("projected")
        qkv_ready = sem("qkv_ready")
        km_ready = sem("km_ready")
        qm_ready = sem("qm_ready")
        a_full = sem("a_full")
        a_free = sem("a_free")
        nm_ready = sem("nm_ready")
        m_transposed = sem("m_transposed")
        mm_ready = sem("mm_ready")
        b_full = sem("b_full")
        e_ready = sem("e_ready")
        pv_done = sem("pv_done")
        att_ready = sem("att_ready")
        att_transposed = sem("att_transposed")
        attT_ready = sem("attT_ready")
        y_ready = sem("y_ready")
        x_done = sem("x_done")
        stats2_ready = sem("stats2_ready")
        rstd2_ready = sem("rstd2_ready")
        dve_chain = sem("dve_chain")
        pool_chain = sem("pool_chain")

        n_w = 6 + (1 if causal else 0) * 2 + (4 if diff else 0)
        stage = ExitStack()
        block = stage.enter_context(nc.Block())

        @block.sync
        def _(sp):
            if diff:
                sp.dma_start(X[:, 0:4, :], d["x"][0:4].rearrange("b t c -> t b c")).then_inc(x_first, 16)
            sp.dma_start(wT[:, :, :], d["w"]).then_inc(w_in, 16)
            sp.dma_start(qkb[:, :], d["qkb"]).then_inc(w_in, 16)
            sp.dma_start(rows[:, :, :], d["rows"]).then_inc(w_in, 16)
            sp.dma_start(mask_j[:, :], d["mask_j"]).then_inc(w_in, 16)
            sp.dma_start(mask_m[:, :], d["mask_m"]).then_inc(w_in, 16)
            sp.dma_start(sel_q[:, :, :], d["sel_q"]).then_inc(w_in, 16)
            if causal:
                sp.dma_start(cm[:, :, :, :], d["cm"]).then_inc(w_in, 16)
                sp.dma_start(gb[:, :, :], d["gb"].partition_broadcast(P)).then_inc(w_in, 16)
            if diff:
                for n in range(4):
                    sp.dma_start(lq[:, n, :], d["lam"][n].partition_broadcast(P)).then_inc(w_in, 16)
                sp.dma_start(X[:, 4:NB, :], d["x"][4:NB].rearrange("b t c -> t b c")).then_inc(x_rest, 16)

            def slot(i, u):
                n = 2 * i + u
                after(sp, src_transposed, n - 1)
                sp.dma_start(cx[0:S, u, :], d["ctx"][n]).then_inc(ctx_in[u], 16)

            if not causal:
                pairs(sp, slot, NB)

        @block.gpsimd
        def _(pool):
            chain = Chain(pool, pool_chain)
            LINKS = 2 if norm else 1

            def head_rstd(n, u):
                pool.wait_ge(stats_ready, n + 1)
                chain.link(nc.gpsimd.tensor_tensor(veps[:, :], mv[:, u, 1:2], env.eps[:, :], ALU.add))
                nc.gpsimd.tensor_tensor(rstd[:, u:u + 1], veps[:, :], env.minus_half[:, :],
                                        ALU.pow).then_inc(rstd_ready, 1)

            def keep(n, u):
                pool.wait_ge(xn_ready, n + 1)
                nc.gpsimd.tensor_copy(H[:, n, :], xn[:, u, :]).then_inc(xn_kept, 1)

            def head_masks(n, u):
                pool.wait_ge(qkv_ready, n + 1)
                nc.gpsimd.tensor_tensor(
                    Km[:, u, :, :], Kb[:, u, :].unsqueeze(1).to_broadcast([P, J, S]),
                    mask_j[:, :].unsqueeze(2).to_broadcast([P, J, S]), ALU.mult).then_inc(km_ready, 1)
                nc.gpsimd.tensor_tensor(
                    Qm[:, u, :, :], Qb[:, u, :].unsqueeze(1).to_broadcast([P, J, P]),
                    mask_j[:, :].unsqueeze(2).to_broadcast([P, J, P]), ALU.mult).then_inc(qm_ready, 1)

            def tail_rstd(b):
                pool.wait_ge(stats2_ready, b + 1)
                chain.link(nc.gpsimd.tensor_tensor(veps2[:, :], mv2[:, 1:2], env.eps[:, :], ALU.add))
                nc.gpsimd.tensor_tensor(rstd2[:, :], veps2[:, :], env.minus_half[:, :],
                                        ALU.pow).then_inc(rstd2_ready, 1)

            pool.wait_ge(w_in, 16 * n_w)
            chain.slot(0)
            for n in range(2):
                head_rstd(n, n)
                if causal:
                    keep(n, n)
            head_masks(0, 0)

            def slot(i, u):
                b = 2 * i + u
                last = isinstance(b, int) and b >= NB - 2
                end = isinstance(b, int) and b >= NB - 1
                chain.slot(2 + b * LINKS if not end else 2 + (NB - 2) * LINKS + LINKS - 1)
                if not last:
                    head_rstd(b + 2, u)
                if not end:
                    head_masks(b + 1, 1 - u)
                if causal and not last:
                    keep(b + 2, u)
                if norm:
                    tail_rstd(b)

            pairs(pool, slot, NB)

        @block.scalar
        def _(act):
            def head_src(n, u):
                act.wait_ge(src_transposed, n + 1)
                nc.scalar.activation(srcT[:, u, 0:WS], psH[:, 0:WS], ACT.Copy).then_inc(srcT_ready, 1)

            def head_qkv(n, u):
                act.wait_ge(projected, n + 1)
                nc.scalar.activation(Kb[:, u, :], psH[:, P:P + S], ACT.Identity, bias=qkb[:, 1:2])
                nc.scalar.activation(Qb[:, u, :], psH[:, 0:P], ACT.Identity, bias=qbs[:, 0:1], scale=SCALE)
                nc.scalar.activation(Va[0:S, u, :, 0:HD],
                                     psH[0:S, 2 * P:3 * P].rearrange("s (h e) -> s h e", e=HD),
                                     ACT.Copy).then_inc(qkv_ready, 1)

            def exps(b, u, g):
                act.wait_ge(b_full, b * NP + g + 1)
                if NP == 2 or u < 2:
                    k = g % 2
                nc.scalar.activation(
                    E[0:S, u, 8 * g:8 * g + 8, :].rearrange("s (k m) t -> s k (m t)", k=2),
                    psB[0:S, 2 * k:2 * k + 2, :], ACT.Exp).then_inc(e_ready, 1)

            if diff:
                act.wait_ge(lam_dots, 1)
                nc.scalar.activation(le[:, :], ld[:, :], ACT.Exp).then_inc(lam_exp, 1)
            act.wait_ge(setup_done, 1)
            head_src(0, 0)
            head_qkv(0, 0)

            def slot(i, u):
                b = 2 * i + u
                end = isinstance(b, int) and b >= NB - 1
                if not end:
                    head_src(b + 1, 1 - u)
                for g in range(NP // 2):
                    exps(b, u, g)
                if not end:
                    head_qkv(b + 1, 1 - u)
                for g in range(NP // 2, NP):
                    exps(b, u, g)

            pairs(act, slot, NB)

        @block.vector
        def _(dve):
            chain = Chain(dve, dve_chain)

            def head_stats(n, u):
                chain.link(nc.vector.bn_stats(stats[:, :], X[:, n, :]))
                apart(nc, env)
                nc.vector.bn_aggr(mv[:, u, :], stats[:, :]).then_inc(stats_ready, 1)

            def head_norm(n, u):
                dve.wait_ge(rstd_ready, n + 1)
                after(dve, src_transposed, n - 1)
                if causal:
                    after(dve, xn_kept, n - 1)
                nc.vector.tensor_scalar(xn[:, u, :], X[:, n, :], mv[:, u, 0:1], rstd[:, u:u + 1],
                                        ALU.subtract, ALU.mult).then_inc(xn_ready, 1)

            def head_max(n, u):
                for m in range(NM):
                    dve.wait_ge(a_full, n * NM + m + 1)
                    nc.vector.tensor_reduce(M[:, 4 * m:4 * m + 4],
                                            psA[:, m % 2, 0:4 * S].rearrange("t (j s) -> t j s", j=4),
                                            AX.X, ALU.max).then_inc(a_free, 1)
                dve.wait_ge(a_free, (n + 1) * NM)
                chain.link(nc.vector.tensor_scalar(nM[:, u, 0:NS], M[:, :], -1.0, None, ALU.mult))
                nc.vector.scalar_tensor_tensor(nM[:, u, QUAD:QUAD + NS], M[:, :], -1.0, nM[:, u, 0:NS],
                                               ALU.mult, ALU.subtract).then_inc(nm_ready, 1)

            def head_mask_m(n, u):
                dve.wait_ge(m_transposed, n + 1)
                nc.vector.tensor_tensor(
                    Mm[:, u, :, :], psHb[0:2 * QUAD, 0:P].unsqueeze(1).to_broadcast([2 * QUAD, J, P]),
                    mask_m[:, :].unsqueeze(2).to_broadcast([2 * QUAD, J, P]), ALU.mult).then_inc(mm_ready, 1)

            def tail_att(b, u):
                dve.wait_ge(pv_done, b + 1)
                O = psO[:, 0:NS * (HD + 1)].rearrange("t (n e) -> t n e", e=HD + 1)
                chain.link(nc.vector.reciprocal(rec[:, :], O[:, :, HD]))
                to = pv if diff else att
                ins = nc.vector.tensor_tensor(to[:, :, :], O[:, :, 0:HD],
                                              rec[:, :].unsqueeze(2).to_broadcast([P, NS, HD]), ALU.mult)
                if diff:
                    chain.link(ins)
                    two = pv[:, :, :].rearrange("t (h k) e -> t h k e", k=2)
                    ins = nc.vector.scalar_tensor_tensor(att[:, :, :], two[:, :, 1, :], nlam[:, 0:1],
                                                         two[:, :, 0, :], ALU.mult, ALU.add)
                ins.then_inc(att_ready, 1)

            def tail_attT(b):
                dve.wait_ge(att_transposed, b + 1)
                nc.vector.tensor_scalar(attT[:, :], psO[:, 0:P], (1.0 - LAMBDA_INIT) if diff else 1.0,
                                        None, ALU.mult).then_inc(attT_ready, 1)

            def tail_out(b):
                dve.wait_ge(y_ready, b + 1)
                y = psO[:, P:2 * P]
                if not causal:
                    nc.vector.tensor_tensor(X[:, b, :], X[:, b, :], y, ALU.add).then_inc(x_done, 1)
                    if not norm:
                        return
                    dve.wait_ge(x_done, b + 1)
                    apart(nc, env)
                    chain.link(nc.vector.bn_stats(stats2[:, :], X[:, b, :]))
                    apart(nc, env)
                    nc.vector.bn_aggr(mv2[:, :], stats2[:, :]).then_inc(stats2_ready, 1)
                    dve.wait_ge(rstd2_ready, b + 1)
                    chain.link(nc.vector.tensor_scalar(H[:, b, :], X[:, b, :], mv2[:, 0:1], rstd2[:, 0:1],
                                                       ALU.subtract, ALU.mult))
                    return
                dve.wait_ge(xn_kept, b + 1)
                nc.vector.tensor_tensor(z[:, :], H[:, b, :], y, ALU.add).then_inc(x_done, 1)
                dve.wait_ge(x_done, b + 1)
                chain.link(nc.vector.bn_stats(stats2[:, :], z[:, :]))
                apart(nc, env)
                nc.vector.bn_aggr(mv2[:, :], stats2[:, :]).then_inc(stats2_ready, 1)
                dve.wait_ge(rstd2_ready, b + 1)
                chain.link(nc.vector.tensor_scalar(z[:, :], z[:, :], mv2[:, 0:1], rstd2[:, 0:1],
                                                   ALU.subtract, ALU.mult))
                chain.link(nc.vector.tensor_tensor(z[:, :], z[:, :], gb[:, 0, :], ALU.mult))
                chain.link(nc.vector.tensor_tensor(H[:, b, :], z[:, :], gb[:, 1, :], ALU.add))

            dve.wait_ge(w_in, 16 * n_w)
            chain.slot(0)
            nc.vector.memset(Va[:, :, :, HD:HD + 1], 1.0)
            chain.link(nc.vector.memset(nM[:, :, :], 0.0))
            if diff:
                for n in range(2):
                    chain.link(nc.vector.tensor_tensor(lp[:, n, :], lq[:, 2 * n, :], lq[:, 2 * n + 1, :], ALU.mult))
                nc.vector.tensor_reduce(ld[:, :], lp[:, :, :], AX.X, ALU.add).then_inc(lam_dots, 1)
                dve.wait_ge(lam_exp, 1)
                chain.link(nc.vector.tensor_tensor(nlam[:, :], le[:, 1:2], le[:, 0:1], ALU.subtract))
                chain.link(nc.vector.tensor_scalar(nlam[:, :], nlam[:, :], -LAMBDA_INIT, None, ALU.add))
            nc.vector.tensor_scalar(qbs[:, :], qkb[:, 0:1], SCALE, None, ALU.mult).then_inc(setup_done, 1)
            if diff:
                dve.wait_ge(x_first, 16)
            for n in range(2):
                head_stats(n, n)
                head_norm(n, n)
            head_max(0, 0)
            head_mask_m(0, 0)
            SETUP = chain.n
            LINKS = [None]

            def slot(i, u):
                b = 2 * i + u
                last = isinstance(b, int) and b >= NB - 2
                end = isinstance(b, int) and b >= NB - 1
                per = LINKS[0] or 0
                chain.slot(SETUP + b * per if not end else SETUP + (NB - 2) * per + per - 1)
                if diff and isinstance(b, int) and b == 0:
                    dve.wait_ge(x_rest, 16)
                if not last:
                    head_stats(b + 2, u)
                if not end:
                    head_max(b + 1, 1 - u)
                if not last:
                    head_norm(b + 2, u)
                tail_att(b, u)
                if not end:
                    head_mask_m(b + 1, 1 - u)
                tail_attT(b)
                tail_out(b)
                if LINKS[0] is None:
                    LINKS[0] = chain.n

            pairs(dve, slot, NB)

        @block.tensor
        def _(pe):
            def head_transpose(n, h, u):
                pe.wait_ge(xn_ready, n + 1)
                after(pe, mm_ready, n)
                mm = nc.tensor.transpose(psH[:, 0:P], xn[:, u, :], ident[:, :])
                if not causal:
                    pe.wait_ge(ctx_in[u], 16 * (h + 1))
                    mm = nc.tensor.transpose(psH[:, P:P + S], cx[0:S, u, :], ident[0:S, 0:S])
                mm.then_inc(src_transposed, 1)

            def head_project(n, u):
                pe.wait_ge(srcT_ready, n + 1)
                nc.tensor.matmul(psH[:, 0:P], wT[:, 0, :], srcT[:, u, 0:P], start=True, stop=True)
                nc.tensor.matmul(psH[:, P:P + S], wT[:, 1, :], srcT[:, u, kv:kv + S], start=True, stop=True)
                nc.tensor.matmul(psH[0:S, 2 * P:3 * P], srcT[:, u, kv:kv + S], wT[:, 2, :], start=True, stop=False)
                nc.tensor.matmul(psH[0:S, 2 * P:3 * P], rows[0:1, 2, 0:S], rows[0:1, 0, :], start=False,
                                 stop=True).then_inc(projected, 1)

            def scores(n, u):
                pe.wait_ge(qkv_ready, n + 1)
                pe.wait_ge(km_ready, n + 1)
                for m in range(NM):
                    q, g = m // JG, m % JG
                    after(pe, a_free, n * NM + m - 1)
                    mm = nc.tensor.matmul(psA[:, m % 2, 0:4 * S], Qb[QUAD * q:QUAD * q + QUAD, u, :],
                                          Km[QUAD * q:QUAD * q + QUAD, u, 4 * g:4 * g + 4, :],
                                          start=True, stop=not causal)
                    if causal:
                        mm = nc.tensor.matmul(psA[:, m % 2, :], env.identb[:, :], cm[:, 0, :, :],
                                              start=False, stop=True)
                    mm.then_inc(a_full, 1)

            def head_m(n, u):
                pe.wait_ge(nm_ready, n + 1)
                nc.tensor.transpose(psHb[:, 0:P], nM[:, u, :], env.identb[:, :]).then_inc(m_transposed, 1)

            def scores_less_max(b, u, pairs_):
                pe.wait_ge(mm_ready, b + 1)
                pe.wait_ge(qm_ready, b + 1)
                for k in pairs_:
                    after(pe, e_ready, b * NP + k - 1)
                    for m in (2 * k, 2 * k + 1):
                        q, g = m // JG, m % JG
                        out = psB[0:S, m % 4, :]
                        nc.tensor.matmul(out, Kb[QUAD * q:QUAD * q + QUAD, u, :],
                                         Qm[QUAD * q:QUAD * q + QUAD, u, 4 * g:4 * g + 4, :],
                                         start=True, stop=False)
                        mm = nc.tensor.matmul(out, sel_q[:, q, :], Mm[:, u, 4 * g:4 * g + 4, :],
                                              start=False, stop=not causal)
                        if causal:
                            mm = nc.tensor.matmul(out, env.identb[:, :], cm[:, 1, :, :], start=False, stop=True)
                    mm.then_inc(b_full, 1)

            def weigh_values(b, u):
                after(pe, x_done, b)
                for n in range(NS):
                    if n % 8 == 0:
                        pe.wait_ge(e_ready, b * NP + n // 8 + 1)
                    mm = nc.tensor.matmul(psO[:, n * (HD + 1):(n + 1) * (HD + 1)], E[0:S, u, n, :],
                                          Va[0:S, u, n * HEADS // NS, :], start=True, stop=True)
                mm.then_inc(pv_done, 1)

            def project_out(b):
                pe.wait_ge(att_ready, b + 1)
                nc.tensor.transpose(psO[:, 0:P], att[:, :, :].rearrange("t h e -> t (h e)"),
                                    ident[:, :]).then_inc(att_transposed, 1)
                pe.wait_ge(attT_ready, b + 1)
                nc.tensor.matmul(psO[:, P:2 * P], attT[:, :], wT[:, 3, :], start=True, stop=False)
                nc.tensor.matmul(psO[:, P:2 * P], rows[0:1, 2, :], rows[0:1, 1, :], start=False,
                                 stop=True).then_inc(y_ready, 1)

            pe.wait_ge(w_in, 16 * n_w)
            head_transpose(0, 0, 0)
            head_project(0, 0)
            scores(0, 0)
            head_m(0, 0)

            def slot(i, u):
                b = 2 * i + u
                end = isinstance(b, int) and b >= NB - 1
                if not end:
                    head_transpose(b + 1, i + u, 1 - u)
                scores_less_max(b, u, range(NP // 2))
                if not end:
                    head_project(b + 1, 1 - u)
                scores_less_max(b, u, range(NP // 2, NP))
                if not end:
                    scores(b + 1, 1 - u)
                weigh_values(b, u)
                if not end:
                    head_m(b + 1, 1 - u)
                project_out(b)

            pairs(pe, slot, NB)

        stage.close()
        clear(nc, sems)


def mixture(nc, env, tag, E, L, d):
    X, H, ident = env.X, env.H, env.ident
    post = L == 1
    NCH = env.NB // CB
    K = L * NCH
    FT = 4
    GELU = ACT.Gelu_apprx_tanh if post else ACT.Gelu
    AT = dict(x=1, logits=2, xh=None, gates=5) if post else dict(x=0, logits=1, xh=2, gates=3)
    TANH_AT = AT["logits"] + 1

    with ExitStack() as ctx:
        def sb(name, shape, dt=F32):
            return ctx.enter_context(nc.sbuf_tensor(f"{tag}_{name}", shape, dt))

        def ps(name, shape):
            return ctx.enter_context(nc.psum_tensor(f"{tag}_{name}", shape, F32))

        sems = []

        def sem(name):
            sems.append(ctx.enter_context(nc.semaphore(f"{tag}_{name}")))
            return sems[-1]

        w1 = sb("w1", [P, E, FT * P])
        w2 = sb("w2", [P, E, FT, P])
        b1 = sb("b1", [P, L * E * FT])
        b2 = sb("b2", [E, P])
        rw = sb("rw", [P, L * E])
        rank = sb("rank", [P, E])
        sel = sb("sel", [E, E, P])
        xs = sb("xs", [P, 2, CB, P])
        xT = sb("xT", [P, 2, CT])
        lg = sb("lg", [P, CB, E])
        l2 = sb("l2", [P, CB, E])
        t1 = sb("t1", [P, CB, E])
        k1 = sb("k1", [P, CB, E])
        k2 = sb("k2", [P, CB, E])
        m1 = sb("m1", [P, CB])
        m2 = sb("m2", [P, CB])
        r1 = sb("r1", [P, CB])
        gap = sb("gap", [P, CB])
        th = sb("th", [P, CB])
        wa = sb("wa", [P, CB])
        wb = sb("wb", [P, CB])
        sw = sb("sw", [P, 2, CB])
        comb = sb("comb", [P, CB, E])
        gT = sb("gT", [E, 2, CT])
        h1 = sb("h1", [P, 2, FT, CT])
        yT = sb("yT", [P, CT])
        st = sb("st", [P, CB, 6])
        mv = sb("mv", [P, CB, 2])
        veps = sb("veps", [P, CB])
        rstd = sb("rstd", [P, CB])
        if post:
            z = sb("z", [P, CB, P])
            gb = sb("gb", [P, 2, P])
        else:
            lng = sb("lng", [P, L * E])
            lnb = sb("lnb", [P, L * E])
            rb = sb("rb", [P, L * E])
            xh = sb("xh", [P, CB, P])
            xhT = sb("xhT", [P, 2, CT])
            mark = sb("mark", [P, NCH])
            xe = sb("xe", [P, 2, CT])

        psR = ps("psR", [P, FT, BANK])
        psG = ps("psG", [P, 2, BANK])
        psY = ps("psY", [P, BANK])
        psH = ps("psH", [P, BANK])

        c_in = sem("c_in")
        w_in = [sem(f"w_in{e}") for e in range(E)]
        b2_in = sem("b2_in")
        xs_in = [sem("xs_in0"), sem("xs_in1")]
        stats_ready = sem("stats_ready")
        rstd_ready = sem("rstd_ready")
        xh_ready = sem("xh_ready")
        x_transposed = sem("x_transposed")
        xT_ready = sem("xT_ready")
        logits_full = sem("logits_full")
        logits_read = sem("logits_read")
        gap_ready = sem("gap_ready")
        tanh_ready = sem("tanh_ready")
        comb_ready = sem("comb_ready")
        xh_transposed = sem("xh_transposed")
        xhT_ready = sem("xhT_ready")
        g_transposed = sem("g_transposed")
        gT_ready = sem("gT_ready")
        g_full = sem("g_full")
        xe_ready = sem("xe_ready")
        r_full = sem("r_full")
        h1_ready = sem("h1_ready")
        hg_ready = sem("hg_ready")
        expert_done = sem("expert_done")
        y_full = sem("y_full")
        yT_ready = sem("yT_ready")
        z_full = sem("z_full")
        z_read = sem("z_read")
        x_done = sem("x_done")
        dve_chain = sem("dve_chain")
        pool_chain = sem("pool_chain")
        sum_ready = sem("sum_ready")
        out_written = sem("out_written")
        n_c = 5 + (1 if post else 3) + (0 if not post else 0)

        stage = ExitStack()
        block = stage.enter_context(nc.Block())

        def load_expert(sp, l, e):
            sp.dma_start(w1[:, e, :], d["w1"][l * E + e]).then_inc(w_in[e], 16)
            sp.dma_start(w2[:, e, :, :], d["w2"][l * E + e].rearrange("(t p) m -> p t m", p=P)).then_inc(w_in[e], 16)

        @block.sync
        def _(sp):
            sp.dma_start(b1[:, :], d["b1"]).then_inc(c_in, 16)
            sp.dma_start(rw[:, :], d["rw"]).then_inc(c_in, 16)
            sp.dma_start(rank[:, :], d["rank"]).then_inc(c_in, 16)
            sp.dma_start(sel[:, :, :], d["sel"]).then_inc(c_in, 16)
            if post:
                sp.dma_start(gb[:, :, :], d["gb"].partition_broadcast(P)).then_inc(c_in, 16)
            else:
                sp.dma_start(lng[:, :], d["lng"]).then_inc(c_in, 16)
                sp.dma_start(lnb[:, :], d["lnb"]).then_inc(c_in, 16)
                sp.dma_start(rb[:, :], d["rb"].partition_broadcast(P)).then_inc(c_in, 16)
            sp.dma_start(b2[:, :], d["b2"][0]).then_inc(b2_in, 16)
            for e in range(E):
                load_expert(sp, 0, e)
            if L > 1:
                with sp.Fori(1, L) as l:
                    for e in range(E):
                        sp.wait_ge(expert_done, (l * NCH - 1) * E + e + 1)
                        load_expert(sp, l, e)
                    sp.wait_ge(y_full, l * NCH)
                    sp.dma_start(b2[:, :], d["b2"][l]).then_inc(b2_in, 16)
                for c in range(NCH):
                    sp.wait_ge(sum_ready, c + 1)
                    sp.dma_start(d["out"][CB * c:CB * c + CB].rearrange("b t m -> t b m"),
                                 X[:, CB * c:CB * c + CB, :]).then_inc(out_written, 16)
                sp.wait_ge(out_written, 16 * NCH)

        @block.gpsimd
        def _(pool):
            chain = Chain(pool, pool_chain)

            def load_source(n, u):
                after(pool, x_transposed, n - 1)
                if not post:
                    pool.wait_ge(x_done, n + 1)
                c = n % NCH
                pool.dma_start(xs[:, u, :, :], H[:, bass.ds(CB * c, CB), :]).then_inc(xs_in[u], 16)

            def rstds(n):
                pool.wait_ge(stats_ready, n + 1)
                chain.link(nc.gpsimd.tensor_tensor(veps[:, :], mv[:, :, 1], env.eps[:, 0:1].to_broadcast([P, CB]), ALU.add))
                nc.gpsimd.tensor_tensor(rstd[:, :], veps[:, :], env.minus_half[:, 0:1].to_broadcast([P, CB]),
                                        ALU.pow).then_inc(rstd_ready, 1)

            def add_residual(c):
                pool.wait_ge(x_done, L * NCH + c + 1)
                nc.gpsimd.tensor_tensor(X[:, CB * c:CB * c + CB, :], X[:, CB * c:CB * c + CB, :],
                                        H[:, CB * c:CB * c + CB, :], ALU.add).then_inc(sum_ready, 1)

            load_source(0, 0)
            load_source(1, 1)
            chain.slot(0)
            if not post:
                rstds(0)

            def slot(i, u):
                k = 2 * i + u
                first = isinstance(k, int) and k == 0
                last = isinstance(k, int) and k >= K - 2
                end = isinstance(k, int) and k >= K - 1
                if post:
                    chain.slot(max(k - 1, 0) if isinstance(k, int) else k - 1)
                    if not first:
                        rstds(k - 1)
                else:
                    chain.slot(k + 1)
                    if not end:
                        rstds(k + 1)
                if not last:
                    load_source(k + 2, u)
                if not post and last:
                    for c in range(0 if not end else NCH - 3, NCH - 3 if not end else NCH - 2):
                        add_residual(c)

            pairs(pool, slot, K)
            if not post:
                for c in range(NCH - 2, NCH):
                    add_residual(c)
            else:
                chain.slot(K - 1)
                rstds(K - 1)

        @block.scalar
        def _(act):
            def head_xT(n, u):
                act.wait_ge(x_transposed, n + 1)
                nc.scalar.activation(xT[:, u, :], psH[:, :], ACT.Copy).then_inc(xT_ready, 1)

            def head_tanh(n):
                act.wait_ge(gap_ready, n + 1)
                nc.scalar.activation(th[:, :], gap[:, :], ACT.Tanh, scale=0.5).then_inc(tanh_ready, 1)

            def head_xhT(n, u):
                act.wait_ge(xh_transposed, n + 1)
                nc.scalar.activation(xhT[:, u, :], psH[:, :], ACT.Copy).then_inc(xhT_ready, 1)

            def gelus(k, e):
                g = k * E + e
                l = k // NCH if L > 1 else 0
                after(act, expert_done, g - 1)
                for f in range(FT):
                    act.wait_ge(r_full, FT * g + f + 1)
                    nc.scalar.activation(h1[:, e % 2, f, :], psR[:, f, :], GELU,
                                         bias=b1[:, bass.ds((l * E + e) * FT + f, 1)]).then_inc(h1_ready, 1)

            act.wait_ge(c_in, 16 * (n_c - 1))
            head_xT(0, 0)
            head_tanh(0)
            if not post:
                head_xhT(0, 0)

            def slot(i, u):
                k = 2 * i + u
                end = isinstance(k, int) and k >= K - 1
                for e in range(E):
                    gelus(k, e)
                    if end:
                        continue
                    if e == AT["x"]:
                        head_xT(k + 1, 1 - u)
                    if e == TANH_AT:
                        head_tanh(k + 1)
                    if e == AT["xh"]:
                        head_xhT(k + 1, 1 - u)
                act.wait_ge(y_full, k + 1)
                nc.scalar.activation(yT[:, :], psY[:, :], ACT.Copy).then_inc(yT_ready, 1)

            pairs(act, slot, K)

        @block.vector
        def _(dve):
            chain = Chain(dve, dve_chain)

            def col(t):
                return t.unsqueeze(2).to_broadcast([P, CB, E])

            def row(t):
                return t.unsqueeze(1).to_broadcast([P, CB, E])

            def head_norm(n, c):
                if post:
                    return
                for j in range(CB):
                    mm = nc.vector.bn_stats(st[:, j, :], H[:, CB * c + j, :])
                chain.link(mm)
                apart(nc, env)
                for j in range(CB):
                    mm = nc.vector.bn_aggr(mv[:, j, :], st[:, j, :])
                mm.then_inc(stats_ready, 1)
                dve.wait_ge(rstd_ready, n + 1)
                after(dve, xh_transposed, n)
                for j in range(CB):
                    mm = nc.vector.tensor_scalar(xh[:, j, :], H[:, CB * c + j, :], mv[:, j, 0:1],
                                                 rstd[:, j:j + 1], ALU.subtract, ALU.mult)
                mm.then_inc(xh_ready, 1)

            def route_pick(n):
                l = n // NCH if L > 1 else 0
                dve.wait_ge(logits_full, n + 1)
                full = psH[:, 0:CB * E].rearrange("t (j e) -> t j e", e=E)
                if post:
                    nc.vector.tensor_copy(lg[:, :, :], full).then_inc(logits_read, 1)
                else:
                    nc.vector.tensor_tensor(lg[:, :, :], full, row(rb[:, bass.ds(l * E, E)]),
                                            ALU.add).then_inc(logits_read, 1)
                dve.wait_ge(logits_read, n + 1)
                link = chain.link
                for src, top, mask in ((lg, m1, k1), (l2, m2, k2)):
                    if src is l2:
                        link(nc.vector.scalar_tensor_tensor(l2[:, :, :], k1[:, :, :], 3.0 * NEG, lg[:, :, :],
                                                            ALU.mult, ALU.add))
                    link(nc.vector.tensor_reduce(top[:, :], src[:, :, :], AX.X, ALU.max))
                    link(nc.vector.tensor_tensor(t1[:, :, :], src[:, :, :], col(top[:, :]), ALU.is_ge))
                    link(nc.vector.tensor_tensor(t1[:, :, :], t1[:, :, :], row(rank[:, :]), ALU.mult))
                    link(nc.vector.tensor_reduce(r1[:, :], t1[:, :, :], AX.X, ALU.max))
                    link(nc.vector.tensor_tensor(mask[:, :, :], t1[:, :, :], col(r1[:, :]), ALU.is_equal))
                nc.vector.tensor_tensor(gap[:, :], m1[:, :], m2[:, :], ALU.subtract).then_inc(gap_ready, 1)

            def route_weigh(n, u):
                dve.wait_ge(tanh_ready, n + 1)
                nc.vector.tensor_scalar(wa[:, :], th[:, :], 0.5, 0.5, ALU.mult, ALU.add)
                chain.link(nc.vector.tensor_scalar(wb[:, :], th[:, :], -0.5, 0.5, ALU.mult, ALU.add))
                nc.vector.tensor_tensor(sw[:, u, :], wa[:, :], wb[:, :], ALU.add)
                nc.vector.tensor_tensor(k1[:, :, :], k1[:, :, :], col(wa[:, :]), ALU.mult)
                chain.link(nc.vector.tensor_tensor(k2[:, :, :], k2[:, :, :], col(wb[:, :]), ALU.mult))
                nc.vector.tensor_tensor(comb[:, :, :], k1[:, :, :], k2[:, :, :], ALU.add).then_inc(comb_ready, 1)

            def head_gT(n, u):
                dve.wait_ge(g_transposed, n + 1)
                nc.vector.tensor_copy(gT[:, u, :], psH[0:E, :]).then_inc(gT_ready, 1)

            def expert_input(k, u, e):
                g = k * E + e
                if post:
                    return
                l = k // NCH
                dve.wait_ge(xhT_ready, k + 1)
                after(dve, r_full, FT * (g - 1))
                nc.vector.tensor_scalar(xe[:, e % 2, :], xhT[:, u, :], lng[:, bass.ds(l * E + e, 1)],
                                        lnb[:, bass.ds(l * E + e, 1)], ALU.mult, ALU.add).then_inc(xe_ready, 1)

            def gate_hidden(k, e):
                g = k * E + e
                dve.wait_ge(g_full, g + 1)
                for f in range(FT):
                    dve.wait_ge(h1_ready, FT * g + f + 1)
                    nc.vector.tensor_tensor(h1[:, e % 2, f, :], h1[:, e % 2, f, :], psG[:, e % 2, :],
                                            ALU.mult).then_inc(hg_ready, 1)

            def finish(k, u, c):
                dve.wait_ge(z_full, k + 1)
                zz = psY[:, :].rearrange("t (j m) -> t j m", m=P)
                if not post:
                    for j in range(CB):
                        mm = nc.vector.scalar_tensor_tensor(H[:, CB * c + j, :], H[:, CB * c + j, :],
                                                            sw[:, u, j:j + 1], zz[:, j, :], ALU.mult, ALU.add)
                    mm.then_inc(x_done, 1)
                    return
                nc.vector.tensor_tensor(z[:, :, :], H[:, bass.ds(CB * c, CB), :], zz, ALU.add).then_inc(z_read, 1)
                dve.wait_ge(z_read, k + 1)
                for j in range(CB):
                    mm = nc.vector.bn_stats(st[:, j, :], z[:, j, :])
                chain.link(mm)
                apart(nc, env)
                for j in range(CB):
                    mm = nc.vector.bn_aggr(mv[:, j, :], st[:, j, :])
                mm.then_inc(stats_ready, 1)
                dve.wait_ge(rstd_ready, k + 1)
                for j in range(CB):
                    mm = nc.vector.tensor_scalar(z[:, j, :], z[:, j, :], mv[:, j, 0:1], rstd[:, j:j + 1],
                                                 ALU.subtract, ALU.mult)
                chain.link(mm)
                for n, op in ((0, ALU.mult), (1, ALU.add)):
                    chain.link(nc.vector.tensor_tensor(z[:, :, :], z[:, :, :],
                                                       gb[:, n, :].unsqueeze(1).to_broadcast([P, CB, P]), op))
                nc.vector.tensor_tensor(X[:, bass.ds(CB * c, CB), :], X[:, bass.ds(CB * c, CB), :], z[:, :, :],
                                        ALU.add).then_inc(x_done, 1)

            dve.wait_ge(c_in, 16 * (n_c - 1))
            chain.slot(0)
            if not post:
                for c in range(NCH):
                    nc.vector.memset(mark[:, c:c + 1], 0.0).then_inc(x_done, 1)
            head_norm(0, 0)
            route_pick(0)
            route_weigh(0, 0)
            head_gT(0, 0)
            SETUP = chain.n
            LINKS = [None, None]

            def slot(i, u):
                k = 2 * i + u
                first = isinstance(k, int) and k == 0
                end = isinstance(k, int) and k >= K - 1
                if first:
                    chain.slot(SETUP)
                else:
                    chain.slot(SETUP + LINKS[0] + (LINKS[1] or 0) * (k - 1))
                expert_input(k, u, 0)
                for e in range(E):
                    if e + 1 < E:
                        expert_input(k, u, e + 1)
                    gate_hidden(k, e)
                    if e == 0 and not first:
                        finish(k - 1, 1 - u, (k - 1) % NCH)
                    if end:
                        continue
                    if e == AT["x"]:
                        head_norm(k + 1, (k + 1) % NCH)
                    if e == AT["logits"]:
                        route_pick(k + 1)
                    if e == TANH_AT:
                        route_weigh(k + 1, 1 - u)
                    if e == AT["gates"]:
                        head_gT(k + 1, 1 - u)
                if first:
                    LINKS[0] = chain.n
                elif LINKS[1] is None:
                    LINKS[1] = chain.n

            pairs(dve, slot, K)
            finish(K - 1, (K - 1) % 2, (K - 1) % NCH)

        @block.tensor
        def _(pe):
            def head_x(n, h, u):
                pe.wait_ge(xs_in[u], 16 * (h + 1))
                after(pe, gT_ready, n)
                for j in range(CB):
                    mm = nc.tensor.transpose(psH[:, P * j:P * j + P], xs[:, u, j, :], ident[:, :])
                mm.then_inc(x_transposed, 1)

            def head_logits(n, u):
                l = n // NCH if L > 1 else 0
                pe.wait_ge(xT_ready, n + 1)
                for j in range(CB):
                    mm = nc.tensor.matmul(psH[:, E * j:E * j + E], xT[:, u, P * j:P * j + P],
                                          rw[:, bass.ds(l * E, E)], start=True, stop=True)
                mm.then_inc(logits_full, 1)

            def head_xh(n):
                pe.wait_ge(xh_ready, n + 1)
                pe.wait_ge(logits_read, n + 1)
                for j in range(CB):
                    mm = nc.tensor.transpose(psH[:, P * j:P * j + P], xh[:, j, :], ident[:, :])
                mm.then_inc(xh_transposed, 1)

            def head_gates(n):
                pe.wait_ge(comb_ready, n + 1)
                if not post:
                    pe.wait_ge(xhT_ready, n + 1)
                for j in range(CB):
                    mm = nc.tensor.transpose(psH[0:E, P * j:P * j + P], comb[:, j, :], ident[:, :])
                mm.then_inc(g_transposed, 1)

            def gates(k, u, e):
                g = k * E + e
                pe.wait_ge(gT_ready, k + 1)
                after(pe, hg_ready, FT * (g - 1))
                nc.tensor.matmul(psG[:, e % 2, :], sel[:, e, :], gT[:, u, :], start=True,
                                 stop=True).then_inc(g_full, 1)

            def hidden(k, u, e):
                g = k * E + e
                l = k // NCH if L > 1 else 0
                pe.wait_ge(w_in[e], 32 * (l + 1))
                pe.wait_ge(xT_ready, k + 1) if post else pe.wait_ge(xe_ready, g + 1)
                for f in range(FT):
                    after(pe, h1_ready, FT * (g - 1) + f + 1)
                    rhs = xT[:, u, :] if post else xe[:, e % 2, :]
                    nc.tensor.matmul(psR[:, f, :], w1[:, e, P * f:P * f + P], rhs, start=True,
                                     stop=True).then_inc(r_full, 1)

            def outputs(k, u, e):
                g = k * E + e
                if e == 0:
                    after(pe, z_read, k) if post else pe.wait_ge(x_done, k + NCH)
                for f in range(FT):
                    pe.wait_ge(hg_ready, FT * g + f + 1)
                    mm = nc.tensor.matmul(psY[:, :], w2[:, e, f, :], h1[:, e % 2, f, :],
                                          start=(e == 0 and f == 0), stop=False)
                mm.then_inc(expert_done, 1)
                if e == E - 1:
                    l = k // NCH if L > 1 else 0
                    pe.wait_ge(b2_in, 16 * (l + 1))
                    nc.tensor.matmul(psY[:, :], b2[:, :], gT[:, u, :], start=False, stop=True).then_inc(y_full, 1)

            def back(k):
                pe.wait_ge(yT_ready, k + 1)
                for j in range(CB):
                    mm = nc.tensor.transpose(psY[:, P * j:P * j + P], yT[:, P * j:P * j + P], ident[:, :])
                mm.then_inc(z_full, 1)

            pe.wait_ge(c_in, 16 * (n_c - 1))
            head_x(0, 0, 0)
            head_logits(0, 0)
            if not post:
                head_xh(0)
            head_gates(0)

            def slot(i, u):
                k = 2 * i + u
                first = isinstance(k, int) and k == 0
                end = isinstance(k, int) and k >= K - 1
                for e in range(E):
                    gates(k, u, e)
                    hidden(k, u, e)
                    if e == 0 and not first:
                        back(k - 1)
                    if e >= 1:
                        outputs(k, u, e - 1)
                    if end:
                        continue
                    if e == AT["x"]:
                        head_x(k + 1, i + u, 1 - u)
                    if e == AT["logits"]:
                        head_logits(k + 1, 1 - u)
                    if e == AT["xh"]:
                        head_xh(k + 1)
                    if e == AT["gates"]:
                        head_gates(k + 1)
                outputs(k, u, E - 1)

            pairs(pe, slot, K)
            back(K - 1)

        stage.close()
        clear(nc, sems)


def build(nc, a, NB, S):
    with ExitStack() as ctx:
        env = Env()
        env.NB = NB
        env.X = ctx.enter_context(nc.sbuf_tensor("X", [P, NB, P], F32))
        env.H = ctx.enter_context(nc.sbuf_tensor("H", [P, NB, P], F32))
        env.ident = ctx.enter_context(nc.sbuf_tensor("ident", [P, P], F32))
        env.identb = ctx.enter_context(nc.sbuf_tensor("identb", [P, P], BF16))
        env.scratch = ctx.enter_context(nc.sbuf_tensor("scratch", [P, 1], F32))
        env.eps = ctx.enter_context(nc.sbuf_tensor("eps", [P, 1], F32))
        env.minus_half = ctx.enter_context(nc.sbuf_tensor("minus_half", [P, 1], F32))
        const_in = ctx.enter_context(nc.semaphore("const_in"))
        with nc.Block() as block:
            @block.sync
            def _(sp):
                sp.dma_start(env.ident[:, :], a["c_ident"]).then_inc(const_in, 16)
                sp.dma_start(env.identb[:, :], a["c_identb"]).then_inc(const_in, 16)
                sp.dma_start(env.minus_half[:, :], a["c_minus_half"]).then_inc(const_in, 16)
                sp.dma_start(env.eps[:, :], a["c_eps"]).then_inc(const_in, 16)
                sp.wait_ge(const_in, 64)

        wide = dict(mask_j=a["c_mask_j32"], mask_m=a["c_mask_m32"], sel_q=a["c_sel_q32"])
        narrow = dict(mask_j=a["c_mask_j16"], mask_m=a["c_mask_m16"])
        attention(nc, env, "xa0", NB, S, 2 * HEADS, False, True, False, dict(
            wide, x=a["x"], ctx=a["ctx"], w=a["xa0_w"], qkb=a["xa0_qkb"], rows=a["xa0_rows"],
            lam=[a[f"lam{n}"] for n in range(4)]))
        attention(nc, env, "sa", NB, P, HEADS, True, False, True, dict(
            narrow, sel_q=a["c_sel_q16s"], w=a["sa_w"], qkb=a["sa_qkb"], rows=a["sa_rows"], cm=a["c_cm"],
            gb=a["sa_gb"]))
        mixture(nc, env, "m0", a["m0_b2"].shape[1], 1, dict(
            {n: a[f"m0_{n}"] for n in ("w1", "w2", "b1", "b2", "rw", "gb")}, rank=a["c_rank8"], sel=a["c_sel8"]))
        attention(nc, env, "xa1", NB, S, HEADS, False, False, True, dict(
            narrow, sel_q=a["c_sel_q16"], ctx=a["ctx"], w=a["xa1_w"], qkb=a["xa1_qkb"], rows=a["xa1_rows"]))
        mixture(nc, env, "m1", a["m1_b2"].shape[1], a["m1_b2"].shape[0], dict(
            {n: a[f"m1_{n}"] for n in ("w1", "w2", "b1", "b2", "rw", "lng", "lnb", "rb")},
            rank=a["c_rank4"], sel=a["c_sel4"], out=a["out"]))


def constants(NP, S):
    bf = mybir.dt.np(BF16)
    r = NP.arange
    c = {"ident": NP.eye(P, dtype="float32"), "identb": NP.eye(P).astype(bf),
         "eps": NP.full((P, 1), EPS, "float32"), "minus_half": NP.full((P, 1), -0.5, "float32")}
    for ns in (32, 16):
        J = ns // 4
        c[f"mask_j{ns}"] = ((r(P)[:, None] % QUAD) // (P // ns) == r(J)[None]).astype("float32")
        rr = r(2 * QUAD)[:, None] % QUAD
        c[f"mask_m{ns}"] = (rr % J == r(J)[None]).astype("float32")
        q = ((rr // J == r(4)[None]) & (rr < ns))[:, :, None]
        c[f"sel_q{ns}"] = NP.ascontiguousarray(NP.broadcast_to(q, (2 * QUAD, 4, S))).astype(bf)
        if ns == 16:
            c["sel_q16s"] = NP.ascontiguousarray(NP.broadcast_to(q, (2 * QUAD, 4, P))).astype(bf)
    future = (r(P)[None, :] > r(P)[:, None])
    m = NP.stack([future, future.T], 1)[:, :, None, :] * NEG
    c["cm"] = NP.ascontiguousarray(NP.broadcast_to(m, (P, 2, 4, P))).astype(bf)
    for e in (8, 4):
        c[f"rank{e}"] = NP.broadcast_to((e - r(e))[None], (P, e)).astype("float32")
        c[f"sel{e}"] = NP.ascontiguousarray(NP.broadcast_to(NP.eye(e)[:, :, None], (e, e, P))).astype("float32")
    return c


def kernel(**inputs):
    import numpy as np
    import concourse.bacc as _bacc
    from concourse import mybir as _mybir
    from concourse.bass_utils import run_bass_kernel_spmd as _run

    i = {n: np.asarray(v) for n, v in inputs.items()}
    NB, T, D = i["x"].shape
    S = i["ctx_1024"].shape[1]
    L, E4, _, F = i["L1_ffn_w1"].shape
    E8 = i["L0_ffn_wg"].shape[1]
    zero = np.zeros(D, "float32")
    one = np.ones(D, "float32")
    wi, bi = i["L0_xattn_in_proj_weight"], i["L0_xattn_in_proj_bias"]
    wq = i["L0_ffn_w_qkv"]
    arr = {
        "x": i["x"], "ctx": i["ctx_1024"],
        "xa0_w": np.stack([wi[:D].T, wi[D:2 * D].T, wi[2 * D:].T, i["L0_xattn_out_proj_weight"].T], 1),
        "xa0_qkb": np.stack([bi[:D], bi[D:2 * D]], 1),
        "xa0_rows": np.stack([bi[2 * D:], i["L0_xattn_out_proj_bias"], one])[None],
        "lam0": i["L0_xattn_lambda_q1"], "lam1": i["L0_xattn_lambda_k1"],
        "lam2": i["L0_xattn_lambda_q2"], "lam3": i["L0_xattn_lambda_k2"],
        "sa_w": np.stack([wq[:, :D], wq[:, D:2 * D], wq[:, 2 * D:], i["L0_ffn_w_o"]], 1),
        "sa_qkb": np.stack([zero, zero], 1), "sa_rows": np.stack([zero, zero, one])[None],
        "sa_gb": np.stack([i["L0_ffn_g1"], i["L0_ffn_b1"]]),
        "m0_w1": i["L0_ffn_w1"], "m0_w2": i["L0_ffn_w2"], "m0_b2": i["L0_ffn_bb2"][None],
        "m0_b1": i["L0_ffn_bb1"].reshape(E8 * F // P, P).T, "m0_rw": i["L0_ffn_wg"],
        "m0_gb": np.stack([i["L0_ffn_g2"], i["L0_ffn_b2"]]),
        "xa1_w": np.stack([i["L1_xattn_Wq"], i["L1_xattn_Wk"], i["L1_xattn_Wv"], i["L1_xattn_Wo"]], 1),
        "xa1_qkb": np.stack([i["L1_xattn_bq"], i["L1_xattn_bk"]], 1),
        "xa1_rows": np.stack([i["L1_xattn_bv"], i["L1_xattn_bo"], one])[None],
        "m1_w1": i["L1_ffn_w1"].reshape(L * E4, D, F), "m1_w2": i["L1_ffn_w2"].reshape(L * E4, F, D),
        "m1_b2": i["L1_ffn_b2"], "m1_b1": i["L1_ffn_b1"].reshape(L * E4 * F // P, P).T,
        "m1_rw": i["L1_ffn_router_w"].transpose(1, 0, 2).reshape(D, L * E4),
        "m1_lng": i["L1_ffn_ln_g"].reshape(L * E4, D).T, "m1_lnb": i["L1_ffn_ln_b"].reshape(L * E4, D).T,
        "m1_rb": i["L1_ffn_router_b"].reshape(L * E4),
    }
    arr.update({f"c_{n}": v for n, v in constants(np, S).items()})
    arr = {n: np.ascontiguousarray(v) for n, v in arr.items()}

    nc = _bacc.Bacc("TRN2", target_bir_lowering=False, num_devices=1)
    aps = {n: nc.dram_tensor(f"in_{n}", v.shape, _mybir.dt.from_np(v.dtype), kind="ExternalInput").ap()
           for n, v in arr.items()}
    aps["out"] = nc.dram_tensor("out_x", (NB, T, D), F32, kind="ExternalOutput").ap()
    build(nc, aps, NB, S)
    r = _run(nc, [{f"in_{n}": v for n, v in arr.items()}], core_ids=[0])
    return r.results[0]["out_x"]
```

```python
from contextlib import ExitStack

import concourse.bass as bass
from concourse import mybir

F32 = mybir.dt.float32
BF16 = mybir.dt.bfloat16
ALU = mybir.AluOpType
ACT = mybir.ActivationFunctionType
AX = mybir.AxisListType

P = 128
HEADS = 16
HD = P // HEADS
QUAD = 32
BANK = 512
EPS = 1e-5
LAMBDA_INIT = 0.2
CB = 4
CT = CB * P
NEG = -1.0e30


def after(eng, sem, value):
    if not isinstance(value, int) or value > 0:
        eng.wait_ge(sem, value)


def pairs(eng, slot, n):
    slot(0, 0)
    slot(0, 1)
    with eng.Fori(1, n // 2 - 1) as i:
        slot(i, 0)
        slot(i, 1)
    slot(n // 2 - 1, 0)
    slot(n // 2 - 1, 1)


def apart(nc, env):
    nc.vector.memset(env.scratch[:, :], 0.0)


class Chain:

    def __init__(self, eng, sem):
        self.eng, self.sem, self.base, self.n = eng, sem, 0, 0

    def slot(self, base):
        self.base, self.n = base, 0

    def link(self, ins):
        self.n += 1
        ins.then_inc(self.sem, 1)
        self.eng.wait_ge(self.sem, self.base + self.n)


def clear(nc, sems):
    with nc.Block() as block:
        @block.sync
        def _(sp):
            for s in sems:
                sp.sem_clear(s)


class Env:
    pass


def attention(nc, env, tag, NB, S, NS, causal, diff, norm, d):
    G = NS // 4
    R = 8 // G
    NX = G * R
    NT = NX // (4 * R)
    SCALE = 1.0 / float(P // NS) ** 0.5
    X, H, ident, identb = env.X, env.H, env.ident, env.identb
    KR = 96
    VW = QUAD
    kv = P if not causal else 0
    WS = S + P if not causal else P
    use = d["use"]

    with ExitStack() as ctx:
        def sb(name, shape, dt=F32):
            return ctx.enter_context(nc.sbuf_tensor(f"{tag}_{name}", shape, dt))

        def ps(name, shape):
            return ctx.enter_context(nc.psum_tensor(f"{tag}_{name}", shape, F32))

        sems = []

        def sem(name):
            sems.append(ctx.enter_context(nc.semaphore(f"{tag}_{name}")))
            return sems[-1]

        wT = sb("wT", [P, 4, P])
        qkb = sb("qkb", [P, 2])
        qbs = sb("qbs", [P, 1])
        rows = sb("rows", [1, 3, P])
        mask = sb("mask", [P, 4])
        n_sel = sum(len(part) for sides in use for part in sides)
        sel = sb("sel", [P, n_sel, KR], BF16)
        xn = sb("xn", [P, 2, P])
        stats = sb("stats", [P, 6])
        mv = sb("mv", [P, 2, 2])
        veps = sb("veps", [P, 1])
        rstd = sb("rstd", [P, 2])
        cx = sb("cx", [P, 2, P])
        srcT = sb("srcT", [P, 2, WS])
        QK = sb("QK", [P, S + P])
        rest = sb("rest", [P, S + P])
        parts = sb("parts", [P, 2, 3, S + P], BF16)
        Va = sb("Va", [P, 2, HEADS, VW])
        Kr = sb("Kr", [P, 2, NX, S], BF16)
        Qr = sb("Qr", [P, NX, P], BF16)
        Km = sb("Km", [P, NX, 4, S], BF16)
        Qm = sb("Qm", [P, NX, 4, P], BF16)
        M = sb("M", [P, NS])
        Mr = sb("Mr", [P, NS])
        nM = sb("nM", [P, G, QUAD], BF16)
        E = sb("E", [P, 4, 4 * P])
        OTs = sb("OTs", [P, NS * QUAD])
        rec = sb("rec", [P, NS])
        pv = sb("pv", [P, NS, HD])
        att = sb("att", [P, P])
        attT = sb("attT", [P, P])
        if causal:
            cm = sb("cm", [P, 2, 4, P], BF16)
            z = sb("z", [P, P])
            gb = sb("gb", [P, 2, P])
        if norm:
            stats2 = sb("stats2", [P, 6])
            mv2 = sb("mv2", [P, 2])
            veps2 = sb("veps2", [P, 1])
            rstd2 = sb("rstd2", [P, 1])
        if diff:
            lq = sb("lq", [P, 4, P // NS])
            lp = sb("lp", [P, 2, P // NS])
            ld = sb("ld", [P, 2])
            le = sb("le", [P, 2])
            nlam = sb("nlam", [P, 1])

        psA = ps("psA", [P, 2, BANK])
        psB = ps("psB", [P, 2, BANK])
        psX = ps("psX", [P, BANK])
        psH = ps("psH", [P, BANK])
        psO = ps("psO", [P, 2 * BANK])

        w_in = sem("w_in")
        x_first = sem("x_first")
        x_rest = sem("x_rest")
        ctx_in = [sem("ctx_in0"), sem("ctx_in1")]
        setup_done = sem("setup_done")
        lam_dots = sem("lam_dots")
        lam_exp = sem("lam_exp")
        stats_ready = sem("stats_ready")
        rstd_ready = sem("rstd_ready")
        xn_ready = sem("xn_ready")
        xn_kept = sem("xn_kept")
        src_transposed = sem("src_transposed")
        srcT_ready = sem("srcT_ready")
        qk_projected = sem("qk_projected")
        qk_ready = sem("qk_ready")
        parts_ready = sem("parts_ready")
        v_projected = sem("v_projected")
        v_ready = sem("v_ready")
        rows_full = sem("rows_full")
        rows_ready = sem("rows_ready")
        km_ready = sem("km_ready")
        a_full = sem("a_full")
        a_free = sem("a_free")
        nm_ready = sem("nm_ready")
        m_transposed = sem("m_transposed")
        m_rows_ready = sem("m_rows_ready")
        qm_ready = sem("qm_ready")
        b_full = sem("b_full")
        e_ready = sem("e_ready")
        pv_done = sem("pv_done")
        ot_ready = sem("ot_ready")
        back_done = sem("back_done")
        att_ready = sem("att_ready")
        att_transposed = sem("att_transposed")
        attT_ready = sem("attT_ready")
        y_ready = sem("y_ready")
        x_done = sem("x_done")
        stats2_ready = sem("stats2_ready")
        rstd2_ready = sem("rstd2_ready")
        dve_chain = sem("dve_chain")
        pool_chain = sem("pool_chain")

        n_w = 5 + (2 if causal else 0) + (4 if diff else 0)
        if G == 8:
            BEFORE = [["rows0"], ["source"], ["rows1"], ["qk"], ["rows2", "max0"], ["max1"],
                      ["rows3", "max2"], ["v", "max3"]]
        else:
            BEFORE = [["rows0", "source"], ["rows1"], ["rows2", "qk"], ["rows3", "max0", "v"]]
        REST = [f"max{g}" for g in range(4 if G == 8 else 1, G)]
        BACK = len(REST) // 2

        stage = ExitStack()
        block = stage.enter_context(nc.Block())

        @block.sync
        def _(sp):
            if diff:
                sp.dma_start(X[:, 0:4, :], d["x"][0:4].rearrange("b t c -> t b c")).then_inc(x_first, 16)
            sp.dma_start(wT[:, :, :], d["w"]).then_inc(w_in, 16)
            sp.dma_start(qkb[:, :], d["qkb"]).then_inc(w_in, 16)
            sp.dma_start(rows[:, :, :], d["rows"]).then_inc(w_in, 16)
            sp.dma_start(mask[:, :], d["mask"]).then_inc(w_in, 16)
            sp.dma_start(sel[:, :, :], d["sel"]).then_inc(w_in, 16)
            if causal:
                sp.dma_start(cm[:, :, :, :], d["cm"]).then_inc(w_in, 16)
                sp.dma_start(gb[:, :, :], d["gb"].partition_broadcast(P)).then_inc(w_in, 16)
            if diff:
                for n in range(4):
                    sp.dma_start(lq[:, n, :], d["lam"][n].partition_broadcast(P)).then_inc(w_in, 16)
                sp.dma_start(X[:, 4:NB, :], d["x"][4:NB].rearrange("b t c -> t b c")).then_inc(x_rest, 16)

            def slot(i, u):
                n = 2 * i + u
                after(sp, src_transposed, n - 1)
                sp.dma_start(cx[0:S, u, :], d["ctx"][n]).then_inc(ctx_in[u], 16)

            if not causal:
                pairs(sp, slot, NB)

        @block.gpsimd
        def _(pool):
            chain = Chain(pool, pool_chain)
            HEAD, TAIL = 3, 1 if norm else 0

            def head_rstd(n, u):
                pool.wait_ge(stats_ready, n + 1)
                chain.link(nc.gpsimd.tensor_tensor(veps[:, :], mv[:, u, 1:2], env.eps[:, :], ALU.add))
                nc.gpsimd.tensor_tensor(rstd[:, u:u + 1], veps[:, :], env.minus_half[:, :],
                                        ALU.pow).then_inc(rstd_ready, 1)

            def keep(n, u):
                pool.wait_ge(xn_ready, n + 1)
                nc.gpsimd.tensor_tensor(H[:, n, :], xn[:, u, :], env.zero[:, 0:1].to_broadcast([P, P]),
                                        ALU.add).then_inc(xn_kept, 1)

            def split(n, u):
                pool.wait_ge(qk_ready, n + 1)
                chain.link(nc.gpsimd.tensor_tensor(parts[:, u, 0, :], QK[:, :], env.zero[:, 0:1].to_broadcast([P, S + P]),
                                                  ALU.add))
                chain.link(nc.gpsimd.tensor_tensor(rest[:, :], QK[:, :], parts[:, u, 0, :], ALU.subtract))
                nc.gpsimd.tensor_tensor(parts[:, u, 1, :], rest[:, :], env.zero[:, 0:1].to_broadcast([P, S + P]),
                                        ALU.add).then_inc(parts_ready, 1)
                pool.wait_ge(parts_ready, 2 * n + 1)
                nc.gpsimd.tensor_tensor(parts[:, u, 2, :], rest[:, :], parts[:, u, 1, :],
                                        ALU.subtract).then_inc(parts_ready, 1)

            def tail_rstd(b):
                pool.wait_ge(stats2_ready, b + 1)
                chain.link(nc.gpsimd.tensor_tensor(veps2[:, :], mv2[:, 1:2], env.eps[:, :], ALU.add))
                nc.gpsimd.tensor_tensor(rstd2[:, :], veps2[:, :], env.minus_half[:, :],
                                        ALU.pow).then_inc(rstd2_ready, 1)

            pool.wait_ge(w_in, 16 * n_w)
            chain.slot(0)
            for n in range(2):
                head_rstd(n, n)
                if causal:
                    keep(n, n)
                split(n, n)

            def slot(i, u):
                b = 2 * i + u
                last = isinstance(b, int) and b >= NB - 2
                end = isinstance(b, int) and b >= NB - 1
                chain.slot(HEAD * 2 + b * (HEAD + TAIL) if not end
                           else HEAD * NB + (NB - 1) * TAIL)
                if not last:
                    head_rstd(b + 2, u)
                    if causal:
                        keep(b + 2, u)
                    split(b + 2, u)
                if norm:
                    tail_rstd(b)

            pairs(pool, slot, NB)

        @block.scalar
        def _(act):
            def head_src(n, u):
                act.wait_ge(src_transposed, n + 1)
                nc.scalar.activation(srcT[:, u, :], psH[:, 0:WS], ACT.Copy).then_inc(srcT_ready, 1)

            def head_qk(n):
                act.wait_ge(qk_projected, n + 1)
                after(act, parts_ready, 2 * n)
                nc.scalar.activation(QK[:, 0:S], psH[:, P:P + S], ACT.Identity, bias=qkb[:, 1:2])
                nc.scalar.activation(QK[:, S:S + P], psH[:, 0:P], ACT.Identity, bias=qbs[:, 0:1],
                                     scale=SCALE).then_inc(qk_ready, 1)

            def head_v(n, u):
                act.wait_ge(v_projected, n + 1)
                nc.scalar.activation(Va[0:S, u, :, 0:HD], psH[0:S, 0:P].rearrange("s (h e) -> s h e", e=HD),
                                     ACT.Copy).then_inc(v_ready, 1)

            def head_rows(n, u, y):
                act.wait_ge(rows_full, 4 * n + y + 1)
                if y == 0:
                    after(act, qm_ready, n)
                nc.scalar.activation(Kr[0:KR, u, 2 * y:2 * y + 2, :],
                                     psX[0:KR, 0:2 * S].rearrange("r (x s) -> r x s", x=2), ACT.Copy)
                nc.scalar.activation(Qr[0:KR, 2 * y:2 * y + 2, :],
                                     psX[0:KR, 2 * S:2 * S + 2 * P].rearrange("r (x t) -> r x t", x=2),
                                     ACT.Copy).then_inc(rows_ready, 1)

            def head_m(n):
                for k in range(NT):
                    act.wait_ge(m_transposed, NT * n + k + 1)
                    nc.scalar.activation(Qr[KR:P, 4 * k * R:4 * (k + 1) * R:R, :],
                                         psH[KR:P, :].rearrange("r (g t) -> r g t", g=4),
                                         ACT.Copy).then_inc(m_rows_ready, 1)

            def exps(b, g):
                n = b * G + g
                act.wait_ge(b_full, n + 1)
                after(act, pv_done, n - 3)
                nc.scalar.activation(E[0:S, g % 4, :], psB[0:S, g % 2, :], ACT.Exp).then_inc(e_ready, 1)

            def tail_OT(b):
                act.wait_ge(pv_done, (b + 1) * G)
                nc.scalar.activation(OTs[:, :], psO[:, 0:NS * QUAD], ACT.Copy).then_inc(ot_ready, 1)

            def step(name, b, u, last, end):
                if name == "source" and not last:
                    head_src(b + 2, u)
                if name == "qk" and not last:
                    head_qk(b + 2)
                if name == "v" and not end:
                    head_v(b + 1, 1 - u)
                if name[:4] == "rows" and not end:
                    head_rows(b + 1, 1 - u, int(name[4:]))

            if diff:
                act.wait_ge(lam_dots, 1)
                nc.scalar.activation(le[:, :], ld[:, :], ACT.Exp).then_inc(lam_exp, 1)
            act.wait_ge(setup_done, 1)
            for n in range(2):
                head_src(n, n)
                head_qk(n)
            for y in range(4):
                head_rows(0, 0, y)
            head_v(0, 0)
            head_m(0)

            def slot(i, u):
                b = 2 * i + u
                last = isinstance(b, int) and b >= NB - 2
                end = isinstance(b, int) and b >= NB - 1
                for g in range(G):
                    for name in BEFORE[g]:
                        step(name, b, u, last, end)
                    exps(b, g)
                tail_OT(b)
                if not end:
                    head_m(b + 1)

            pairs(act, slot, NB)

        @block.vector
        def _(dve):
            chain = Chain(dve, dve_chain)

            def head_norm(n, u):
                chain.link(nc.vector.bn_stats(stats[:, :], X[:, n, :]))
                apart(nc, env)
                nc.vector.bn_aggr(mv[:, u, :], stats[:, :]).then_inc(stats_ready, 1)
                dve.wait_ge(rstd_ready, n + 1)
                after(dve, src_transposed, n - 1)
                if causal:
                    after(dve, xn_kept, n - 1)
                nc.vector.tensor_scalar(xn[:, u, :], X[:, n, :], mv[:, u, 0:1], rstd[:, u:u + 1],
                                        ALU.subtract, ALU.mult).then_inc(xn_ready, 1)

            def head_km(n, u, half):
                dve.wait_ge(rows_ready, 4 * n + 2 * half + 2)
                x = 4 * half
                for j in range(4):
                    mm = nc.vector.tensor_scalar(Km[0:KR, x:x + 4, j, :], Kr[0:KR, u, x:x + 4, :],
                                                 mask[0:KR, j:j + 1], None, ALU.mult)
                mm.then_inc(km_ready, 1)

            def head_max(n, g):
                dve.wait_ge(a_full, n * G + g + 1)
                nc.vector.tensor_reduce(M[:, 4 * g:4 * g + 4],
                                        psA[:, g % 2, 0:4 * S].rearrange("t (j s) -> t j s", j=4),
                                        AX.X, ALU.max).then_inc(a_free, 1)

            def head_nm(n):
                dve.wait_ge(a_free, (n + 1) * G)
                m4 = M[:, :].rearrange("t (g j) -> t g j", j=4)
                r4 = Mr[:, :].rearrange("t (g j) -> t g j", j=4)
                chain.link(nc.vector.tensor_scalar(nM[:, :, 0:4], m4, -1.0, None, ALU.mult))
                chain.link(nc.vector.scalar_tensor_tensor(r4, m4, -1.0, nM[:, :, 0:4], ALU.mult, ALU.subtract))
                chain.link(nc.vector.tensor_copy(nM[:, :, 4:8], r4))
                nc.vector.tensor_tensor(nM[:, :, 8:12], r4, nM[:, :, 4:8], ALU.subtract).then_inc(nm_ready, 1)

            def head_qm(n):
                dve.wait_ge(m_rows_ready, NT * (n + 1))
                for j in range(4):
                    mm = nc.vector.tensor_scalar(Qm[:, :, j, :], Qr[:, :, :], mask[:, j:j + 1], None, ALU.mult)
                mm.then_inc(qm_ready, 1)

            def tail_att(b):
                dve.wait_ge(back_done, b + 1)
                O = psO[:, 0:NS * QUAD].rearrange("t (n e) -> t n e", e=QUAD)
                chain.link(nc.vector.reciprocal(rec[:, :], O[:, :, HD]))
                to = pv[:, :, :] if diff else att[:, :].rearrange("t (n e) -> t n e", e=HD)
                ins = nc.vector.tensor_tensor(to, O[:, :, 0:HD],
                                              rec[:, :].unsqueeze(2).to_broadcast([P, NS, HD]), ALU.mult)
                if diff:
                    chain.link(ins)
                    two = pv[:, :, :].rearrange("t (q k j) e -> t q k (j e)", q=4, k=2)
                    ins = nc.vector.scalar_tensor_tensor(att[:, :].rearrange("t (q m) -> t q m", q=4),
                                                         two[:, :, 1, :], nlam[:, 0:1], two[:, :, 0, :],
                                                         ALU.mult, ALU.add)
                ins.then_inc(att_ready, 1)

            def tail_attT(b):
                dve.wait_ge(att_transposed, b + 1)
                nc.vector.tensor_scalar(attT[:, :], psO[:, 0:P], (1.0 - LAMBDA_INIT) if diff else 1.0,
                                        None, ALU.mult).then_inc(attT_ready, 1)

            def tail_out(b):
                dve.wait_ge(y_ready, b + 1)
                y = psO[:, P:2 * P]
                if not causal:
                    nc.vector.tensor_tensor(X[:, b, :], X[:, b, :], y, ALU.add).then_inc(x_done, 1)
                    if not norm:
                        return
                    dve.wait_ge(x_done, b + 1)
                    apart(nc, env)
                    chain.link(nc.vector.bn_stats(stats2[:, :], X[:, b, :]))
                    apart(nc, env)
                    nc.vector.bn_aggr(mv2[:, :], stats2[:, :]).then_inc(stats2_ready, 1)
                    dve.wait_ge(rstd2_ready, b + 1)
                    chain.link(nc.vector.tensor_scalar(H[:, b, :], X[:, b, :], mv2[:, 0:1], rstd2[:, 0:1],
                                                       ALU.subtract, ALU.mult))
                    return
                dve.wait_ge(xn_kept, b + 1)
                nc.vector.tensor_tensor(z[:, :], H[:, b, :], y, ALU.add).then_inc(x_done, 1)
                dve.wait_ge(x_done, b + 1)
                chain.link(nc.vector.bn_stats(stats2[:, :], z[:, :]))
                apart(nc, env)
                nc.vector.bn_aggr(mv2[:, :], stats2[:, :]).then_inc(stats2_ready, 1)
                dve.wait_ge(rstd2_ready, b + 1)
                chain.link(nc.vector.tensor_scalar(z[:, :], z[:, :], mv2[:, 0:1], rstd2[:, 0:1],
                                                   ALU.subtract, ALU.mult))
                chain.link(nc.vector.tensor_tensor(z[:, :], z[:, :], gb[:, 0, :], ALU.mult))
                chain.link(nc.vector.tensor_tensor(H[:, b, :], z[:, :], gb[:, 1, :], ALU.add))

            dve.wait_ge(w_in, 16 * n_w)
            chain.slot(0)
            nc.vector.memset(Kr[KR:P, :, :, :], 1.0)
            nc.vector.memset(Qr[KR:P, :, :], 0.0)
            nc.vector.memset(nM[:, :, :], 0.0)
            chain.link(nc.vector.memset(Va[:, :, :, :], 0.0))
            chain.link(nc.vector.memset(Va[:, :, :, HD:HD + 1], 1.0))
            if diff:
                for n in range(2):
                    chain.link(nc.vector.tensor_tensor(lp[:, n, :], lq[:, 2 * n, :], lq[:, 2 * n + 1, :], ALU.mult))
                nc.vector.tensor_reduce(ld[:, :], lp[:, :, :], AX.X, ALU.add).then_inc(lam_dots, 1)
                dve.wait_ge(lam_exp, 1)
                chain.link(nc.vector.tensor_tensor(nlam[:, :], le[:, 1:2], le[:, 0:1], ALU.subtract))
                chain.link(nc.vector.tensor_scalar(nlam[:, :], nlam[:, :], -LAMBDA_INIT, None, ALU.add))
            nc.vector.tensor_scalar(qbs[:, :], qkb[:, 0:1], SCALE, None, ALU.mult).then_inc(setup_done, 1)
            if diff:
                dve.wait_ge(x_first, 16)
            for n in range(2):
                head_norm(n, n)
            head_km(0, 0, 0)
            head_km(0, 0, 1)
            for g in range(G):
                head_max(0, g)
            head_nm(0)
            head_qm(0)
            SETUP = chain.n
            LINKS = [None]

            def step(name, b, u, end):
                if end:
                    return
                if name == "rows1":
                    head_km(b + 1, 1 - u, 0)
                if name == "rows3":
                    head_km(b + 1, 1 - u, 1)
                if name[:3] == "max":
                    head_max(b + 1, int(name[3:]))

            def slot(i, u):
                b = 2 * i + u
                last = isinstance(b, int) and b >= NB - 2
                end = isinstance(b, int) and b >= NB - 1
                per = LINKS[0] or 0
                chain.slot(SETUP + b * per if not end else SETUP + (NB - 2) * per + per - 1)
                if diff and isinstance(b, int) and b == 0:
                    dve.wait_ge(x_rest, 16)
                if not last:
                    head_norm(b + 2, u)
                for g in range(G):
                    for name in BEFORE[g]:
                        step(name, b, u, end)
                for k, name in enumerate(REST):
                    if k == BACK + 1:
                        tail_att(b)
                    step(name, b, u, end)
                if BACK + 1 >= len(REST):
                    tail_att(b)
                if not end:
                    head_nm(b + 1)
                tail_attT(b)
                tail_out(b)
                if not end:
                    head_qm(b + 1)
                if LINKS[0] is None:
                    LINKS[0] = chain.n

            pairs(dve, slot, NB)

        @block.tensor
        def _(pe):
            def head_source(n, h, u):
                pe.wait_ge(xn_ready, n + 1)
                after(pe, m_rows_ready, NT * (n - 1))
                after(pe, qk_ready, n)
                mm = nc.tensor.transpose(psH[:, 0:P], xn[:, u, :], ident[:, :])
                if not causal:
                    pe.wait_ge(ctx_in[u], 16 * (h + 1))
                    mm = nc.tensor.transpose(psH[:, P:P + S], cx[0:S, u, :], ident[0:S, 0:S])
                mm.then_inc(src_transposed, 1)

            def head_qk(n, u):
                pe.wait_ge(srcT_ready, n + 1)
                nc.tensor.matmul(psH[:, 0:P], wT[:, 0, :], srcT[:, u, 0:P], start=True, stop=True)
                nc.tensor.matmul(psH[:, P:P + S], wT[:, 1, :], srcT[:, u, kv:kv + S], start=True,
                                 stop=True).then_inc(qk_projected, 1)

            def head_v(n, u, one):
                pe.wait_ge(qk_ready, n + 2) if one else pe.wait_ge(m_rows_ready, NT * n)
                nc.tensor.matmul(psH[0:S, 0:P], srcT[:, u, kv:kv + S], wT[:, 2, :], start=True, stop=False)
                nc.tensor.matmul(psH[0:S, 0:P], rows[0:1, 2, 0:S], rows[0:1, 0, :], start=False,
                                 stop=True).then_inc(v_projected, 1)

            at = [0]
            place = {}
            for x in range(NX):
                for side in range(2):
                    for part in use[x][side]:
                        place[x, side, part] = at[0]
                        at[0] += 1

            def head_rows(n, u, y):
                pe.wait_ge(parts_ready, 2 * (n + 1))
                after(pe, rows_ready, 4 * n + y)
                for x in (2 * y, 2 * y + 1):
                    for side, lo, w, o in ((0, 0, S, (x % 2) * S), (1, S, P, 2 * S + (x % 2) * P)):
                        mine = use[x][side]
                        for part in mine:
                            mm = nc.tensor.matmul(psX[0:KR, o:o + w], sel[:, place[x, side, part], :],
                                                  parts[:, u, part, lo:lo + w], start=(part == mine[0]),
                                                  stop=(part == mine[-1]))
                mm.then_inc(rows_full, 1)

            def head_max(n, g):
                pe.wait_ge(km_ready, 2 * n + g // (G // 2) + 1)
                after(pe, a_free, n * G + g - 1)
                for r in range(R):
                    x = g * R + r
                    mm = nc.tensor.matmul(psA[:, g % 2, 0:4 * S], Qr[0:KR, x, :], Km[0:KR, x, :, :],
                                          start=(r == 0), stop=(r == R - 1 and not causal))
                if causal:
                    mm = nc.tensor.matmul(psA[:, g % 2, :], identb[:, :], cm[:, 0, :, :], start=False, stop=True)
                mm.then_inc(a_full, 1)

            def head_m(n, k):
                pe.wait_ge(nm_ready, n + 1)
                pe.wait_ge(v_ready, n + 1)
                after(pe, m_rows_ready, NT * n + k)
                for g in range(4 * k, 4 * k + 4):
                    mm = nc.tensor.matmul(psH[KR:P, (g % 4) * P:(g % 4) * P + P], nM[:, g, :], identb[:, :],
                                          start=True, stop=True)
                mm.then_inc(m_transposed, 1)

            def scores(b, u, g):
                pe.wait_ge(qm_ready, b + 1)
                after(pe, e_ready, b * G + g - 1)
                for r in range(R):
                    x = g * R + r
                    mm = nc.tensor.matmul(psB[0:S, g % 2, :], Kr[:, u, x, :], Qm[:, x, :, :],
                                          start=(r == 0), stop=(r == R - 1 and not causal))
                if causal:
                    mm = nc.tensor.matmul(psB[0:S, g % 2, :], identb[:, :], cm[:, 1, :, :], start=False, stop=True)
                mm.then_inc(b_full, 1)

            def values(b, u, g):
                pe.wait_ge(e_ready, b * G + g + 1)
                if g == 0:
                    after(pe, x_done, b)
                per = 4 * HEADS // NS
                w = 4 * P // per
                for k in range(per):
                    h = g * per + k
                    j, o = h % 4, (h // 4) * w
                    mm = nc.tensor.matmul(psO[QUAD * j:QUAD * j + QUAD, o:o + w], Va[0:S, u, h, :],
                                          E[0:S, g % 4, k * w:k * w + w], start=True, stop=True)
                mm.then_inc(pv_done, 1)

            def back(b):
                pe.wait_ge(ot_ready, b + 1)
                for q in range(G):
                    mm = nc.tensor.transpose(psO[:, P * q:P * q + P], OTs[:, P * q:P * q + P], ident[:, :])
                mm.then_inc(back_done, 1)

            def turn_att(b):
                pe.wait_ge(att_ready, b + 1)
                nc.tensor.transpose(psO[:, 0:P], att[:, :], ident[:, :]).then_inc(att_transposed, 1)

            def project_out(b):
                pe.wait_ge(attT_ready, b + 1)
                nc.tensor.matmul(psO[:, P:2 * P], attT[:, :], wT[:, 3, :], start=True, stop=False)
                nc.tensor.matmul(psO[:, P:2 * P], rows[0:1, 2, :], rows[0:1, 1, :], start=False,
                                 stop=True).then_inc(y_ready, 1)

            pe.wait_ge(w_in, 16 * n_w)
            pe.wait_ge(setup_done, 1)
            for n in range(2):
                head_source(n, 0, n)
                head_qk(n, n)
            for y in range(4):
                head_rows(0, 0, y)
            head_v(0, 0, True)
            for g in range(G):
                head_max(0, g)
            for k in range(NT):
                head_m(0, k)

            def step(name, b, i, u, last, end):
                if name == "source" and not last:
                    head_source(b + 2, i + 1, u)
                if name == "qk" and not last:
                    head_qk(b + 2, u)
                if name == "v" and not end:
                    head_v(b + 1, 1 - u, not last)
                if name[:4] == "rows" and not end:
                    head_rows(b + 1, 1 - u, int(name[4:]))
                if name[:3] == "max" and not end:
                    head_max(b + 1, int(name[3:]))

            def slot(i, u):
                b = 2 * i + u
                last = isinstance(b, int) and b >= NB - 2
                end = isinstance(b, int) and b >= NB - 1
                for g in range(G):
                    for name in BEFORE[g]:
                        step(name, b, i, u, last, end)
                    scores(b, u, g)
                    if g >= 2:
                        values(b, u, g - 2)
                values(b, u, G - 2)
                values(b, u, G - 1)
                for k, name in enumerate(REST):
                    if k == BACK:
                        back(b)
                    step(name, b, i, u, last, end)
                turn_att(b)
                if not end:
                    head_m(b + 1, 0)
                project_out(b)
                if not end and NT == 2:
                    head_m(b + 1, 1)

            pairs(pe, slot, NB)

        stage.close()
        clear(nc, sems)


def mixture(nc, env, tag, E, L, d):
    X, H, ident = env.X, env.H, env.ident
    post = L == 1
    NCH = env.NB // CB
    K = L * NCH
    FT = 4
    GELU = ACT.Gelu_apprx_tanh if post else ACT.Gelu
    AT = dict(x=1, logits=2, xh=None, gates=5) if post else dict(x=0, logits=1, xh=2, gates=3)
    TANH_AT = AT["logits"] + 1

    with ExitStack() as ctx:
        def sb(name, shape, dt=F32):
            return ctx.enter_context(nc.sbuf_tensor(f"{tag}_{name}", shape, dt))

        def ps(name, shape):
            return ctx.enter_context(nc.psum_tensor(f"{tag}_{name}", shape, F32))

        sems = []

        def sem(name):
            sems.append(ctx.enter_context(nc.semaphore(f"{tag}_{name}")))
            return sems[-1]

        w1 = sb("w1", [P, E, FT * P])
        w2 = sb("w2", [P, E, FT, P])
        b1 = sb("b1", [P, L * E * FT])
        b2 = sb("b2", [E, P])
        rw = sb("rw", [P, L * E])
        rank = sb("rank", [P, E])
        sel = sb("sel", [E, E, P])
        xs = sb("xs", [P, 2, CB, P])
        xT = sb("xT", [P, 2, CT])
        lg = sb("lg", [P, CB, E])
        l2 = sb("l2", [P, CB, E])
        t1 = sb("t1", [P, CB, E])
        k1 = sb("k1", [P, CB, E])
        k2 = sb("k2", [P, CB, E])
        m1 = sb("m1", [P, CB])
        m2 = sb("m2", [P, CB])
        r1 = sb("r1", [P, CB])
        gap = sb("gap", [P, CB])
        th = sb("th", [P, CB])
        wa = sb("wa", [P, CB])
        wb = sb("wb", [P, CB])
        sw = sb("sw", [P, 2, CB])
        comb = sb("comb", [P, CB, E])
        gT = sb("gT", [E, 2, CT])
        h1 = sb("h1", [P, 2, FT, CT])
        yT = sb("yT", [P, CT])
        st = sb("st", [P, CB, 6])
        mv = sb("mv", [P, CB, 2])
        veps = sb("veps", [P, CB])
        rstd = sb("rstd", [P, CB])
        if post:
            z = sb("z", [P, CB, P])
            gb = sb("gb", [P, 2, P])
        else:
            lng = sb("lng", [P, L * E])
            lnb = sb("lnb", [P, L * E])
            rb = sb("rb", [P, L * E])
            xh = sb("xh", [P, CB, P])
            xhT = sb("xhT", [P, 2, CT])
            mark = sb("mark", [P, NCH])
            xe = sb("xe", [P, 2, CT])

        psR = ps("psR", [P, FT, BANK])
        psG = ps("psG", [P, 2, BANK])
        psY = ps("psY", [P, BANK])
        psH = ps("psH", [P, BANK])

        c_in = sem("c_in")
        w_in = [sem(f"w_in{e}") for e in range(E)]
        b2_in = sem("b2_in")
        xs_in = [sem("xs_in0"), sem("xs_in1")]
        stats_ready = sem("stats_ready")
        rstd_ready = sem("rstd_ready")
        xh_ready = sem("xh_ready")
        x_transposed = sem("x_transposed")
        xT_ready = sem("xT_ready")
        logits_full = sem("logits_full")
        logits_read = sem("logits_read")
        gap_ready = sem("gap_ready")
        tanh_ready = sem("tanh_ready")
        comb_ready = sem("comb_ready")
        xh_transposed = sem("xh_transposed")
        xhT_ready = sem("xhT_ready")
        g_transposed = sem("g_transposed")
        gT_ready = sem("gT_ready")
        g_full = sem("g_full")
        xe_ready = sem("xe_ready")
        r_full = sem("r_full")
        h1_ready = sem("h1_ready")
        hg_ready = sem("hg_ready")
        expert_done = sem("expert_done")
        y_full = sem("y_full")
        yT_ready = sem("yT_ready")
        z_full = sem("z_full")
        z_read = sem("z_read")
        x_done = sem("x_done")
        dve_chain = sem("dve_chain")
        pool_chain = sem("pool_chain")
        sum_ready = sem("sum_ready")
        out_written = sem("out_written")
        n_c = 5 + (1 if post else 3) + (0 if not post else 0)

        stage = ExitStack()
        block = stage.enter_context(nc.Block())

        def load_expert(sp, l, e):
            sp.dma_start(w1[:, e, :], d["w1"][l * E + e]).then_inc(w_in[e], 16)
            sp.dma_start(w2[:, e, :, :], d["w2"][l * E + e].rearrange("(t p) m -> p t m", p=P)).then_inc(w_in[e], 16)

        @block.sync
        def _(sp):
            sp.dma_start(b1[:, :], d["b1"]).then_inc(c_in, 16)
            sp.dma_start(rw[:, :], d["rw"]).then_inc(c_in, 16)
            sp.dma_start(rank[:, :], d["rank"]).then_inc(c_in, 16)
            sp.dma_start(sel[:, :, :], d["sel"]).then_inc(c_in, 16)
            if post:
                sp.dma_start(gb[:, :, :], d["gb"].partition_broadcast(P)).then_inc(c_in, 16)
            else:
                sp.dma_start(lng[:, :], d["lng"]).then_inc(c_in, 16)
                sp.dma_start(lnb[:, :], d["lnb"]).then_inc(c_in, 16)
                sp.dma_start(rb[:, :], d["rb"].partition_broadcast(P)).then_inc(c_in, 16)
            sp.dma_start(b2[:, :], d["b2"][0]).then_inc(b2_in, 16)
            for e in range(E):
                load_expert(sp, 0, e)
            if L > 1:
                with sp.Fori(1, L) as l:
                    for e in range(E):
                        sp.wait_ge(expert_done, (l * NCH - 1) * E + e + 1)
                        load_expert(sp, l, e)
                    sp.wait_ge(y_full, l * NCH)
                    sp.dma_start(b2[:, :], d["b2"][l]).then_inc(b2_in, 16)
                for c in range(NCH):
                    sp.wait_ge(sum_ready, c + 1)
                    sp.dma_start(d["out"][CB * c:CB * c + CB].rearrange("b t m -> t b m"),
                                 X[:, CB * c:CB * c + CB, :]).then_inc(out_written, 16)
                sp.wait_ge(out_written, 16 * NCH)

        @block.gpsimd
        def _(pool):
            chain = Chain(pool, pool_chain)

            def load_source(n, u):
                after(pool, x_transposed, n - 1)
                if not post:
                    pool.wait_ge(x_done, n + 1)
                c = n % NCH
                pool.dma_start(xs[:, u, :, :], H[:, bass.ds(CB * c, CB), :]).then_inc(xs_in[u], 16)

            def rstds(n):
                pool.wait_ge(stats_ready, n + 1)
                chain.link(nc.gpsimd.tensor_tensor(veps[:, :], mv[:, :, 1], env.eps[:, 0:1].to_broadcast([P, CB]), ALU.add))
                nc.gpsimd.tensor_tensor(rstd[:, :], veps[:, :], env.minus_half[:, 0:1].to_broadcast([P, CB]),
                                        ALU.pow).then_inc(rstd_ready, 1)

            def add_residual(c):
                pool.wait_ge(x_done, L * NCH + c + 1)
                nc.gpsimd.tensor_tensor(X[:, CB * c:CB * c + CB, :], X[:, CB * c:CB * c + CB, :],
                                        H[:, CB * c:CB * c + CB, :], ALU.add).then_inc(sum_ready, 1)

            load_source(0, 0)
            load_source(1, 1)
            chain.slot(0)
            if not post:
                rstds(0)

            def slot(i, u):
                k = 2 * i + u
                first = isinstance(k, int) and k == 0
                last = isinstance(k, int) and k >= K - 2
                end = isinstance(k, int) and k >= K - 1
                if post:
                    chain.slot(max(k - 1, 0) if isinstance(k, int) else k - 1)
                    if not first:
                        rstds(k - 1)
                else:
                    chain.slot(k + 1)
                    if not end:
                        rstds(k + 1)
                if not last:
                    load_source(k + 2, u)
                if not post and last:
                    for c in range(0 if not end else NCH - 3, NCH - 3 if not end else NCH - 2):
                        add_residual(c)

            pairs(pool, slot, K)
            if not post:
                for c in range(NCH - 2, NCH):
                    add_residual(c)
            else:
                chain.slot(K - 1)
                rstds(K - 1)

        @block.scalar
        def _(act):
            def head_xT(n, u):
                act.wait_ge(x_transposed, n + 1)
                nc.scalar.activation(xT[:, u, :], psH[:, :], ACT.Copy).then_inc(xT_ready, 1)

            def head_tanh(n):
                act.wait_ge(gap_ready, n + 1)
                nc.scalar.activation(th[:, :], gap[:, :], ACT.Tanh, scale=0.5).then_inc(tanh_ready, 1)

            def head_xhT(n, u):
                act.wait_ge(xh_transposed, n + 1)
                nc.scalar.activation(xhT[:, u, :], psH[:, :], ACT.Copy).then_inc(xhT_ready, 1)

            def gelus(k, e):
                g = k * E + e
                l = k // NCH if L > 1 else 0
                after(act, expert_done, g - 1)
                for f in range(FT):
                    act.wait_ge(r_full, FT * g + f + 1)
                    nc.scalar.activation(h1[:, e % 2, f, :], psR[:, f, :], GELU,
                                         bias=b1[:, bass.ds((l * E + e) * FT + f, 1)]).then_inc(h1_ready, 1)

            act.wait_ge(c_in, 16 * (n_c - 1))
            head_xT(0, 0)
            head_tanh(0)
            if not post:
                head_xhT(0, 0)

            def slot(i, u):
                k = 2 * i + u
                end = isinstance(k, int) and k >= K - 1
                for e in range(E):
                    gelus(k, e)
                    if end:
                        continue
                    if e == AT["x"]:
                        head_xT(k + 1, 1 - u)
                    if e == TANH_AT:
                        head_tanh(k + 1)
                    if e == AT["xh"]:
                        head_xhT(k + 1, 1 - u)
                act.wait_ge(y_full, k + 1)
                nc.scalar.activation(yT[:, :], psY[:, :], ACT.Copy).then_inc(yT_ready, 1)

            pairs(act, slot, K)

        @block.vector
        def _(dve):
            chain = Chain(dve, dve_chain)

            def col(t):
                return t.unsqueeze(2).to_broadcast([P, CB, E])

            def row(t):
                return t.unsqueeze(1).to_broadcast([P, CB, E])

            def head_norm(n, c):
                if post:
                    return
                for j in range(CB):
                    mm = nc.vector.bn_stats(st[:, j, :], H[:, CB * c + j, :])
                chain.link(mm)
                apart(nc, env)
                for j in range(CB):
                    mm = nc.vector.bn_aggr(mv[:, j, :], st[:, j, :])
                mm.then_inc(stats_ready, 1)
                dve.wait_ge(rstd_ready, n + 1)
                after(dve, xh_transposed, n)
                for j in range(CB):
                    mm = nc.vector.tensor_scalar(xh[:, j, :], H[:, CB * c + j, :], mv[:, j, 0:1],
                                                 rstd[:, j:j + 1], ALU.subtract, ALU.mult)
                mm.then_inc(xh_ready, 1)

            def route_pick(n):
                l = n // NCH if L > 1 else 0
                dve.wait_ge(logits_full, n + 1)
                full = psH[:, 0:CB * E].rearrange("t (j e) -> t j e", e=E)
                if post:
                    nc.vector.tensor_copy(lg[:, :, :], full).then_inc(logits_read, 1)
                else:
                    nc.vector.tensor_tensor(lg[:, :, :], full, row(rb[:, bass.ds(l * E, E)]),
                                            ALU.add).then_inc(logits_read, 1)
                dve.wait_ge(logits_read, n + 1)
                link = chain.link
                for src, top, mask in ((lg, m1, k1), (l2, m2, k2)):
                    if src is l2:
                        link(nc.vector.scalar_tensor_tensor(l2[:, :, :], k1[:, :, :], 3.0 * NEG, lg[:, :, :],
                                                            ALU.mult, ALU.add))
                    link(nc.vector.tensor_reduce(top[:, :], src[:, :, :], AX.X, ALU.max))
                    link(nc.vector.tensor_tensor(t1[:, :, :], src[:, :, :], col(top[:, :]), ALU.is_ge))
                    link(nc.vector.tensor_tensor(t1[:, :, :], t1[:, :, :], row(rank[:, :]), ALU.mult))
                    link(nc.vector.tensor_reduce(r1[:, :], t1[:, :, :], AX.X, ALU.max))
                    link(nc.vector.tensor_tensor(mask[:, :, :], t1[:, :, :], col(r1[:, :]), ALU.is_equal))
                nc.vector.tensor_tensor(gap[:, :], m1[:, :], m2[:, :], ALU.subtract).then_inc(gap_ready, 1)

            def route_weigh(n, u):
                dve.wait_ge(tanh_ready, n + 1)
                nc.vector.tensor_scalar(wa[:, :], th[:, :], 0.5, 0.5, ALU.mult, ALU.add)
                chain.link(nc.vector.tensor_scalar(wb[:, :], th[:, :], -0.5, 0.5, ALU.mult, ALU.add))
                nc.vector.tensor_tensor(sw[:, u, :], wa[:, :], wb[:, :], ALU.add)
                nc.vector.tensor_tensor(k1[:, :, :], k1[:, :, :], col(wa[:, :]), ALU.mult)
                chain.link(nc.vector.tensor_tensor(k2[:, :, :], k2[:, :, :], col(wb[:, :]), ALU.mult))
                nc.vector.tensor_tensor(comb[:, :, :], k1[:, :, :], k2[:, :, :], ALU.add).then_inc(comb_ready, 1)

            def head_gT(n, u):
                dve.wait_ge(g_transposed, n + 1)
                nc.vector.tensor_copy(gT[:, u, :], psH[0:E, :]).then_inc(gT_ready, 1)

            def expert_input(k, u, e):
                g = k * E + e
                if post:
                    return
                l = k // NCH
                dve.wait_ge(xhT_ready, k + 1)
                after(dve, r_full, FT * (g - 1))
                nc.vector.tensor_scalar(xe[:, e % 2, :], xhT[:, u, :], lng[:, bass.ds(l * E + e, 1)],
                                        lnb[:, bass.ds(l * E + e, 1)], ALU.mult, ALU.add).then_inc(xe_ready, 1)

            def gate_hidden(k, e):
                g = k * E + e
                dve.wait_ge(g_full, g + 1)
                for f in range(FT):
                    dve.wait_ge(h1_ready, FT * g + f + 1)
                    nc.vector.tensor_tensor(h1[:, e % 2, f, :], h1[:, e % 2, f, :], psG[:, e % 2, :],
                                            ALU.mult).then_inc(hg_ready, 1)

            def finish(k, u, c):
                dve.wait_ge(z_full, k + 1)
                zz = psY[:, :].rearrange("t (j m) -> t j m", m=P)
                if not post:
                    for j in range(CB):
                        mm = nc.vector.scalar_tensor_tensor(H[:, CB * c + j, :], H[:, CB * c + j, :],
                                                            sw[:, u, j:j + 1], zz[:, j, :], ALU.mult, ALU.add)
                    mm.then_inc(x_done, 1)
                    return
                nc.vector.tensor_tensor(z[:, :, :], H[:, bass.ds(CB * c, CB), :], zz, ALU.add).then_inc(z_read, 1)
                dve.wait_ge(z_read, k + 1)
                for j in range(CB):
                    mm = nc.vector.bn_stats(st[:, j, :], z[:, j, :])
                chain.link(mm)
                apart(nc, env)
                for j in range(CB):
                    mm = nc.vector.bn_aggr(mv[:, j, :], st[:, j, :])
                mm.then_inc(stats_ready, 1)
                dve.wait_ge(rstd_ready, k + 1)
                for j in range(CB):
                    mm = nc.vector.tensor_scalar(z[:, j, :], z[:, j, :], mv[:, j, 0:1], rstd[:, j:j + 1],
                                                 ALU.subtract, ALU.mult)
                chain.link(mm)
                for n, op in ((0, ALU.mult), (1, ALU.add)):
                    chain.link(nc.vector.tensor_tensor(z[:, :, :], z[:, :, :],
                                                       gb[:, n, :].unsqueeze(1).to_broadcast([P, CB, P]), op))
                nc.vector.tensor_tensor(X[:, bass.ds(CB * c, CB), :], X[:, bass.ds(CB * c, CB), :], z[:, :, :],
                                        ALU.add).then_inc(x_done, 1)

            dve.wait_ge(c_in, 16 * (n_c - 1))
            chain.slot(0)
            if not post:
                for c in range(NCH):
                    nc.vector.memset(mark[:, c:c + 1], 0.0).then_inc(x_done, 1)
            head_norm(0, 0)
            route_pick(0)
            route_weigh(0, 0)
            head_gT(0, 0)
            SETUP = chain.n
            LINKS = [None, None]

            def slot(i, u):
                k = 2 * i + u
                first = isinstance(k, int) and k == 0
                end = isinstance(k, int) and k >= K - 1
                if first:
                    chain.slot(SETUP)
                else:
                    chain.slot(SETUP + LINKS[0] + (LINKS[1] or 0) * (k - 1))
                expert_input(k, u, 0)
                for e in range(E):
                    if e + 1 < E:
                        expert_input(k, u, e + 1)
                    gate_hidden(k, e)
                    if e == 0 and not first:
                        finish(k - 1, 1 - u, (k - 1) % NCH)
                    if end:
                        continue
                    if e == AT["x"]:
                        head_norm(k + 1, (k + 1) % NCH)
                    if e == AT["logits"]:
                        route_pick(k + 1)
                    if e == TANH_AT:
                        route_weigh(k + 1, 1 - u)
                    if e == AT["gates"]:
                        head_gT(k + 1, 1 - u)
                if first:
                    LINKS[0] = chain.n
                elif LINKS[1] is None:
                    LINKS[1] = chain.n

            pairs(dve, slot, K)
            finish(K - 1, (K - 1) % 2, (K - 1) % NCH)

        @block.tensor
        def _(pe):
            def head_x(n, h, u):
                pe.wait_ge(xs_in[u], 16 * (h + 1))
                after(pe, gT_ready, n)
                for j in range(CB):
                    mm = nc.tensor.transpose(psH[:, P * j:P * j + P], xs[:, u, j, :], ident[:, :])
                mm.then_inc(x_transposed, 1)

            def head_logits(n, u):
                l = n // NCH if L > 1 else 0
                pe.wait_ge(xT_ready, n + 1)
                for j in range(CB):
                    mm = nc.tensor.matmul(psH[:, E * j:E * j + E], xT[:, u, P * j:P * j + P],
                                          rw[:, bass.ds(l * E, E)], start=True, stop=True)
                mm.then_inc(logits_full, 1)

            def head_xh(n):
                pe.wait_ge(xh_ready, n + 1)
                pe.wait_ge(logits_read, n + 1)
                for j in range(CB):
                    mm = nc.tensor.transpose(psH[:, P * j:P * j + P], xh[:, j, :], ident[:, :])
                mm.then_inc(xh_transposed, 1)

            def head_gates(n):
                pe.wait_ge(comb_ready, n + 1)
                if not post:
                    pe.wait_ge(xhT_ready, n + 1)
                for j in range(CB):
                    mm = nc.tensor.transpose(psH[0:E, P * j:P * j + P], comb[:, j, :], ident[:, :])
                mm.then_inc(g_transposed, 1)

            def gates(k, u, e):
                g = k * E + e
                pe.wait_ge(gT_ready, k + 1)
                after(pe, hg_ready, FT * (g - 1))
                nc.tensor.matmul(psG[:, e % 2, :], sel[:, e, :], gT[:, u, :], start=True,
                                 stop=True).then_inc(g_full, 1)

            def hidden(k, u, e):
                g = k * E + e
                l = k // NCH if L > 1 else 0
                pe.wait_ge(w_in[e], 32 * (l + 1))
                pe.wait_ge(xT_ready, k + 1) if post else pe.wait_ge(xe_ready, g + 1)
                for f in range(FT):
                    after(pe, h1_ready, FT * (g - 1) + f + 1)
                    rhs = xT[:, u, :] if post else xe[:, e % 2, :]
                    nc.tensor.matmul(psR[:, f, :], w1[:, e, P * f:P * f + P], rhs, start=True,
                                     stop=True).then_inc(r_full, 1)

            def outputs(k, u, e):
                g = k * E + e
                if e == 0:
                    after(pe, z_read, k) if post else pe.wait_ge(x_done, k + NCH)
                for f in range(FT):
                    pe.wait_ge(hg_ready, FT * g + f + 1)
                    mm = nc.tensor.matmul(psY[:, :], w2[:, e, f, :], h1[:, e % 2, f, :],
                                          start=(e == 0 and f == 0), stop=False)
                mm.then_inc(expert_done, 1)
                if e == E - 1:
                    l = k // NCH if L > 1 else 0
                    pe.wait_ge(b2_in, 16 * (l + 1))
                    nc.tensor.matmul(psY[:, :], b2[:, :], gT[:, u, :], start=False, stop=True).then_inc(y_full, 1)

            def back(k):
                pe.wait_ge(yT_ready, k + 1)
                for j in range(CB):
                    mm = nc.tensor.transpose(psY[:, P * j:P * j + P], yT[:, P * j:P * j + P], ident[:, :])
                mm.then_inc(z_full, 1)

            pe.wait_ge(c_in, 16 * (n_c - 1))
            head_x(0, 0, 0)
            head_logits(0, 0)
            if not post:
                head_xh(0)
            head_gates(0)

            def slot(i, u):
                k = 2 * i + u
                first = isinstance(k, int) and k == 0
                end = isinstance(k, int) and k >= K - 1
                for e in range(E):
                    gates(k, u, e)
                    hidden(k, u, e)
                    if e == 0 and not first:
                        back(k - 1)
                    if e >= 1:
                        outputs(k, u, e - 1)
                    if end:
                        continue
                    if e == AT["x"]:
                        head_x(k + 1, i + u, 1 - u)
                    if e == AT["logits"]:
                        head_logits(k + 1, 1 - u)
                    if e == AT["xh"]:
                        head_xh(k + 1)
                    if e == AT["gates"]:
                        head_gates(k + 1)
                outputs(k, u, E - 1)

            pairs(pe, slot, K)
            back(K - 1)

        stage.close()
        clear(nc, sems)


def build(nc, a, NB, S):
    with ExitStack() as ctx:
        env = Env()
        env.NB = NB
        env.X = ctx.enter_context(nc.sbuf_tensor("X", [P, NB, P], F32))
        env.H = ctx.enter_context(nc.sbuf_tensor("H", [P, NB, P], F32))
        env.ident = ctx.enter_context(nc.sbuf_tensor("ident", [P, P], F32))
        env.identb = ctx.enter_context(nc.sbuf_tensor("identb", [P, P], BF16))
        env.scratch = ctx.enter_context(nc.sbuf_tensor("scratch", [P, 1], F32))
        env.eps = ctx.enter_context(nc.sbuf_tensor("eps", [P, 1], F32))
        env.zero = ctx.enter_context(nc.sbuf_tensor("zero", [P, 1], F32))
        env.minus_half = ctx.enter_context(nc.sbuf_tensor("minus_half", [P, 1], F32))
        const_in = ctx.enter_context(nc.semaphore("const_in"))
        with nc.Block() as block:
            @block.sync
            def _(sp):
                sp.dma_start(env.ident[:, :], a["c_ident"]).then_inc(const_in, 16)
                sp.dma_start(env.identb[:, :], a["c_identb"]).then_inc(const_in, 16)
                sp.dma_start(env.minus_half[:, :], a["c_minus_half"]).then_inc(const_in, 16)
                sp.dma_start(env.eps[:, :], a["c_eps"]).then_inc(const_in, 16)
                sp.dma_start(env.zero[:, :], a["c_zero"]).then_inc(const_in, 16)
                sp.wait_ge(const_in, 80)

        wide = dict(mask=a["c_mask32"], sel=a["c_sel32"], use=part_use(32))
        narrow = dict(mask=a["c_mask16"], sel=a["c_sel16"], use=part_use(16))
        attention(nc, env, "xa0", NB, S, 2 * HEADS, False, True, False, dict(
            wide, x=a["x"], ctx=a["ctx"], w=a["xa0_w"], qkb=a["xa0_qkb"], rows=a["xa0_rows"],
            lam=[a[f"lam{n}"] for n in range(4)]))
        attention(nc, env, "sa", NB, P, HEADS, True, False, True, dict(
            narrow, w=a["sa_w"], qkb=a["sa_qkb"], rows=a["sa_rows"], cm=a["c_cm"], gb=a["sa_gb"]))
        mixture(nc, env, "m0", a["m0_b2"].shape[1], 1, dict(
            {n: a[f"m0_{n}"] for n in ("w1", "w2", "b1", "b2", "rw", "gb")}, rank=a["c_rank8"], sel=a["c_sel8"]))
        attention(nc, env, "xa1", NB, S, HEADS, False, False, True, dict(
            narrow, ctx=a["ctx"], w=a["xa1_w"], qkb=a["xa1_qkb"], rows=a["xa1_rows"]))
        mixture(nc, env, "m1", a["m1_b2"].shape[1], a["m1_b2"].shape[0], dict(
            {n: a[f"m1_{n}"] for n in ("w1", "w2", "b1", "b2", "rw", "lng", "lnb", "rb")},
            rank=a["c_rank4"], sel=a["c_sel4"], out=a["out"]))


HI, MID, LO = 0, 1, 2
PRODUCTS = [(HI, HI), (HI, MID), (MID, HI), (MID, MID), (HI, LO), (LO, HI)]


def set_products(ns, x):
    R = 8 // (ns // 4)
    n = 6 // R
    return PRODUCTS[n * (x % R):n * (x % R) + n]


def part_use(ns):
    return [[sorted({pr[side] for pr in set_products(ns, x)}) for side in range(2)] for x in range(8)]


def constants(NP, S):
    bf = mybir.dt.np(BF16)
    r = NP.arange
    c = {"ident": NP.eye(P, dtype="float32"), "identb": NP.eye(P).astype(bf),
         "eps": NP.full((P, 1), EPS, "float32"), "minus_half": NP.full((P, 1), -0.5, "float32"),
         "zero": NP.zeros((P, 1), "float32")}
    for ns in (32, 16):
        w = 4 * (P // ns)
        R = 8 // (ns // 4)
        mask = NP.zeros((P, 4), "float32")
        mask[r(96), (r(96) % w) // (w // 4)] = 1
        mask[96 + r(12), r(12) % 4] = 1
        c[f"mask{ns}"] = mask
        sel = []
        for x in range(8):
            for side in range(2):
                for part in part_use(ns)[x][side]:
                    m = NP.zeros((P, 96))
                    for n, pr in enumerate(set_products(ns, x)):
                        if pr[side] == part:
                            m[w * (x // R) + r(w), w * n + r(w)] = 1
                    sel.append(m)
        c[f"sel{ns}"] = NP.stack(sel, 1).astype(bf)
    future = (r(P)[None, :] > r(P)[:, None])
    m = NP.stack([future, future.T], 1)[:, :, None, :] * NEG
    c["cm"] = NP.ascontiguousarray(NP.broadcast_to(m, (P, 2, 4, P))).astype(bf)
    for e in (8, 4):
        c[f"rank{e}"] = NP.broadcast_to((e - r(e))[None], (P, e)).astype("float32")
        c[f"sel{e}"] = NP.ascontiguousarray(NP.broadcast_to(NP.eye(e)[:, :, None], (e, e, P))).astype("float32")
    return c


def kernel(**inputs):
    import numpy as np
    import concourse.bacc as _bacc
    from concourse import mybir as _mybir
    from concourse.bass_utils import run_bass_kernel_spmd as _run

    i = {n: np.asarray(v) for n, v in inputs.items()}
    NB, T, D = i["x"].shape
    S = i["ctx_1024"].shape[1]
    L, E4, _, F = i["L1_ffn_w1"].shape
    E8 = i["L0_ffn_wg"].shape[1]
    zero = np.zeros(D, "float32")
    one = np.ones(D, "float32")
    wi, bi = i["L0_xattn_in_proj_weight"], i["L0_xattn_in_proj_bias"]
    wq = i["L0_ffn_w_qkv"]
    arr = {
        "x": i["x"], "ctx": i["ctx_1024"],
        "xa0_w": np.stack([wi[:D].T, wi[D:2 * D].T, wi[2 * D:].T, i["L0_xattn_out_proj_weight"].T], 1),
        "xa0_qkb": np.stack([bi[:D], bi[D:2 * D]], 1),
        "xa0_rows": np.stack([bi[2 * D:], i["L0_xattn_out_proj_bias"], one])[None],
        "lam0": i["L0_xattn_lambda_q1"], "lam1": i["L0_xattn_lambda_k1"],
        "lam2": i["L0_xattn_lambda_q2"], "lam3": i["L0_xattn_lambda_k2"],
        "sa_w": np.stack([wq[:, :D], wq[:, D:2 * D], wq[:, 2 * D:], i["L0_ffn_w_o"]], 1),
        "sa_qkb": np.stack([zero, zero], 1), "sa_rows": np.stack([zero, zero, one])[None],
        "sa_gb": np.stack([i["L0_ffn_g1"], i["L0_ffn_b1"]]),
        "m0_w1": i["L0_ffn_w1"], "m0_w2": i["L0_ffn_w2"], "m0_b2": i["L0_ffn_bb2"][None],
        "m0_b1": i["L0_ffn_bb1"].reshape(E8 * F // P, P).T, "m0_rw": i["L0_ffn_wg"],
        "m0_gb": np.stack([i["L0_ffn_g2"], i["L0_ffn_b2"]]),
        "xa1_w": np.stack([i["L1_xattn_Wq"], i["L1_xattn_Wk"], i["L1_xattn_Wv"], i["L1_xattn_Wo"]], 1),
        "xa1_qkb": np.stack([i["L1_xattn_bq"], i["L1_xattn_bk"]], 1),
        "xa1_rows": np.stack([i["L1_xattn_bv"], i["L1_xattn_bo"], one])[None],
        "m1_w1": i["L1_ffn_w1"].reshape(L * E4, D, F), "m1_w2": i["L1_ffn_w2"].reshape(L * E4, F, D),
        "m1_b2": i["L1_ffn_b2"], "m1_b1": i["L1_ffn_b1"].reshape(L * E4 * F // P, P).T,
        "m1_rw": i["L1_ffn_router_w"].transpose(1, 0, 2).reshape(D, L * E4),
        "m1_lng": i["L1_ffn_ln_g"].reshape(L * E4, D).T, "m1_lnb": i["L1_ffn_ln_b"].reshape(L * E4, D).T,
        "m1_rb": i["L1_ffn_router_b"].reshape(L * E4),
    }
    arr.update({f"c_{n}": v for n, v in constants(np, S).items()})
    arr = {n: np.ascontiguousarray(v) for n, v in arr.items()}

    nc = _bacc.Bacc("TRN2", target_bir_lowering=False, num_devices=1)
    aps = {n: nc.dram_tensor(f"in_{n}", v.shape, _mybir.dt.from_np(v.dtype), kind="ExternalInput").ap()
           for n, v in arr.items()}
    aps["out"] = nc.dram_tensor("out_x", (NB, T, D), F32, kind="ExternalOutput").ap()
    build(nc, aps, NB, S)
    r = _run(nc, [{f"in_{n}": v for n, v in arr.items()}], core_ids=[0])
    return r.results[0]["out_x"]
```

```python
from contextlib import ExitStack

import concourse.bass as bass
from concourse import mybir

F32 = mybir.dt.float32
BF16 = mybir.dt.bfloat16
F32R = mybir.dt.float32r
ALU = mybir.AluOpType
ACT = mybir.ActivationFunctionType
AX = mybir.AxisListType

P = 128
HEADS = 16
HD = P // HEADS
QUAD = 32
BANK = 512
EPS = 1e-5
LAMBDA_INIT = 0.2
CB = 4
CT = CB * P
NEG = -1.0e30


def after(eng, sem, value):
    if not isinstance(value, int) or value > 0:
        eng.wait_ge(sem, value)


def pairs(eng, slot, n):
    slot(0, 0)
    slot(0, 1)
    with eng.Fori(1, n // 2 - 1) as i:
        slot(i, 0)
        slot(i, 1)
    slot(n // 2 - 1, 0)
    slot(n // 2 - 1, 1)


def apart(nc, env):
    nc.vector.memset(env.scratch[:, :], 0.0)


class Chain:

    def __init__(self, eng, sem):
        self.eng, self.sem, self.base, self.n = eng, sem, 0, 0

    def slot(self, base):
        self.base, self.n = base, 0

    def link(self, ins):
        self.n += 1
        ins.then_inc(self.sem, 1)
        self.eng.wait_ge(self.sem, self.base + self.n)


def clear(nc, sems):
    with nc.Block() as block:
        @block.sync
        def _(sp):
            for s in sems:
                sp.sem_clear(s)


class Env:
    pass


def attention(nc, env, tag, NB, S, NS, causal, diff, norm, d):
    G = NS // 4
    R = 8 // G
    NX = G * R
    SCALE = 1.0 / float(P // NS) ** 0.5
    X, H, ident, identb = env.X, env.H, env.ident, env.identb
    KR = 96
    VW = QUAD
    kv = P if not causal else 0
    WS = S + P if not causal else P
    use = d["use"]

    with ExitStack() as ctx:
        def sb(name, shape, dt=F32):
            return ctx.enter_context(nc.sbuf_tensor(f"{tag}_{name}", shape, dt))

        def ps(name, shape):
            return ctx.enter_context(nc.psum_tensor(f"{tag}_{name}", shape, F32))

        sems = []

        def sem(name):
            sems.append(ctx.enter_context(nc.semaphore(f"{tag}_{name}")))
            return sems[-1]

        wT = sb("wT", [P, 4, P])
        qkb = sb("qkb", [P, 2])
        qbs = sb("qbs", [P, 1])
        rows = sb("rows", [1, 3, P])
        mask = sb("mask", [P, 4])
        n_sel = sum(len(part) for sides in use for part in sides)
        sel = sb("sel", [P, n_sel, KR], BF16)
        xn = sb("xn", [P, 2, P])
        stats = sb("stats", [P, 6])
        mv = sb("mv", [P, 2, 2])
        veps = sb("veps", [P, 1])
        rstd = sb("rstd", [P, 2])
        cx = sb("cx", [P, 2, P])
        srcT = sb("srcT", [P, 2, WS])
        QK = sb("QK", [P, S + P])
        rest = sb("rest", [P, S + P])
        parts = sb("parts", [P, 2, 3, S + P], BF16)
        Va = sb("Va", [P, 2, HEADS, VW])
        Kr = sb("Kr", [P, 2, NX, S], BF16)
        Qr = sb("Qr", [P, 2, NX, P], BF16)
        Km = sb("Km", [P, NX, 4, S], BF16)
        Qm = sb("Qm", [P, NX, 4, P], BF16)
        M = sb("M", [P, NS])
        Mr = sb("Mr", [P, NS])
        nM = sb("nM", [P, G, QUAD], BF16)
        E = sb("E", [P, 4, 4 * P])
        OTs = sb("OTs", [P, NS * QUAD])
        rec = sb("rec", [P, NS])
        pv = sb("pv", [P, NS, HD])
        att = sb("att", [P, P])
        attT = sb("attT", [P, P])
        if causal:
            cm = sb("cm", [P, 2, 4, P], BF16)
            z = sb("z", [P, P])
            gb = sb("gb", [P, 2, P])
        if norm:
            stats2 = sb("stats2", [P, 6])
            mv2 = sb("mv2", [P, 2])
            veps2 = sb("veps2", [P, 1])
            rstd2 = sb("rstd2", [P, 1])
        if diff:
            lq = sb("lq", [P, 4, P // NS])
            lp = sb("lp", [P, 2, P // NS])
            ld = sb("ld", [P, 2])
            le = sb("le", [P, 2])
            nlam = sb("nlam", [P, 1])

        psA = ps("psA", [P, 2, BANK])
        psB = ps("psB", [P, 2, BANK])
        psX = ps("psX", [P, BANK])
        psH = ps("psH", [P, BANK])
        psO = ps("psO", [P, 2, BANK])

        w_in = sem("w_in")
        x_first = sem("x_first")
        x_rest = sem("x_rest")
        ctx_in = [sem("ctx_in0"), sem("ctx_in1")]
        setup_done = sem("setup_done")
        lam_dots = sem("lam_dots")
        lam_exp = sem("lam_exp")
        stats_ready = sem("stats_ready")
        rstd_ready = sem("rstd_ready")
        xn_ready = sem("xn_ready")
        xn_kept = sem("xn_kept")
        src_transposed = sem("src_transposed")
        srcT_ready = sem("srcT_ready")
        qk_projected = sem("qk_projected")
        qk_ready = sem("qk_ready")
        parts_ready = sem("parts_ready")
        v_projected = sem("v_projected")
        v_ready = sem("v_ready")
        rows_full = sem("rows_full")
        rows_ready = sem("rows_ready")
        km_ready = sem("km_ready")
        a_full = sem("a_full")
        a_free = sem("a_free")
        nm_ready = sem("nm_ready")
        m_transposed = sem("m_transposed")
        m_rows_ready = sem("m_rows_ready")
        qm_ready = sem("qm_ready")
        b_full = sem("b_full")
        e_ready = sem("e_ready")
        pv_done = sem("pv_done")
        ot_ready = sem("ot_ready")
        back_done = sem("back_done")
        att_ready = sem("att_ready")
        att_transposed = sem("att_transposed")
        attT_ready = sem("attT_ready")
        y_ready = sem("y_ready")
        x_done = sem("x_done")
        stats2_ready = sem("stats2_ready")
        rstd2_ready = sem("rstd2_ready")
        dve_chain = sem("dve_chain")
        pool_chain = sem("pool_chain")

        n_w = 5 + (2 if causal else 0) + (4 if diff else 0)
        if diff:
            ORDER = """mB scores0 stats qmB rows2 norm scores1 lastback max0 max1 values0 v rows3
                source lastatt scores2 kmB scores3 max2 max3 lastturn lastattT qk values1
                values2 max4 scores4 max5 scores5 lastproj values3 nmA otA max6 scores6 lastadd
                max7 scores7 backA mA rows0 attA values4 nmB values5 rows1 values6 qmA values7
                otB kmA"""
        elif causal:
            ORDER = """stats mB qmB norm scores0 rows2 v max0 rows3 lastback source lastatt kmB max1 qk
                scores1 lastturn nmA lastattT max2 max3 scores2 mA lastproj scores3 rows0
                lastadd values0 values1 nmB values2 qmA rows1 lastout values3 kmA otB"""
        else:
            ORDER = """scores0 lastback stats mB qmB rows2 v norm lastatt scores1 rows3 max0 source
                max1 lastturn qk lastattT scores2 values0 nmA lastproj mA values1 scores3 kmB
                qmA max2 values2 max3 rows0 lastadd values3 nmB otB rows1 lastout kmA"""
        ORDER = ORDER.split()
        HALF = G // 2
        OB = 2 if G == 8 else 1

        stage = ExitStack()
        block = stage.enter_context(nc.Block())

        @block.sync
        def _(sp):
            if diff:
                sp.dma_start(X[:, 0:4, :], d["x"][0:4].rearrange("b t c -> t b c")).then_inc(x_first, 16)
            sp.dma_start(wT[:, :, :], d["w"]).then_inc(w_in, 16)
            sp.dma_start(qkb[:, :], d["qkb"]).then_inc(w_in, 16)
            sp.dma_start(rows[:, :, :], d["rows"]).then_inc(w_in, 16)
            sp.dma_start(mask[:, :], d["mask"]).then_inc(w_in, 16)
            sp.dma_start(sel[:, :, :], d["sel"]).then_inc(w_in, 16)
            if causal:
                sp.dma_start(cm[:, :, :, :], d["cm"]).then_inc(w_in, 16)
                sp.dma_start(gb[:, :, :], d["gb"].partition_broadcast(P)).then_inc(w_in, 16)
            if diff:
                for n in range(4):
                    sp.dma_start(lq[:, n, :], d["lam"][n].partition_broadcast(P)).then_inc(w_in, 16)
                sp.dma_start(X[:, 4:NB, :], d["x"][4:NB].rearrange("b t c -> t b c")).then_inc(x_rest, 16)

            def slot(i, u):
                n = 2 * i + u
                after(sp, src_transposed, n - 1)
                sp.dma_start(cx[0:S, u, :], d["ctx"][n]).then_inc(ctx_in[u], 16)

            if not causal:
                pairs(sp, slot, NB)

        @block.gpsimd
        def _(pool):
            chain = Chain(pool, pool_chain)
            HEAD, TAIL = 3, 1 if norm else 0

            def head_rstd(n, u):
                pool.wait_ge(stats_ready, n + 1)
                chain.link(nc.gpsimd.tensor_tensor(veps[:, :], mv[:, u, 1:2], env.eps[:, :], ALU.add))
                nc.gpsimd.tensor_tensor(rstd[:, u:u + 1], veps[:, :], env.minus_half[:, :],
                                        ALU.pow).then_inc(rstd_ready, 1)

            def keep(n, u):
                pool.wait_ge(xn_ready, n + 1)
                nc.gpsimd.tensor_tensor(H[:, n, :], xn[:, u, :], env.zero[:, 0:1].to_broadcast([P, P]),
                                        ALU.add).then_inc(xn_kept, 1)

            def split(n, u):
                pool.wait_ge(qk_ready, n + 1)
                chain.link(nc.gpsimd.tensor_tensor(parts[:, u, 0, :], QK[:, :], env.zero[:, 0:1].to_broadcast([P, S + P]),
                                                  ALU.add))
                chain.link(nc.gpsimd.tensor_tensor(rest[:, :], QK[:, :], parts[:, u, 0, :], ALU.subtract))
                nc.gpsimd.tensor_tensor(parts[:, u, 1, :], rest[:, :], env.zero[:, 0:1].to_broadcast([P, S + P]),
                                        ALU.add).then_inc(parts_ready, 1)
                pool.wait_ge(parts_ready, 2 * n + 1)
                nc.gpsimd.tensor_tensor(parts[:, u, 2, :], rest[:, :], parts[:, u, 1, :],
                                        ALU.subtract).then_inc(parts_ready, 1)

            def tail_rstd(b):
                pool.wait_ge(stats2_ready, b + 1)
                chain.link(nc.gpsimd.tensor_tensor(veps2[:, :], mv2[:, 1:2], env.eps[:, :], ALU.add))
                nc.gpsimd.tensor_tensor(rstd2[:, :], veps2[:, :], env.minus_half[:, :],
                                        ALU.pow).then_inc(rstd2_ready, 1)

            pool.wait_ge(w_in, 16 * n_w)
            chain.slot(0)
            for n in range(2):
                head_rstd(n, n)
                if causal:
                    keep(n, n)
                split(n, n)

            def slot(i, u):
                b = 2 * i + u
                first = isinstance(b, int) and b == 0
                last = isinstance(b, int) and b >= NB - 2
                end = isinstance(b, int) and b >= NB - 1
                chain.slot(HEAD * 2 if first else
                           (HEAD * NB if end else HEAD * (b + 2)) + TAIL * (b - 1))
                for step in ORDER:
                    if step == "stats" and not last:
                        head_rstd(b + 2, u)
                    if step == "norm" and not last and causal:
                        keep(b + 2, u)
                    if step == "qk" and not last:
                        split(b + 2, u)
                    if step == "lastadd" and norm and not first:
                        tail_rstd(b - 1)

            pairs(pool, slot, NB)
            if norm:
                tail_rstd(NB - 1)

        @block.scalar
        def _(act):
            def head_src(n, u):
                act.wait_ge(src_transposed, n + 1)
                nc.scalar.activation(srcT[:, u, :], psH[:, 0:WS], ACT.Copy).then_inc(srcT_ready, 1)

            def head_qk(n):
                act.wait_ge(qk_projected, n + 1)
                after(act, parts_ready, 2 * n)
                nc.scalar.activation(QK[:, 0:S], psH[:, P:P + S], ACT.Identity, bias=qkb[:, 1:2])
                nc.scalar.activation(QK[:, S:S + P], psH[:, 0:P], ACT.Identity, bias=qbs[:, 0:1],
                                     scale=SCALE).then_inc(qk_ready, 1)

            def head_v(n, u):
                act.wait_ge(v_projected, n + 1)
                nc.scalar.activation(Va[0:S, u, :, 0:HD], psH[0:S, 0:P].rearrange("s (h e) -> s h e", e=HD),
                                     ACT.Copy).then_inc(v_ready, 1)

            def head_rows(n, u, y):
                act.wait_ge(rows_full, 4 * n + y + 1)
                if y % 2 == 0:
                    after(act, qm_ready, 2 * n - 3 + y // 2)
                nc.scalar.activation(Kr[0:KR, u, 2 * y:2 * y + 2, :],
                                     psX[0:KR, 0:2 * S].rearrange("r (x s) -> r x s", x=2), ACT.Copy)
                nc.scalar.activation(Qr[0:KR, u, 2 * y:2 * y + 2, :],
                                     psX[0:KR, 2 * S:2 * S + 2 * P].rearrange("r (x t) -> r x t", x=2),
                                     ACT.Copy).then_inc(rows_ready, 1)

            def head_m(n, u, half):
                act.wait_ge(m_transposed, 2 * n + half + 1)
                nc.scalar.activation(Qr[KR:P, u, 4 * half:4 * half + 4:R, :],
                                     psH[KR:P, 0:HALF * P].rearrange("r (g t) -> r g t", g=HALF),
                                     ACT.Copy).then_inc(m_rows_ready, 1)

            def exps(b, g):
                n = b * G + g
                act.wait_ge(b_full, n + 1)
                after(act, pv_done, n - 3)
                nc.scalar.activation(E[0:S, g % 4, :], psB[0:S, g % 2, :], ACT.Exp).then_inc(e_ready, 1)

            def tail_OT(b, u, k):
                act.wait_ge(pv_done, b * G + (k + 1) * (G // OB))
                bank = k if OB == 2 else u
                nc.scalar.activation(OTs[:, BANK * k:BANK * k + BANK], psO[:, bank, :],
                                     ACT.Copy).then_inc(ot_ready, 1)

            if diff:
                act.wait_ge(lam_dots, 1)
                nc.scalar.activation(le[:, :], ld[:, :], ACT.Exp).then_inc(lam_exp, 1)
            act.wait_ge(setup_done, 1)
            for n in range(2):
                head_src(n, n)
                head_qk(n)
                if n == 0:
                    head_v(0, 0)
            for y in range(6):
                head_rows(y // 4, y // 4, y % 4)
            head_m(0, 0, 0)

            def slot(i, u):
                b = 2 * i + u
                last = isinstance(b, int) and b >= NB - 2
                end = isinstance(b, int) and b >= NB - 1
                for step in ORDER:
                    if step[:6] == "scores":
                        exps(b, int(step[6:]))
                    if step == "mB":
                        head_m(b, u, 1)
                    if step == "otA":
                        tail_OT(b, u, 0)
                    if step == "otB":
                        tail_OT(b, u, OB - 1)
                    if step == "source" and not last:
                        head_src(b + 2, u)
                    if step == "qk" and not last:
                        head_qk(b + 2)
                    if step in ("rows2", "rows3") and not end:
                        head_rows(b + 1, 1 - u, int(step[4:]))
                    if step in ("rows0", "rows1") and not last:
                        head_rows(b + 2, u, int(step[4:]))
                    if step == "v" and not end:
                        head_v(b + 1, 1 - u)
                    if step == "mA" and not end:
                        head_m(b + 1, 1 - u, 0)

            pairs(act, slot, NB)

        @block.vector
        def _(dve):
            chain = Chain(dve, dve_chain)

            def head_stats(n, u):
                chain.link(nc.vector.bn_stats(stats[:, :], X[:, n, :]))
                apart(nc, env)
                nc.vector.bn_aggr(mv[:, u, :], stats[:, :]).then_inc(stats_ready, 1)

            def head_norm(n, u):
                dve.wait_ge(rstd_ready, n + 1)
                after(dve, src_transposed, n - 1)
                if causal:
                    after(dve, xn_kept, n - 1)
                nc.vector.tensor_scalar(xn[:, u, :], X[:, n, :], mv[:, u, 0:1], rstd[:, u:u + 1],
                                        ALU.subtract, ALU.mult).then_inc(xn_ready, 1)

            def head_km(n, u, half):
                dve.wait_ge(rows_ready, 4 * n + 2 * half + 2)
                x = 4 * half
                for j in range(4):
                    mm = nc.vector.tensor_scalar(Km[0:KR, x:x + 4, j, :], Kr[0:KR, u, x:x + 4, :],
                                                 mask[0:KR, j:j + 1], None, ALU.mult)
                mm.then_inc(km_ready, 1)

            def head_max(n, g):
                dve.wait_ge(a_full, n * G + g + 1)
                nc.vector.tensor_reduce(M[:, 4 * g:4 * g + 4],
                                        psA[:, g % 2, 0:4 * S].rearrange("t (j s) -> t j s", j=4),
                                        AX.X, ALU.max).then_inc(a_free, 1)

            def head_nm(n, half):
                dve.wait_ge(a_free, n * G + (half + 1) * HALF)
                mine = slice(half * HALF, half * HALF + HALF)
                m4 = M[:, :].rearrange("t (g j) -> t g j", j=4)[:, mine, :]
                r4 = Mr[:, :].rearrange("t (g j) -> t g j", j=4)[:, mine, :]
                chain.link(nc.vector.tensor_scalar(nM[:, mine, 0:4], m4, -1.0, None, ALU.mult))
                chain.link(nc.vector.scalar_tensor_tensor(r4, m4, -1.0, nM[:, mine, 0:4], ALU.mult, ALU.subtract))
                chain.link(nc.vector.tensor_copy(nM[:, mine, 4:8], r4))
                nc.vector.tensor_tensor(nM[:, mine, 8:12], r4, nM[:, mine, 4:8],
                                        ALU.subtract).then_inc(nm_ready, 1)

            def head_qm(n, u, half):
                dve.wait_ge(m_rows_ready, 2 * n + half + 1)
                after(dve, b_full, (n - 1) * G + (half + 1) * HALF)
                x = 4 * half
                for j in range(4):
                    mm = nc.vector.tensor_scalar(Qm[:, x:x + 4, j, :], Qr[:, u, x:x + 4, :],
                                                 mask[:, j:j + 1], None, ALU.mult)
                mm.then_inc(qm_ready, 1)

            def tail_att(b, u, k):
                dve.wait_ge(back_done, OB * b + k + 1)
                N = NS // OB
                mine = slice(k * N, k * N + N)
                O = psO[:, k if OB == 2 else u, :].rearrange("t (n e) -> t n e", e=QUAD)
                chain.link(nc.vector.reciprocal(rec[:, mine], O[:, :, HD]))
                to = pv[:, mine, :] if diff else att[:, :].rearrange("t (n e) -> t n e", e=HD)
                ins = nc.vector.tensor_tensor(to, O[:, :, 0:HD],
                                              rec[:, mine].unsqueeze(2).to_broadcast([P, N, HD]), ALU.mult)
                if diff:
                    chain.link(ins)
                    two = pv[:, mine, :].rearrange("t (q k j) e -> t q k (j e)", q=2, k=2)
                    ins = nc.vector.scalar_tensor_tensor(
                        att[:, k * (P // 2):(k + 1) * (P // 2)].rearrange("t (q m) -> t q m", q=2),
                        two[:, :, 1, :], nlam[:, 0:1], two[:, :, 0, :], ALU.mult, ALU.add)
                ins.then_inc(att_ready, 1)

            def tail_attT(b, u):
                dve.wait_ge(att_transposed, b + 1)
                nc.vector.tensor_scalar(attT[:, :], psO[:, 1 if OB == 2 else u, 0:P],
                                        (1.0 - LAMBDA_INIT) if diff else 1.0,
                                        None, ALU.mult).then_inc(attT_ready, 1)

            def tail_add(b, u):
                dve.wait_ge(y_ready, b + 1)
                y = psO[:, 1 if OB == 2 else u, P:2 * P]
                if causal:
                    dve.wait_ge(xn_kept, b + 1)
                    base, to = H[:, b, :], z[:, :]
                else:
                    base = to = X[:, b, :]
                nc.vector.tensor_tensor(to, base, y, ALU.add).then_inc(x_done, 1)
                if not norm:
                    return
                dve.wait_ge(x_done, b + 1)
                if not causal:
                    apart(nc, env)
                chain.link(nc.vector.bn_stats(stats2[:, :], to))
                apart(nc, env)
                nc.vector.bn_aggr(mv2[:, :], stats2[:, :]).then_inc(stats2_ready, 1)

            def tail_out(b):
                if not norm:
                    return
                dve.wait_ge(rstd2_ready, b + 1)
                base, to = (z[:, :], z[:, :]) if causal else (X[:, b, :], H[:, b, :])
                chain.link(nc.vector.tensor_scalar(to, base, mv2[:, 0:1], rstd2[:, 0:1],
                                                   ALU.subtract, ALU.mult))
                if causal:
                    chain.link(nc.vector.tensor_tensor(z[:, :], z[:, :], gb[:, 0, :], ALU.mult))
                    chain.link(nc.vector.tensor_tensor(H[:, b, :], z[:, :], gb[:, 1, :], ALU.add))

            dve.wait_ge(w_in, 16 * n_w)
            chain.slot(0)
            nc.vector.memset(Kr[KR:P, :, :, :], 1.0)
            nc.vector.memset(Qr[KR:P, :, :, :], 0.0)
            nc.vector.memset(nM[:, :, :], 0.0)
            chain.link(nc.vector.memset(Va[:, :, :, :], 0.0))
            chain.link(nc.vector.memset(Va[:, :, :, HD:HD + 1], 1.0))
            if diff:
                for n in range(2):
                    chain.link(nc.vector.tensor_tensor(lp[:, n, :], lq[:, 2 * n, :], lq[:, 2 * n + 1, :], ALU.mult))
                nc.vector.tensor_reduce(ld[:, :], lp[:, :, :], AX.X, ALU.add).then_inc(lam_dots, 1)
                dve.wait_ge(lam_exp, 1)
                chain.link(nc.vector.tensor_tensor(nlam[:, :], le[:, 1:2], le[:, 0:1], ALU.subtract))
                chain.link(nc.vector.tensor_scalar(nlam[:, :], nlam[:, :], -LAMBDA_INIT, None, ALU.add))
            nc.vector.tensor_scalar(qbs[:, :], qkb[:, 0:1], SCALE, None, ALU.mult).then_inc(setup_done, 1)
            if diff:
                dve.wait_ge(x_first, 16)
            for n in range(2):
                head_stats(n, n)
                head_norm(n, n)
            head_km(0, 0, 0)
            head_km(0, 0, 1)
            for g in range(G):
                head_max(0, g)
            head_nm(0, 0)
            head_qm(0, 0, 0)
            head_km(1, 1, 0)
            head_nm(0, 1)
            SETUP = chain.n
            LINKS = [None, None]

            def slot(i, u):
                b = 2 * i + u
                first = isinstance(b, int) and b == 0
                last = isinstance(b, int) and b >= NB - 2
                end = isinstance(b, int) and b >= NB - 1
                if first:
                    chain.slot(SETUP)
                    if diff:
                        dve.wait_ge(x_rest, 16)
                else:
                    chain.slot(SETUP + LINKS[0] + (LINKS[1] or 0) * (b - 1) - (1 if end else 0))
                for step in ORDER:
                    if step == "qmB":
                        head_qm(b, u, 1)
                    if step == "kmA" and not last:
                        head_km(b + 2, u, 0)
                    if step == "attA":
                        tail_att(b, u, 0)
                    if step == "stats" and not last:
                        head_stats(b + 2, u)
                    if step == "norm" and not last:
                        head_norm(b + 2, u)
                    if step == "lastatt" and not first:
                        tail_att(b - 1, 1 - u, OB - 1)
                    if step == "lastattT" and not first:
                        tail_attT(b - 1, 1 - u)
                    if step == "lastadd" and not first:
                        tail_add(b - 1, 1 - u)
                    if step == "lastout" and not first:
                        tail_out(b - 1)
                    if end:
                        continue
                    if step == "kmB":
                        head_km(b + 1, 1 - u, 1)
                    if step[:3] == "max":
                        head_max(b + 1, int(step[3:]))
                    if step[:2] == "nm":
                        head_nm(b + 1, "AB".index(step[2]))
                    if step == "qmA":
                        head_qm(b + 1, 1 - u, 0)
                if first:
                    LINKS[0] = chain.n
                elif LINKS[1] is None:
                    LINKS[1] = chain.n

            pairs(dve, slot, NB)
            tail_att(NB - 1, 1, OB - 1)
            tail_attT(NB - 1, 1)
            tail_add(NB - 1, 1)
            tail_out(NB - 1)

        @block.tensor
        def _(pe):
            def head_source(n, h, u):
                pe.wait_ge(xn_ready, n + 1)
                after(pe, v_ready, n)
                mm = nc.tensor.transpose(psH[:, 0:P], xn[:, u, :], ident[:, :])
                if not causal:
                    pe.wait_ge(ctx_in[u], 16 * (h + 1))
                    mm = nc.tensor.transpose(psH[:, P:P + S], cx[0:S, u, :], ident[0:S, 0:S])
                mm.then_inc(src_transposed, 1)

            def head_qk(n, u):
                pe.wait_ge(srcT_ready, n + 1)
                nc.tensor.matmul(psH[:, 0:P], wT[:, 0, :], srcT[:, u, 0:P], start=True, stop=True)
                nc.tensor.matmul(psH[:, P:P + S], wT[:, 1, :], srcT[:, u, kv:kv + S], start=True,
                                 stop=True).then_inc(qk_projected, 1)

            def head_v(n, u):
                setup = isinstance(n, int) and n == 0
                pe.wait_ge(qk_ready, 1) if setup else pe.wait_ge(m_rows_ready, 2 * n)
                nc.tensor.matmul(psH[0:S, 0:P], srcT[:, u, kv:kv + S], wT[:, 2, :], start=True, stop=False)
                nc.tensor.matmul(psH[0:S, 0:P], rows[0:1, 2, 0:S], rows[0:1, 0, :], start=False,
                                 stop=True).then_inc(v_projected, 1)

            at = [0]
            place = {}
            for x in range(NX):
                for side in range(2):
                    for part in use[x][side]:
                        place[x, side, part] = at[0]
                        at[0] += 1

            def head_rows(n, u, y):
                pe.wait_ge(parts_ready, 2 * (n + 1))
                after(pe, rows_ready, 4 * n + y)
                for x in (2 * y, 2 * y + 1):
                    for side, lo, w, o in ((0, 0, S, (x % 2) * S), (1, S, P, 2 * S + (x % 2) * P)):
                        mine = use[x][side]
                        for part in mine:
                            mm = nc.tensor.matmul(psX[0:KR, o:o + w], sel[:, place[x, side, part], :],
                                                  parts[:, u, part, lo:lo + w], start=(part == mine[0]),
                                                  stop=(part == mine[-1]))
                mm.then_inc(rows_full, 1)

            def head_max(n, u, g):
                pe.wait_ge(km_ready, 2 * n + g // HALF + 1)
                after(pe, a_free, n * G + g - 1)
                for r in range(R):
                    x = g * R + r
                    mm = nc.tensor.matmul(psA[:, g % 2, 0:4 * S], Qr[0:KR, u, x, :], Km[0:KR, x, :, :],
                                          start=(r == 0), stop=(r == R - 1 and not causal))
                if causal:
                    mm = nc.tensor.matmul(psA[:, g % 2, :], identb[:, :], cm[:, 0, :, :], start=False, stop=True)
                mm.then_inc(a_full, 1)

            def head_m(n, half, final=False):
                pe.wait_ge(nm_ready, 2 * n + half + 1)
                if half:
                    pe.wait_ge(m_rows_ready, 2 * n + 1)
                elif final:
                    pe.wait_ge(v_ready, n + 1)
                else:
                    pe.wait_ge(qk_ready, n + 2)
                for g in range(HALF):
                    mm = nc.tensor.matmul(psH[KR:P, g * P:g * P + P], nM[:, HALF * half + g, :], identb[:, :],
                                          start=True, stop=True)
                mm.then_inc(m_transposed, 1)

            def scores(b, u, g):
                pe.wait_ge(qm_ready, 2 * b + g // HALF + 1)
                after(pe, e_ready, b * G + g - 1)
                for r in range(R):
                    x = g * R + r
                    mm = nc.tensor.matmul(psB[0:S, g % 2, :], Kr[:, u, x, :], Qm[:, x, :, :],
                                          start=(r == 0), stop=(r == R - 1 and not causal))
                if causal:
                    mm = nc.tensor.matmul(psB[0:S, g % 2, :], identb[:, :], cm[:, 1, :, :], start=False, stop=True)
                mm.then_inc(b_full, 1)

            def values(b, u, g):
                pe.wait_ge(e_ready, b * G + g + 1)
                if OB == 2 and g == 0:
                    after(pe, att_ready, 2 * b - 1)
                if g == (G // 2 if OB == 2 else 0):
                    after(pe, x_done, b if OB == 2 else b - 1)
                per = 4 * HEADS // NS
                w = 4 * P // per
                bank = g // 4 if OB == 2 else u
                for k in range(per):
                    h = g * per + k
                    j, o = h % 4, (h // 4) * w % BANK
                    mm = nc.tensor.matmul(psO[QUAD * j:QUAD * j + QUAD, bank, o:o + w], Va[0:S, u, h, :],
                                          E[0:S, g % 4, k * w:k * w + w], start=True, stop=True)
                mm.then_inc(pv_done, 1)

            def back(b, u, k):
                pe.wait_ge(ot_ready, OB * b + k + 1)
                bank = k if OB == 2 else u
                for q in range(4):
                    mm = nc.tensor.transpose(psO[:, bank, P * q:P * q + P],
                                             OTs[:, BANK * k + P * q:BANK * k + P * q + P], ident[:, :])
                mm.then_inc(back_done, 1)

            def turn_att(b, u):
                pe.wait_ge(att_ready, OB * (b + 1))
                nc.tensor.transpose(psO[:, 1 if OB == 2 else u, 0:P], att[:, :],
                                    ident[:, :]).then_inc(att_transposed, 1)

            def project_out(b, u):
                pe.wait_ge(attT_ready, b + 1)
                y = psO[:, 1 if OB == 2 else u, P:2 * P]
                nc.tensor.matmul(y, attT[:, :], wT[:, 3, :], start=True, stop=False)
                nc.tensor.matmul(y, rows[0:1, 2, :], rows[0:1, 1, :], start=False, stop=True).then_inc(y_ready, 1)

            pe.wait_ge(w_in, 16 * n_w)
            pe.wait_ge(setup_done, 1)
            for n in range(2):
                head_source(n, 0, n)
                head_qk(n, n)
                if n == 0:
                    head_v(0, 0)
            for y in range(6):
                head_rows(y // 4, y // 4, y % 4)
            for g in range(G):
                head_max(0, 0, g)
            head_m(0, 0)

            def slot(i, u):
                b = 2 * i + u
                first = isinstance(b, int) and b == 0
                last = isinstance(b, int) and b >= NB - 2
                end = isinstance(b, int) and b >= NB - 1
                for step in ORDER:
                    if step[:6] == "scores":
                        scores(b, u, int(step[6:]))
                    if step[:6] == "values":
                        values(b, u, int(step[6:]))
                    if step == "mB":
                        head_m(b, 1)
                    if step == "backA":
                        back(b, u, 0)
                    if step == "lastback" and not first:
                        back(b - 1, 1 - u, OB - 1)
                    if step == "lastturn" and not first:
                        turn_att(b - 1, 1 - u)
                    if step == "lastproj" and not first:
                        project_out(b - 1, 1 - u)
                    if step == "source" and not last:
                        head_source(b + 2, i + 1, u)
                    if step == "qk" and not last:
                        head_qk(b + 2, u)
                    if step in ("rows2", "rows3") and not end:
                        head_rows(b + 1, 1 - u, int(step[4:]))
                    if step in ("rows0", "rows1") and not last:
                        head_rows(b + 2, u, int(step[4:]))
                    if step == "v" and not end:
                        head_v(b + 1, 1 - u)
                    if step[:3] == "max" and not end:
                        head_max(b + 1, 1 - u, int(step[3:]))
                    if step == "mA" and not end:
                        head_m(b + 1, 0, last)

            pairs(pe, slot, NB)
            back(NB - 1, 1, OB - 1)
            turn_att(NB - 1, 1)
            project_out(NB - 1, 1)

        stage.close()
        clear(nc, sems)


def mixture(nc, env, tag, E, L, d):
    X, H, ident = env.X, env.H, env.ident
    post = L == 1
    NCH = env.NB // CB
    K = L * NCH
    FT = 4
    HI, LO = 0, 1
    W1, W2 = 0, 1
    GELU = ACT.Gelu_apprx_tanh if post else ACT.Gelu
    AT = dict(x=1, logits=2, xh=None, gates=5) if post else dict(x=0, logits=1, xh=2, gates=3)
    TANH_AT = AT["logits"] + 1
    STAGED = (L - 1) * NCH // 2
    assert post or NCH // 2 == E

    with ExitStack() as ctx:
        def sb(name, shape, dt=F32):
            return ctx.enter_context(nc.sbuf_tensor(f"{tag}_{name}", shape, dt))

        def ps(name, shape):
            return ctx.enter_context(nc.psum_tensor(f"{tag}_{name}", shape, F32))

        sems = []

        def sem(name):
            sems.append(ctx.enter_context(nc.semaphore(f"{tag}_{name}")))
            return sems[-1]

        raw = sb("raw", [P, 2, 2, FT * P])
        ws = sb("ws", [P, E, 2, 2, FT * P], F32R)
        b1 = sb("b1", [P, L * E * FT])
        b2 = sb("b2", [P, L * E])
        rw = sb("rw", [P, L * E])
        rank = sb("rank", [P, E])
        sel32 = sb("sel32", [2 * E, E, P])
        sel = sb("sel", [2 * E, E, P], F32R)
        xs = sb("xs", [P, 2, CB, P])
        xT = sb("xT", [P, 2, CT])
        xe = sb("xe", [P, 2, 2, CT], F32R)
        lg = sb("lg", [P, CB, E])
        l2 = sb("l2", [P, CB, E])
        t1 = sb("t1", [P, CB, E])
        k1 = sb("k1", [P, CB, E])
        k2 = sb("k2", [P, CB, E])
        m1 = sb("m1", [P, CB])
        m2 = sb("m2", [P, CB])
        r1 = sb("r1", [P, CB])
        gap = sb("gap", [P, CB])
        th = sb("th", [P, CB])
        wa = sb("wa", [P, CB])
        wb = sb("wb", [P, CB])
        sw = sb("sw", [P, 2, CB])
        comb = sb("comb", [P, CB, E])
        combp = sb("combp", [P, CB, 2 * E], F32R)
        gT = sb("gT", [2 * E, 2, CT], F32R)
        h32 = sb("h32", [P, FT, CT])
        hp = sb("hp", [P, 2, 2, FT, CT], F32R)
        gs = sb("gs", [P, 2, CT])
        yg = sb("yg", [P, 2, CT])
        yT = sb("yT", [P, 2, CT])
        st = sb("st", [P, CB, 6])
        mv = sb("mv", [P, CB, 2])
        veps = sb("veps", [P, CB])
        rstd = sb("rstd", [P, CB])
        if post:
            z = sb("z", [P, CB, P])
            gb = sb("gb", [P, 2, P])
        else:
            staged = sb("staged", [P, E, 2, 2, FT * P], F32R)
            lng = sb("lng", [P, L * E])
            lnb = sb("lnb", [P, L * E])
            rb = sb("rb", [P, L * E])
            xh = sb("xh", [P, CB, P])
            xhT = sb("xhT", [P, 2, CT])
            xe32 = sb("xe32", [P, 2, CT])
            mark = sb("mark", [P, NCH])

        psR = ps("psR", [P, FT, BANK])
        psG = ps("psG", [P, BANK])
        psY = ps("psY", [P, 2, BANK])
        psH = ps("psH", [P, BANK])

        c_in = sem("c_in")
        raw_in = [sem("raw_in0"), sem("raw_in1")]
        raw_split = sem("raw_split")
        w_in = [sem(f"w_in{e}") for e in range(E)]
        xs_in = [sem("xs_in0"), sem("xs_in1")]
        stats_ready = sem("stats_ready")
        rstd_ready = sem("rstd_ready")
        xh_ready = sem("xh_ready")
        x_transposed = sem("x_transposed")
        xT_ready = sem("xT_ready")
        logits_full = sem("logits_full")
        logits_read = sem("logits_read")
        gap_ready = sem("gap_ready")
        tanh_ready = sem("tanh_ready")
        comb_ready = sem("comb_ready")
        xh_transposed = sem("xh_transposed")
        xhT_ready = sem("xhT_ready")
        g_transposed = sem("g_transposed")
        gT_ready = sem("gT_ready")
        xhi_ready = sem("xhi_ready")
        xe_ready = sem("xe_ready")
        r_full = sem("r_full")
        h_ready = sem("h_ready")
        hlo_ready = sem("hlo_ready")
        expert_done = sem("expert_done")
        g_full = sem("g_full")
        gs_ready = sem("gs_ready")
        yg_ready = sem("yg_ready")
        y_summed = sem("y_summed")
        z_full = sem("z_full")
        z_read = sem("z_read")
        x_done = sem("x_done")
        dve_chain = sem("dve_chain")
        pool_chain = sem("pool_chain")
        sum_ready = sem("sum_ready")
        out_written = sem("out_written")
        if not post:
            next_in = [sem("next_in0"), sem("next_in1")]
            next_hi = sem("next_hi")
            next_split = sem("next_split")
        n_c = 5 + (1 if post else 3)

        stage = ExitStack()
        block = stage.enter_context(nc.Block())

        def weights(l, e, which):
            w = d["w1" if which == W1 else "w2"][l * E + e]
            return w if which == W1 else w.rearrange("(t p) m -> p t m", p=P)

        def as_loaded(tile, which):
            return tile if which == W1 else tile.rearrange("p (t m) -> p t m", t=FT)

        @block.sync
        def _(sp):
            for e in range(E):
                after(sp, raw_split, 2 * (e - 1))
                for which in (W1, W2):
                    sp.dma_start(as_loaded(raw[:, e % 2, which, :], which),
                                 weights(0, e, which)).then_inc(raw_in[e % 2], 16)
                if e == 0:
                    sp.dma_start(rw[:, :], d["rw"]).then_inc(c_in, 16)
                    sp.dma_start(rank[:, :], d["rank"]).then_inc(c_in, 16)
                    sp.dma_start(b1[:, :], d["b1"]).then_inc(c_in, 16)
                    sp.dma_start(b2[:, :], d["b2"]).then_inc(c_in, 16)
                    sp.dma_start(sel32[:, :, :], d["sel"]).then_inc(c_in, 16)
                    if post:
                        sp.dma_start(gb[:, :, :], d["gb"].partition_broadcast(P)).then_inc(c_in, 16)
                    else:
                        sp.dma_start(lng[:, :], d["lng"]).then_inc(c_in, 16)
                        sp.dma_start(lnb[:, :], d["lnb"]).then_inc(c_in, 16)
                        sp.dma_start(rb[:, :], d["rb"].partition_broadcast(P)).then_inc(c_in, 16)
            if L > 1:
                for l in range(1, L):
                    for e in range(E):
                        n = (l - 1) * E + e
                        if n == 0:
                            sp.wait_ge(raw_split, 2 * E)
                        for which in (W1, W2):
                            after(sp, next_split, 2 * (n - 1) + which + 1)
                            sp.dma_start(as_loaded(raw[:, 0, which, :], which),
                                         weights(l, e, which)).then_inc(next_in[which], 16)
                    for e in range(E):
                        sp.wait_ge(next_split, 2 * ((l - 1) * E + e + 1))
                        sp.wait_ge(expert_done, (l * NCH - 1) * E + e + 1)
                        sp.dma_start(ws[:, e, :, :, :].bitcast(F32),
                                     staged[:, e, :, :, :].bitcast(F32)).then_inc(w_in[e], 16)
                for c in range(NCH):
                    sp.wait_ge(sum_ready, c + 1)
                    sp.dma_start(d["out"][CB * c:CB * c + CB].rearrange("b t m -> t b m"),
                                 X[:, CB * c:CB * c + CB, :]).then_inc(out_written, 16)
                sp.wait_ge(out_written, 16 * NCH)

        @block.gpsimd
        def _(pool):
            chain = Chain(pool, pool_chain)

            def load_source(n, u):
                after(pool, x_transposed, n - 1)
                if not post:
                    pool.wait_ge(x_done, n + 1)
                c = n % NCH
                pool.dma_start(xs[:, u, :, :], H[:, bass.ds(CB * c, CB), :]).then_inc(xs_in[u], 16)

            def rstds(n):
                pool.wait_ge(stats_ready, n + 1)
                chain.link(nc.gpsimd.tensor_tensor(veps[:, :], mv[:, :, 1],
                                                   env.eps[:, 0:1].to_broadcast([P, CB]), ALU.add))
                nc.gpsimd.tensor_tensor(rstd[:, :], veps[:, :], env.minus_half[:, 0:1].to_broadcast([P, CB]),
                                        ALU.pow).then_inc(rstd_ready, 1)

            def input_low(k, e):
                if post:
                    return
                g = k * E + e
                pool.wait_ge(xhi_ready, g + 1)
                nc.gpsimd.tensor_tensor(xe[:, e % 2, LO, :], xe32[:, e % 2, :], xe[:, e % 2, HI, :],
                                        ALU.subtract).then_inc(xe_ready, 1)

            def add_expert(k, u, e):
                pool.wait_ge(yg_ready, k * E + e + 1)
                if e > 1:
                    pool.wait_ge(y_summed, k * (E - 1) + e - 1)
                nc.gpsimd.tensor_tensor(yT[:, u, :], yT[:, u, :], yg[:, e % 2, :], ALU.add).then_inc(y_summed, 1)

            def split_next(i, u):
                l = i // E
                pool.wait_ge(next_in[u], 16 * (i + 1))
                pool.wait_ge(r_full, FT * E * (NCH * l + 1))
                e = i % E
                part = lambda n: staged[:, bass.ds(e, 1), u, n, :].rearrange("p o m -> p (o m)")
                nc.gpsimd.tensor_tensor(part(HI), raw[:, 0, u, :], env.zero[:, 0:1].to_broadcast([P, FT * P]),
                                        ALU.add).then_inc(next_hi, 1)
                pool.wait_ge(next_hi, 2 * i + u + 1)
                nc.gpsimd.tensor_tensor(part(LO), raw[:, 0, u, :], part(HI),
                                        ALU.subtract).then_inc(next_split, 1)

            def add_residual(c):
                pool.wait_ge(x_done, L * NCH + c + 1)
                nc.gpsimd.tensor_tensor(X[:, CB * c:CB * c + CB, :], X[:, CB * c:CB * c + CB, :],
                                        H[:, CB * c:CB * c + CB, :], ALU.add).then_inc(sum_ready, 1)

            load_source(0, 0)
            load_source(1, 1)
            chain.slot(0)
            if not post:
                rstds(0)
            input_low(0, 0)
            input_low(0, 1)

            def slot(i, u, split=False):
                k = 2 * i + u
                first = isinstance(k, int) and k == 0
                last = isinstance(k, int) and k >= K - 2
                end = isinstance(k, int) and k >= K - 1
                chain.slot((max(k - 1, 0) if isinstance(k, int) else k - 1) if post else k + 1)
                for e in range(E):
                    if e == E - 1 and not end:
                        input_low(k + 1, 0)
                        input_low(k + 1, 1)
                    if e + 2 < E:
                        input_low(k, e + 2)
                    if e == 0 and not first:
                        add_expert(k - 1, 1 - u, E - 1)
                    if e == 0 and not post and not end:
                        rstds(k + 1)
                    if e == 1 and post and not first:
                        rstds(k - 1)
                    if e >= 2:
                        add_expert(k, u, e - 1)
                    if e == AT["x"] + 1 and not last:
                        load_source(k + 2, u)
                    if e == 2 and split:
                        split_next(i, u)
                if not post and last:
                    for c in range(0 if not end else NCH - 3, NCH - 3 if not end else NCH - 2):
                        add_residual(c)

            if post:
                pairs(pool, slot, K)
            else:
                slot(0, 0, True)
                slot(0, 1, True)
                with pool.Fori(1, STAGED) as i:
                    slot(i, 0, True)
                    slot(i, 1, True)
                with pool.Fori(STAGED, K // 2 - 1) as i:
                    slot(i, 0)
                    slot(i, 1)
                slot(K // 2 - 1, 0)
                slot(K // 2 - 1, 1)
            add_expert(K - 1, 1, E - 1)
            if not post:
                for c in range(NCH - 2, NCH):
                    add_residual(c)
            else:
                chain.slot(K - 1)
                rstds(K - 1)

        @block.scalar
        def _(act):
            def head_xT(n, u):
                act.wait_ge(x_transposed, n + 1)
                nc.scalar.activation(xT[:, u, :], psH[:, :], ACT.Copy).then_inc(xT_ready, 1)

            def head_tanh(n):
                act.wait_ge(gap_ready, n + 1)
                nc.scalar.activation(th[:, :], gap[:, :], ACT.Tanh, scale=0.5).then_inc(tanh_ready, 1)

            def head_xhT(n, u):
                act.wait_ge(xh_transposed, n + 1)
                nc.scalar.activation(xhT[:, u, :], psH[:, :], ACT.Copy).then_inc(xhT_ready, 1)

            def gelus(k, e):
                g = k * E + e
                l = k // NCH if L > 1 else 0
                after(act, expert_done, g - 1)
                for f in range(FT):
                    bias = b1[:, bass.ds((l * E + e) * FT + f, 1)]
                    act.wait_ge(r_full, FT * g + f + 1)
                    after(act, hlo_ready, FT * (g - 1) + f + 1)
                    nc.scalar.activation(h32[:, f, :], psR[:, f, :], GELU, bias=bias)
                    nc.scalar.activation(hp[:, e % 2, HI, f, :], psR[:, f, :], GELU,
                                         bias=bias).then_inc(h_ready, 1)

            def gates(g, b):
                act.wait_ge(g_full, g + 1)
                after(act, yg_ready, g - 1)
                nc.scalar.activation(gs[:, b, :], psG[:, :], ACT.Copy).then_inc(gs_ready, 1)

            act.wait_ge(c_in, 16 * n_c)
            head_xT(0, 0)
            head_tanh(0)
            if not post:
                head_xhT(0, 0)

            def slot(i, u):
                k = 2 * i + u
                end = isinstance(k, int) and k >= K - 1
                for e in range(E):
                    gelus(k, e)
                    if not (isinstance(k, int) and k == 0 and e == 0):
                        gates(k * E + e - 1, (e - 1) % 2)
                    if end:
                        continue
                    if e == AT["x"]:
                        head_xT(k + 1, 1 - u)
                    if e == TANH_AT:
                        head_tanh(k + 1)
                    if e == AT["xh"]:
                        head_xhT(k + 1, 1 - u)

            pairs(act, slot, K)
            gates(K * E - 1, (E - 1) % 2)

        @block.vector
        def _(dve):
            chain = Chain(dve, dve_chain)

            def col(t):
                return t.unsqueeze(2).to_broadcast([P, CB, E])

            def row(t):
                return t.unsqueeze(1).to_broadcast([P, CB, E])

            def split_weights(e):
                for which in (W1, W2):
                    dve.wait_ge(raw_in[e % 2], 16 * (2 * (e // 2) + 2))
                    chain.link(nc.vector.tensor_copy(ws[:, e, which, HI, :], raw[:, e % 2, which, :]))
                    nc.vector.tensor_tensor(ws[:, e, which, LO, :], raw[:, e % 2, which, :],
                                            ws[:, e, which, HI, :], ALU.subtract).then_inc(raw_split, 1)
                dve.wait_ge(raw_split, 2 * e + 2)
                nc.vector.memset(env.scratch[:, :], 0.0).then_inc(w_in[e], 16)

            def head_norm(n, c):
                if post:
                    return
                for j in range(CB):
                    mm = nc.vector.bn_stats(st[:, j, :], H[:, CB * c + j, :])
                chain.link(mm)
                apart(nc, env)
                for j in range(CB):
                    mm = nc.vector.bn_aggr(mv[:, j, :], st[:, j, :])
                mm.then_inc(stats_ready, 1)
                dve.wait_ge(rstd_ready, n + 1)
                after(dve, xh_transposed, n)
                for j in range(CB):
                    mm = nc.vector.tensor_scalar(xh[:, j, :], H[:, CB * c + j, :], mv[:, j, 0:1],
                                                 rstd[:, j:j + 1], ALU.subtract, ALU.mult)
                mm.then_inc(xh_ready, 1)

            def route_pick(n):
                l = n // NCH if L > 1 else 0
                dve.wait_ge(logits_full, n + 1)
                full = psH[:, 0:CB * E].rearrange("t (j e) -> t j e", e=E)
                if post:
                    nc.vector.tensor_copy(lg[:, :, :], full).then_inc(logits_read, 1)
                else:
                    nc.vector.tensor_tensor(lg[:, :, :], full, row(rb[:, bass.ds(l * E, E)]),
                                            ALU.add).then_inc(logits_read, 1)
                dve.wait_ge(logits_read, n + 1)
                link = chain.link
                for src, top, mask in ((lg, m1, k1), (l2, m2, k2)):
                    if src is l2:
                        link(nc.vector.scalar_tensor_tensor(l2[:, :, :], k1[:, :, :], 3.0 * NEG, lg[:, :, :],
                                                            ALU.mult, ALU.add))
                    link(nc.vector.tensor_reduce(top[:, :], src[:, :, :], AX.X, ALU.max))
                    link(nc.vector.tensor_tensor(t1[:, :, :], src[:, :, :], col(top[:, :]), ALU.is_ge))
                    link(nc.vector.tensor_tensor(t1[:, :, :], t1[:, :, :], row(rank[:, :]), ALU.mult))
                    link(nc.vector.tensor_reduce(r1[:, :], t1[:, :, :], AX.X, ALU.max))
                    link(nc.vector.tensor_tensor(mask[:, :, :], t1[:, :, :], col(r1[:, :]), ALU.is_equal))
                nc.vector.tensor_tensor(gap[:, :], m1[:, :], m2[:, :], ALU.subtract).then_inc(gap_ready, 1)

            def route_weigh(n, u):
                dve.wait_ge(tanh_ready, n + 1)
                nc.vector.tensor_scalar(wa[:, :], th[:, :], 0.5, 0.5, ALU.mult, ALU.add)
                chain.link(nc.vector.tensor_scalar(wb[:, :], th[:, :], -0.5, 0.5, ALU.mult, ALU.add))
                nc.vector.tensor_tensor(sw[:, u, :], wa[:, :], wb[:, :], ALU.add)
                nc.vector.tensor_tensor(k1[:, :, :], k1[:, :, :], col(wa[:, :]), ALU.mult)
                chain.link(nc.vector.tensor_tensor(k2[:, :, :], k2[:, :, :], col(wb[:, :]), ALU.mult))
                chain.link(nc.vector.tensor_tensor(comb[:, :, :], k1[:, :, :], k2[:, :, :], ALU.add))
                chain.link(nc.vector.tensor_copy(combp[:, :, 0:E], comb[:, :, :]))
                nc.vector.tensor_tensor(combp[:, :, E:2 * E], comb[:, :, :], combp[:, :, 0:E],
                                        ALU.subtract).then_inc(comb_ready, 1)

            def head_gT(n, u):
                dve.wait_ge(g_transposed, n + 1)
                nc.vector.tensor_copy(gT[:, u, :], psH[0:2 * E, :]).then_inc(gT_ready, 1)

            def split_input(n, u):
                if not post:
                    return
                dve.wait_ge(xT_ready, n + 1)
                nc.vector.tensor_copy(xe[:, u, HI, :], xT[:, u, :]).then_inc(xhi_ready, 1)
                dve.wait_ge(xhi_ready, n + 1)
                nc.vector.tensor_tensor(xe[:, u, LO, :], xT[:, u, :], xe[:, u, HI, :],
                                        ALU.subtract).then_inc(xe_ready, 1)

            def expert_input(k, u, e):
                if post:
                    return
                g = k * E + e
                l = k // NCH
                dve.wait_ge(xhT_ready, k + 1)
                after(dve, r_full, FT * (g - 1))
                chain.link(nc.vector.tensor_scalar(xe32[:, e % 2, :], xhT[:, u, :],
                                                   lng[:, bass.ds(l * E + e, 1)],
                                                   lnb[:, bass.ds(l * E + e, 1)], ALU.mult, ALU.add))
                nc.vector.tensor_copy(xe[:, e % 2, HI, :], xe32[:, e % 2, :]).then_inc(xhi_ready, 1)

            def hidden_low(k, e):
                g = k * E + e
                for f in range(FT):
                    dve.wait_ge(h_ready, FT * g + f + 1)
                    nc.vector.tensor_tensor(hp[:, e % 2, LO, f, :], h32[:, f, :], hp[:, e % 2, HI, f, :],
                                            ALU.subtract).then_inc(hlo_ready, 1)

            def weigh_expert(k, u, e):
                l = k // NCH if L > 1 else 0
                dve.wait_ge(gs_ready, k * E + e + 1)
                dve.wait_ge(expert_done, k * E + e + 1)
                if e > 0:
                    after(dve, y_summed, k * (E - 1) + max(e - 2, 0))
                to = yg[:, e % 2, :] if e else yT[:, u, :]
                nc.vector.scalar_tensor_tensor(to, psY[:, e % 2, :], b2[:, bass.ds(l * E + e, 1)],
                                               gs[:, e % 2, :], ALU.add, ALU.mult).then_inc(yg_ready, 1)

            def finish(k, u, c):
                dve.wait_ge(z_full, k + 1)
                zz = psY[:, 1, :].rearrange("t (j m) -> t j m", m=P)
                if not post:
                    for j in range(CB):
                        mm = nc.vector.scalar_tensor_tensor(H[:, CB * c + j, :], H[:, CB * c + j, :],
                                                            sw[:, u, j:j + 1], zz[:, j, :], ALU.mult, ALU.add)
                    mm.then_inc(x_done, 1)
                    return
                nc.vector.tensor_tensor(z[:, :, :], H[:, bass.ds(CB * c, CB), :], zz, ALU.add).then_inc(z_read, 1)
                dve.wait_ge(z_read, k + 1)
                for j in range(CB):
                    mm = nc.vector.bn_stats(st[:, j, :], z[:, j, :])
                chain.link(mm)
                apart(nc, env)
                for j in range(CB):
                    mm = nc.vector.bn_aggr(mv[:, j, :], st[:, j, :])
                mm.then_inc(stats_ready, 1)
                dve.wait_ge(rstd_ready, k + 1)
                for j in range(CB):
                    mm = nc.vector.tensor_scalar(z[:, j, :], z[:, j, :], mv[:, j, 0:1], rstd[:, j:j + 1],
                                                 ALU.subtract, ALU.mult)
                chain.link(mm)
                for n, op in ((0, ALU.mult), (1, ALU.add)):
                    chain.link(nc.vector.tensor_tensor(z[:, :, :], z[:, :, :],
                                                       gb[:, n, :].unsqueeze(1).to_broadcast([P, CB, P]), op))
                nc.vector.tensor_tensor(X[:, bass.ds(CB * c, CB), :], X[:, bass.ds(CB * c, CB), :], z[:, :, :],
                                        ALU.add).then_inc(x_done, 1)

            chain.slot(0)
            if not post:
                for c in range(NCH):
                    nc.vector.memset(mark[:, c:c + 1], 0.0).then_inc(x_done, 1)
            split_weights(0)
            dve.wait_ge(c_in, 16 * n_c)
            nc.vector.tensor_copy(sel[:, :, :], sel32[:, :, :])
            head_norm(0, 0)
            route_pick(0)
            route_weigh(0, 0)
            head_gT(0, 0)
            split_input(0, 0)
            expert_input(0, 0, 0)
            expert_input(0, 0, 1)
            SETUP = chain.n
            LINKS = [None, None]

            def slot(i, u):
                k = 2 * i + u
                first = isinstance(k, int) and k == 0
                end = isinstance(k, int) and k >= K - 1
                if first:
                    chain.slot(SETUP)
                else:
                    chain.slot(SETUP + LINKS[0] + (LINKS[1] or 0) * (k - 1))
                for e in range(E):
                    if first and e + 1 < E:
                        split_weights(e + 1)
                    if e == E - 1 and not end:
                        expert_input(k + 1, 1 - u, 0)
                    hidden_low(k, e)
                    if e == E - 1 and not end:
                        expert_input(k + 1, 1 - u, 1)
                    if e + 2 < E:
                        expert_input(k, u, e + 2)
                    if e == 1 and not first:
                        finish(k - 1, 1 - u, (k - 1) % NCH)
                    if e > 0:
                        weigh_expert(k, u, e - 1)
                    elif not first:
                        weigh_expert(k - 1, 1 - u, E - 1)
                    if end:
                        continue
                    if e == AT["x"]:
                        head_norm(k + 1, (k + 1) % NCH)
                    if e == AT["logits"]:
                        route_pick(k + 1)
                    if e == TANH_AT:
                        route_weigh(k + 1, 1 - u)
                        split_input(k + 1, 1 - u)
                    if e == AT["gates"]:
                        head_gT(k + 1, 1 - u)
                if first:
                    LINKS[0] = chain.n
                elif LINKS[1] is None:
                    LINKS[1] = chain.n

            pairs(dve, slot, K)
            weigh_expert(K - 1, 1, E - 1)
            finish(K - 1, 1, (K - 1) % NCH)

        @block.tensor
        def _(pe):
            def three_passes(out, stationary, moving, start, stop):
                nc.tensor.matmul(out, stationary(HI), moving(HI), start=start, stop=False)
                nc.tensor.matmul(out, stationary(LO), moving(HI), start=False, stop=False)
                return nc.tensor.matmul(out, stationary(HI), moving(LO), start=False, stop=stop)

            def head_x(n, h, u):
                pe.wait_ge(xs_in[u], 16 * (h + 1))
                after(pe, gT_ready, n)
                for j in range(CB):
                    mm = nc.tensor.transpose(psH[:, P * j:P * j + P], xs[:, u, j, :], ident[:, :])
                mm.then_inc(x_transposed, 1)

            def head_logits(n, u):
                l = n // NCH if L > 1 else 0
                pe.wait_ge(xT_ready, n + 1)
                for j in range(CB):
                    mm = nc.tensor.matmul(psH[:, E * j:E * j + E], xT[:, u, P * j:P * j + P],
                                          rw[:, bass.ds(l * E, E)], start=True, stop=True)
                mm.then_inc(logits_full, 1)

            def head_xh(n):
                pe.wait_ge(xh_ready, n + 1)
                pe.wait_ge(logits_read, n + 1)
                for j in range(CB):
                    mm = nc.tensor.transpose(psH[:, P * j:P * j + P], xh[:, j, :], ident[:, :])
                mm.then_inc(xh_transposed, 1)

            def head_gates(n):
                pe.wait_ge(comb_ready, n + 1)
                if not post:
                    pe.wait_ge(xhT_ready, n + 1)
                for j in range(CB):
                    mm = nc.tensor.transpose(psH[0:2 * E, P * j:P * j + P], combp[:, j, :].bitcast(F32),
                                             ident[:, :])
                mm.then_inc(g_transposed, 1)

            def hidden(k, u, e):
                g = k * E + e
                l = k // NCH if L > 1 else 0
                pe.wait_ge(w_in[e], 16 * (l + 1))
                pe.wait_ge(xe_ready, k + 1 if post else g + 1)
                for f in range(FT):
                    after(pe, h_ready, FT * (g - 1) + f + 1)
                    three_passes(psR[:, f, :], lambda part: ws[:, e, W1, part, P * f:P * f + P],
                                 lambda part: xe[:, u if post else e % 2, part, :], True,
                                 True).then_inc(r_full, 1)

            def outputs(k, u, e):
                g = k * E + e
                after(pe, gs_ready, g)
                pe.wait_ge(gT_ready, k + 1)
                nc.tensor.matmul(psG[:, :], sel[:, e, :], gT[:, u, :], start=True,
                                 stop=True).then_inc(g_full, 1)
                after(pe, yg_ready, g - 1)
                if e == 1:
                    after(pe, z_read, k) if post else pe.wait_ge(x_done, k + NCH)
                for f in range(FT):
                    pe.wait_ge(hlo_ready, FT * g + f + 1)
                    mm = three_passes(psY[:, e % 2, :], lambda part: ws[:, e, W2, part, P * f:P * f + P],
                                      lambda part: hp[:, e % 2, part, f, :], f == 0, f == FT - 1)
                mm.then_inc(expert_done, 1)

            def back(k, u):
                pe.wait_ge(y_summed, (k + 1) * (E - 1))
                for j in range(CB):
                    mm = nc.tensor.transpose(psY[:, 1, P * j:P * j + P], yT[:, u, P * j:P * j + P], ident[:, :])
                mm.then_inc(z_full, 1)

            pe.wait_ge(c_in, 16 * n_c)
            head_x(0, 0, 0)
            head_logits(0, 0)
            if not post:
                head_xh(0)
            head_gates(0)

            def slot(i, u):
                k = 2 * i + u
                first = isinstance(k, int) and k == 0
                end = isinstance(k, int) and k >= K - 1
                for e in range(E):
                    hidden(k, u, e)
                    if e == 1 and not first:
                        back(k - 1, 1 - u)
                    if e > 0:
                        outputs(k, u, e - 1)
                    elif not first:
                        outputs(k - 1, 1 - u, E - 1)
                    if end:
                        continue
                    if e == AT["x"]:
                        head_x(k + 1, i + u, 1 - u)
                    if e == AT["logits"]:
                        head_logits(k + 1, 1 - u)
                    if e == AT["xh"]:
                        head_xh(k + 1)
                    if e == AT["gates"]:
                        head_gates(k + 1)

            pairs(pe, slot, K)
            outputs(K - 1, 1, E - 1)
            back(K - 1, 1)

        stage.close()
        clear(nc, sems)


def build(nc, a, NB, S):
    with ExitStack() as ctx:
        env = Env()
        env.NB = NB
        env.X = ctx.enter_context(nc.sbuf_tensor("X", [P, NB, P], F32))
        env.H = ctx.enter_context(nc.sbuf_tensor("H", [P, NB, P], F32))
        env.ident = ctx.enter_context(nc.sbuf_tensor("ident", [P, P], F32))
        env.identb = ctx.enter_context(nc.sbuf_tensor("identb", [P, P], BF16))
        env.scratch = ctx.enter_context(nc.sbuf_tensor("scratch", [P, 1], F32))
        env.eps = ctx.enter_context(nc.sbuf_tensor("eps", [P, 1], F32))
        env.zero = ctx.enter_context(nc.sbuf_tensor("zero", [P, 1], F32))
        env.minus_half = ctx.enter_context(nc.sbuf_tensor("minus_half", [P, 1], F32))
        const_in = ctx.enter_context(nc.semaphore("const_in"))
        with nc.Block() as block:
            @block.sync
            def _(sp):
                sp.dma_start(env.ident[:, :], a["c_ident"]).then_inc(const_in, 16)
                sp.dma_start(env.identb[:, :], a["c_identb"]).then_inc(const_in, 16)
                sp.dma_start(env.minus_half[:, :], a["c_minus_half"]).then_inc(const_in, 16)
                sp.dma_start(env.eps[:, :], a["c_eps"]).then_inc(const_in, 16)
                sp.dma_start(env.zero[:, :], a["c_zero"]).then_inc(const_in, 16)
                sp.wait_ge(const_in, 80)

        wide = dict(mask=a["c_mask32"], sel=a["c_sel32"], use=part_use(32))
        narrow = dict(mask=a["c_mask16"], sel=a["c_sel16"], use=part_use(16))
        attention(nc, env, "xa0", NB, S, 2 * HEADS, False, True, False, dict(
            wide, x=a["x"], ctx=a["ctx"], w=a["xa0_w"], qkb=a["xa0_qkb"], rows=a["xa0_rows"],
            lam=[a[f"lam{n}"] for n in range(4)]))
        attention(nc, env, "sa", NB, P, HEADS, True, False, True, dict(
            narrow, w=a["sa_w"], qkb=a["sa_qkb"], rows=a["sa_rows"], cm=a["c_cm"], gb=a["sa_gb"]))
        mixture(nc, env, "m0", a["c_rank8"].shape[1], 1, dict(
            {n: a[f"m0_{n}"] for n in ("w1", "w2", "b1", "b2", "rw", "gb")}, rank=a["c_rank8"], sel=a["c_sel8"]))
        attention(nc, env, "xa1", NB, S, HEADS, False, False, True, dict(
            narrow, ctx=a["ctx"], w=a["xa1_w"], qkb=a["xa1_qkb"], rows=a["xa1_rows"]))
        mixture(nc, env, "m1", a["c_rank4"].shape[1], a["m1_b2"].shape[1] // a["c_rank4"].shape[1], dict(
            {n: a[f"m1_{n}"] for n in ("w1", "w2", "b1", "b2", "rw", "lng", "lnb", "rb")},
            rank=a["c_rank4"], sel=a["c_sel4"], out=a["out"]))


HI, MID, LO = 0, 1, 2
PRODUCTS = [(HI, HI), (HI, MID), (MID, HI), (MID, MID), (HI, LO), (LO, HI)]


def set_products(ns, x):
    R = 8 // (ns // 4)
    n = 6 // R
    return PRODUCTS[n * (x % R):n * (x % R) + n]


def part_use(ns):
    return [[sorted({pr[side] for pr in set_products(ns, x)}) for side in range(2)] for x in range(8)]


def constants(NP, S):
    bf = mybir.dt.np(BF16)
    r = NP.arange
    c = {"ident": NP.eye(P, dtype="float32"), "identb": NP.eye(P).astype(bf),
         "eps": NP.full((P, 1), EPS, "float32"), "minus_half": NP.full((P, 1), -0.5, "float32"),
         "zero": NP.zeros((P, 1), "float32")}
    for ns in (32, 16):
        w = 4 * (P // ns)
        R = 8 // (ns // 4)
        mask = NP.zeros((P, 4), "float32")
        mask[r(96), (r(96) % w) // (w // 4)] = 1
        mask[96 + r(12), r(12) % 4] = 1
        c[f"mask{ns}"] = mask
        sel = []
        for x in range(8):
            for side in range(2):
                for part in part_use(ns)[x][side]:
                    m = NP.zeros((P, 96))
                    for n, pr in enumerate(set_products(ns, x)):
                        if pr[side] == part:
                            m[w * (x // R) + r(w), w * n + r(w)] = 1
                    sel.append(m)
        c[f"sel{ns}"] = NP.stack(sel, 1).astype(bf)
    future = (r(P)[None, :] > r(P)[:, None])
    m = NP.stack([future, future.T], 1)[:, :, None, :] * NEG
    c["cm"] = NP.ascontiguousarray(NP.broadcast_to(m, (P, 2, 4, P))).astype(bf)
    for e in (8, 4):
        c[f"rank{e}"] = NP.broadcast_to((e - r(e))[None], (P, e)).astype("float32")
        both = NP.concatenate([NP.eye(e), NP.eye(e)])
        c[f"sel{e}"] = NP.ascontiguousarray(NP.broadcast_to(both[:, :, None], (2 * e, e, P))).astype("float32")
    return c


def kernel(**inputs):
    import numpy as np
    import concourse.bacc as _bacc
    from concourse import mybir as _mybir
    from concourse.bass_utils import run_bass_kernel_spmd as _run

    i = {n: np.asarray(v) for n, v in inputs.items()}
    NB, T, D = i["x"].shape
    S = i["ctx_1024"].shape[1]
    L, E4, _, F = i["L1_ffn_w1"].shape
    E8 = i["L0_ffn_wg"].shape[1]
    zero = np.zeros(D, "float32")
    one = np.ones(D, "float32")
    wi, bi = i["L0_xattn_in_proj_weight"], i["L0_xattn_in_proj_bias"]
    wq = i["L0_ffn_w_qkv"]
    arr = {
        "x": i["x"], "ctx": i["ctx_1024"],
        "xa0_w": np.stack([wi[:D].T, wi[D:2 * D].T, wi[2 * D:].T, i["L0_xattn_out_proj_weight"].T], 1),
        "xa0_qkb": np.stack([bi[:D], bi[D:2 * D]], 1),
        "xa0_rows": np.stack([bi[2 * D:], i["L0_xattn_out_proj_bias"], one])[None],
        "lam0": i["L0_xattn_lambda_q1"], "lam1": i["L0_xattn_lambda_k1"],
        "lam2": i["L0_xattn_lambda_q2"], "lam3": i["L0_xattn_lambda_k2"],
        "sa_w": np.stack([wq[:, :D], wq[:, D:2 * D], wq[:, 2 * D:], i["L0_ffn_w_o"]], 1),
        "sa_qkb": np.stack([zero, zero], 1), "sa_rows": np.stack([zero, zero, one])[None],
        "sa_gb": np.stack([i["L0_ffn_g1"], i["L0_ffn_b1"]]),
        "m0_w1": i["L0_ffn_w1"], "m0_w2": i["L0_ffn_w2"], "m0_b2": i["L0_ffn_bb2"].T,
        "m0_b1": i["L0_ffn_bb1"].reshape(E8 * F // P, P).T, "m0_rw": i["L0_ffn_wg"],
        "m0_gb": np.stack([i["L0_ffn_g2"], i["L0_ffn_b2"]]),
        "xa1_w": np.stack([i["L1_xattn_Wq"], i["L1_xattn_Wk"], i["L1_xattn_Wv"], i["L1_xattn_Wo"]], 1),
        "xa1_qkb": np.stack([i["L1_xattn_bq"], i["L1_xattn_bk"]], 1),
        "xa1_rows": np.stack([i["L1_xattn_bv"], i["L1_xattn_bo"], one])[None],
        "m1_w1": i["L1_ffn_w1"].reshape(L * E4, D, F), "m1_w2": i["L1_ffn_w2"].reshape(L * E4, F, D),
        "m1_b2": i["L1_ffn_b2"].reshape(L * E4, D).T, "m1_b1": i["L1_ffn_b1"].reshape(L * E4 * F // P, P).T,
        "m1_rw": i["L1_ffn_router_w"].transpose(1, 0, 2).reshape(D, L * E4),
        "m1_lng": i["L1_ffn_ln_g"].reshape(L * E4, D).T, "m1_lnb": i["L1_ffn_ln_b"].reshape(L * E4, D).T,
        "m1_rb": i["L1_ffn_router_b"].reshape(L * E4),
    }
    arr.update({f"c_{n}": v for n, v in constants(np, S).items()})
    arr = {n: np.ascontiguousarray(v) for n, v in arr.items()}

    nc = _bacc.Bacc("TRN2", target_bir_lowering=False, num_devices=1)
    aps = {n: nc.dram_tensor(f"in_{n}", v.shape, _mybir.dt.from_np(v.dtype), kind="ExternalInput").ap()
           for n, v in arr.items()}
    aps["out"] = nc.dram_tensor("out_x", (NB, T, D), F32, kind="ExternalOutput").ap()
    build(nc, aps, NB, S)
    r = _run(nc, [{f"in_{n}": v for n, v in arr.items()}], core_ids=[0])
    return r.results[0]["out_x"]
```
